# Optimizing a Trainium2 kernel written in Bass

```python
import numpy as np
import jax
import jax.numpy as jnp

def _softmax(x, axis=-1):
    return jax.nn.softmax(x, axis=axis)

def _gelu(x):
    return jax.nn.gelu(x, approximate=True)

def _silu(x):
    return jax.nn.silu(x)

def _sigmoid(x):
    return jax.nn.sigmoid(x)

def _layernorm(x, axis=-1, eps=1e-05):
    m = jnp.mean(x, axis=axis, keepdims=True)
    v = jnp.var(x, axis=axis, keepdims=True)
    return (x - m) / jnp.sqrt(v + eps)

def _scatter_add(tgt, idx, src, axis=0):
    return tgt.at[idx].add(src)

def _segment_sum(src, seg, n):
    return jax.ops.segment_sum(src, seg, n)
kernel_name = 'mk_adj_resnorm_d2_adj_r2_2d63a9'

def setup_inputs(seed: int=0):
    np.random.seed(seed)
    _w = jnp.asarray

    def _rec_inputs():
        import jax
        import jax.numpy as jnp
        _gk = jax.random.key(seed)
        x = -0.0005207 + 1.001 * jax.random.normal(jax.random.fold_in(_gk, 1), (3327, 128), jnp.float32)
        _a = jax.random.bernoulli(jax.random.fold_in(_gk, 2), 0.00120228, (3327, 3327))
        _a = jnp.logical_or(_a, jnp.swapaxes(_a, -1, -2))
        _a = jnp.logical_or(_a, jnp.eye(3327, dtype=bool))
        _af = _a.astype(jnp.float32)
        _af = _af * jax.random.uniform(jax.random.fold_in(_gk, 3), (3327, 3327), jnp.float32, 0.05, 1)
        adj = _af
        return (x, adj)
    x, adj = _rec_inputs()

    def _L0_gnn_setup():
        import jax, jax.numpy as jnp
        import numpy as np
        D_IN = 128
        D_ATTN = 64
        STEPS = 2
        TOP_P = 0.9
        TAU = 1.0
        LN_EPS = 1e-05
        N_NODES = 4096

        def _top_p_attention(X, W1, W2, W3):
            q = X @ W1.T @ W2.T
            k = X @ W3.T
            logits = q @ k.T / TAU
            probs = jax.nn.softmax(logits, axis=-1)
            idx = jnp.argsort(-probs, axis=-1)
            sp = jnp.take_along_axis(probs, idx, axis=-1)
            cs = jnp.cumsum(sp, axis=-1)
            keep_sorted = cs - sp < TOP_P
            rows = jnp.arange(probs.shape[0])[:, None]
            mask = jnp.zeros(probs.shape, dtype=bool).at[rows, idx].set(keep_sorted)
            A = probs * mask
            return A / jnp.maximum(A.sum(-1, keepdims=True), 1e-12)
        key = jax.random.key(seed)
        ks = jax.random.split(key, 8)
        N, d, da, steps = (N_NODES, D_IN, D_ATTN, STEPS)
        X = jax.random.normal(ks[0], (N, d), dtype=jnp.float32)
        S = jax.random.uniform(ks[1], (N, N), dtype=jnp.float32)
        W1 = jax.random.normal(ks[2], (da, d), dtype=jnp.float32) / np.sqrt(d)
        W2 = jax.random.normal(ks[3], (da, da), dtype=jnp.float32) / np.sqrt(da)
        W3 = jax.random.normal(ks[4], (da, d), dtype=jnp.float32) / np.sqrt(d)
        U1 = jax.random.normal(ks[5], (steps, d, d), dtype=jnp.float32) / np.sqrt(d)
        U2 = jax.random.normal(ks[6], (steps, d, d), dtype=jnp.float32) / np.sqrt(d)
        ln_g = jnp.ones((d,), dtype=jnp.float32)
        ln_b = jnp.zeros((d,), dtype=jnp.float32)
        return {'X': X, 'S': S, 'W1': W1, 'W2': W2, 'W3': W3, 'U1': U1, 'U2': U2, 'ln_g': ln_g, 'ln_b': ln_b}
    _L0_gnn_all = _L0_gnn_setup()
    _L0_gnn_in = {k: v for k, v in _L0_gnn_all.items() if k in ('W1', 'W2', 'W3', 'U1', 'U2', 'ln_g', 'ln_b')}
    del _L0_gnn_all

    def _L1_gnn_setup():
        import jax, jax.numpy as jnp
        import numpy as np
        N, H, HEADS = (2048, 128, 3)
        ALPHA = 0.2
        NEG_INF = -9000000000000000.0

        def _sign_adj(key, n, density):
            k1, k2 = jax.random.split(key)
            mask = jax.random.uniform(k1, (n, n)) < density
            sign = jnp.where(jax.random.uniform(k2, (n, n)) < 0.5, -1.0, 1.0)
            adj = jnp.where(mask, sign, 0.0).astype(jnp.float32)
            idx = jnp.arange(n)
            return adj.at[idx, idx].set(1.0)

        def _gru_cell(x, hstate, Wih, Whh, bih, bhh):
            gi = x @ Wih.T + bih
            gh = hstate @ Whh.T + bhh
            ir, iz, inn = jnp.split(gi, 3, axis=1)
            hr, hz, hn = jnp.split(gh, 3, axis=1)
            r = jax.nn.sigmoid(ir + hr)
            z = jax.nn.sigmoid(iz + hz)
            n = jnp.tanh(inn + r * hn)
            return (1.0 - z) * n + z * hstate

        def _gat_head(h, node_adj, edge_adj, W, a):
            hW = h @ W
            hp = (node_adj > 0).astype(hW.dtype) @ hW
            hm = (node_adj < 0).astype(hW.dtype) @ hW
            e_plus = jax.nn.leaky_relu(jnp.concatenate([hp, hm], axis=1) @ a, ALPHA)[:, 0]
            e_minus = jax.nn.leaky_relu(jnp.concatenate([hm, hp], axis=1) @ a, ALPHA)[:, 0]
            att = jnp.where(edge_adj > 0, e_plus[None, :], NEG_INF)
            att = jnp.where(edge_adj < 0, e_minus[None, :], att)
            att = jax.nn.softmax(att, axis=1)
            return att * edge_adj @ hW
        key = jax.random.key(seed)
        ks = jax.random.split(key, 16)
        std = 0.01
        gain = 1.414
        return {'h': jax.random.normal(ks[0], (N, H), jnp.float32), 'node_adj': _sign_adj(ks[1], N, 0.005), 'edge_adj': _sign_adj(ks[2], N, 0.005), 'gat_W': jax.random.normal(ks[3], (HEADS, H, H), jnp.float32) * (gain / np.sqrt(H, dtype=np.float32)), 'gat_a': jax.random.normal(ks[4], (HEADS, 2 * H, 1), jnp.float32) * 0.1, 'edge_Wih': jax.random.normal(ks[5], (3 * H, H), jnp.float32) * std, 'edge_Whh': jax.random.normal(ks[6], (3 * H, H), jnp.float32) * std, 'edge_bih': jnp.zeros((3 * H,), jnp.float32), 'edge_bhh': jnp.zeros((3 * H,), jnp.float32), 'node_Wih': jax.random.normal(ks[7], (3 * H, H), jnp.float32) * std, 'node_Whh': jax.random.normal(ks[8], (3 * H, H), jnp.float32) * std, 'node_bih': jnp.zeros((3 * H,), jnp.float32), 'node_bhh': jnp.zeros((3 * H,), jnp.float32)}
    _L1_gnn_all = _L1_gnn_setup()
    _L1_gnn_in = {k: v for k, v in _L1_gnn_all.items() if k in ('gat_W', 'gat_a', 'edge_Wih', 'edge_Whh', 'edge_bih', 'edge_bhh', 'node_Wih', 'node_Whh', 'node_bih', 'node_bhh')}
    del _L1_gnn_all
    return {'x': x, 'adj': adj, 'L0_gnn_W1': _L0_gnn_in['W1'], 'L0_gnn_W2': _L0_gnn_in['W2'], 'L0_gnn_W3': _L0_gnn_in['W3'], 'L0_gnn_U1': _L0_gnn_in['U1'], 'L0_gnn_U2': _L0_gnn_in['U2'], 'L0_gnn_ln_g': _L0_gnn_in['ln_g'], 'L0_gnn_ln_b': _L0_gnn_in['ln_b'], 'L1_gnn_gat_W': _L1_gnn_in['gat_W'], 'L1_gnn_gat_a': _L1_gnn_in['gat_a'], 'L1_gnn_edge_Wih': _L1_gnn_in['edge_Wih'], 'L1_gnn_edge_Whh': _L1_gnn_in['edge_Whh'], 'L1_gnn_edge_bih': _L1_gnn_in['edge_bih'], 'L1_gnn_edge_bhh': _L1_gnn_in['edge_bhh'], 'L1_gnn_node_Wih': _L1_gnn_in['node_Wih'], 'L1_gnn_node_Whh': _L1_gnn_in['node_Whh'], 'L1_gnn_node_bih': _L1_gnn_in['node_bih'], 'L1_gnn_node_bhh': _L1_gnn_in['node_bhh']}

def reference(x, adj, L0_gnn_W1, L0_gnn_W2, L0_gnn_W3, L0_gnn_U1, L0_gnn_U2, L0_gnn_ln_g, L0_gnn_ln_b, L1_gnn_gat_W, L1_gnn_gat_a, L1_gnn_edge_Wih, L1_gnn_edge_Whh, L1_gnn_edge_bih, L1_gnn_edge_bhh, L1_gnn_node_Wih, L1_gnn_node_Whh, L1_gnn_node_bih, L1_gnn_node_bhh):
    import jax
    import jax.numpy as jnp

    def _L0_gnn_ref(X, S, W1, W2, W3, U1, U2, ln_g, ln_b):
        import jax, jax.numpy as jnp
        import numpy as np
        D_IN = 128
        D_ATTN = 64
        STEPS = 2
        TOP_P = 0.9
        TAU = 1.0
        LN_EPS = 1e-05
        N_NODES = 4096

        def _top_p_attention(X, W1, W2, W3):
            q = X @ W1.T @ W2.T
            k = X @ W3.T
            logits = q @ k.T / TAU
            probs = jax.nn.softmax(logits, axis=-1)
            idx = jnp.argsort(-probs, axis=-1)
            sp = jnp.take_along_axis(probs, idx, axis=-1)
            cs = jnp.cumsum(sp, axis=-1)
            keep_sorted = cs - sp < TOP_P
            rows = jnp.arange(probs.shape[0])[:, None]
            mask = jnp.zeros(probs.shape, dtype=bool).at[rows, idx].set(keep_sorted)
            A = probs * mask
            return A / jnp.maximum(A.sum(-1, keepdims=True), 1e-12)
        N = X.shape[0]
        R = S + jnp.eye(N, dtype=X.dtype)
        R = R / R.sum(-1, keepdims=True)
        Z = jnp.zeros_like(X)
        Xf = X
        Xa = X
        for n in range(STEPS):
            A = _top_p_attention(Xa, W1, W2, W3)
            Xf = R @ Xf
            Xa = A @ Xa
            Z = Z + Xf @ U1[n].T + Xa @ U2[n].T
        h = X + Z
        mu = h.mean(-1, keepdims=True)
        var = jnp.mean((h - mu) ** 2, axis=-1, keepdims=True)
        return (h - mu) / jnp.sqrt(var + LN_EPS) * ln_g + ln_b

    def _L1_gnn_ref(h, node_adj, edge_adj, gat_W, gat_a, edge_Wih, edge_Whh, edge_bih, edge_bhh, node_Wih, node_Whh, node_bih, node_bhh):
        import jax, jax.numpy as jnp
        import numpy as np
        N, H, HEADS = (2048, 128, 3)
        ALPHA = 0.2
        NEG_INF = -9000000000000000.0

        def _sign_adj(key, n, density):
            k1, k2 = jax.random.split(key)
            mask = jax.random.uniform(k1, (n, n)) < density
            sign = jnp.where(jax.random.uniform(k2, (n, n)) < 0.5, -1.0, 1.0)
            adj = jnp.where(mask, sign, 0.0).astype(jnp.float32)
            idx = jnp.arange(n)
            return adj.at[idx, idx].set(1.0)

        def _gru_cell(x, hstate, Wih, Whh, bih, bhh):
            gi = x @ Wih.T + bih
            gh = hstate @ Whh.T + bhh
            ir, iz, inn = jnp.split(gi, 3, axis=1)
            hr, hz, hn = jnp.split(gh, 3, axis=1)
            r = jax.nn.sigmoid(ir + hr)
            z = jax.nn.sigmoid(iz + hz)
            n = jnp.tanh(inn + r * hn)
            return (1.0 - z) * n + z * hstate

        def _gat_head(h, node_adj, edge_adj, W, a):
            hW = h @ W
            hp = (node_adj > 0).astype(hW.dtype) @ hW
            hm = (node_adj < 0).astype(hW.dtype) @ hW
            e_plus = jax.nn.leaky_relu(jnp.concatenate([hp, hm], axis=1) @ a, ALPHA)[:, 0]
            e_minus = jax.nn.leaky_relu(jnp.concatenate([hm, hp], axis=1) @ a, ALPHA)[:, 0]
            att = jnp.where(edge_adj > 0, e_plus[None, :], NEG_INF)
            att = jnp.where(edge_adj < 0, e_minus[None, :], att)
            att = jax.nn.softmax(att, axis=1)
            return att * edge_adj @ hW
        dn = jnp.diag(node_adj)
        de = jnp.diag(edge_adj)
        idx = jnp.arange(node_adj.shape[0])
        node_adj_norm = node_adj.at[idx, idx].add(-dn)
        edge_adj_norm = edge_adj.at[idx, idx].add(-de)
        node_support = node_adj_norm @ h
        edge_output = _gru_cell(node_support, h, edge_Wih, edge_Whh, edge_bih, edge_bhh)
        edge_support = _gat_head(h, node_adj_norm, edge_adj_norm, gat_W[0], gat_a[0])
        for i in range(1, HEADS):
            edge_support = edge_support + _gat_head(h, node_adj_norm, edge_adj_norm, gat_W[i], gat_a[i])
        edge_support = edge_support / HEADS
        node_output = _gru_cell(edge_support, h, node_Wih, node_Whh, node_bih, node_bhh)
        return de[:, None] * edge_output + dn[:, None] * node_output
    x = _layernorm(x + _L0_gnn_ref(x, adj, L0_gnn_W1, L0_gnn_W2, L0_gnn_W3, L0_gnn_U1, L0_gnn_U2, L0_gnn_ln_g, L0_gnn_ln_b), axis=-1)
    x = _layernorm(x + _L1_gnn_ref(x, adj, adj, L1_gnn_gat_W, L1_gnn_gat_a, L1_gnn_edge_Wih, L1_gnn_edge_Whh, L1_gnn_edge_bih, L1_gnn_edge_bhh, L1_gnn_node_Wih, L1_gnn_node_Whh, L1_gnn_node_bih, L1_gnn_node_bhh), axis=-1)
    return x

_drawn_inputs = setup_inputs


def setup_inputs(seed=0):
    import zlib

    import numpy as np

    out = dict(_drawn_inputs(seed))
    spreads = {'L0_gnn_ln_g': (1.0, 0.2),
     'L0_gnn_ln_b': (0.0, 0.1),
     'L1_gnn_edge_bih': (0.0, 0.423),
     'L1_gnn_edge_bhh': (0.0, 0.729),
     'L1_gnn_node_bih': (0.0, 0.417),
     'L1_gnn_node_bhh': (0.0, 0.645)}
    factors = {'L1_gnn_gat_W': 6.823,
     'L1_gnn_gat_a': 8.0,
     'L1_gnn_edge_Whh': 4.228,
     'L1_gnn_node_Wih': 6.928,
     'L1_gnn_node_Whh': 4.168}
    for name, (base, spread) in spreads.items():
        noise = np.random.default_rng([zlib.crc32(name.encode()), seed]).standard_normal(out[name].shape)
        drawn = base * np.exp(spread * noise) if base else spread * noise
        out[name] = jnp.asarray(drawn.astype(out[name].dtype))
    for name, factor in factors.items():
        out[name] = (out[name] * factor).astype(out[name].dtype)
    return out
```

```python
from contextlib import ExitStack

import concourse.bass as bass
from concourse import mybir

F32 = mybir.dt.float32
I32 = mybir.dt.int32
BF16 = mybir.dt.bfloat16
ALU = mybir.AluOpType
ACT = mybir.ActivationFunctionType
AX = mybir.AxisListType

P = 128
NEG = -9.0e15
EPS = 1e-5
TOP_P = 0.9
BIG_E = 4.0
HOT_ROUNDS = 4


def scope(nc, ctx):
    def sb(name, shape, dt=F32):
        return ctx.enter_context(nc.sbuf_tensor(name, shape, dt))

    def ps(name, shape, dt=F32):
        return ctx.enter_context(nc.psum_tensor(name, shape, dt))

    def sem(name):
        return ctx.enter_context(nc.semaphore(name))

    return sb, ps, sem


def any_row_flag(eng, w, flag, regs):
    eng.drain()
    eng.transpose(w["flags_t"][:, :], w["flags"][:, :])
    eng.drain()
    eng.tensor_reduce(w["flag_max"][:, :], w["flags_t"][:, :], AX.X, ALU.max)
    eng.drain()
    eng.tensor_copy(w["flag_int"][:, :], w["flag_max"][:, :])
    eng.drain()
    for q in range(4):
        eng.reg_load(regs[q], w["flag_int"][32 * q:32 * q + 1, 0:1])
    eng.reg_add(flag, regs[0], regs[1])
    eng.reg_add(flag, flag, regs[2])
    eng.reg_add(flag, flag, regs[3])


def crossing(eng, w):
    eng.tensor_tensor_scan(w["run8"][:, :], w["top8"][:, :], w["zero8"][:, :], w["mass_hi"][:, :],
                           ALU.add, ALU.add)
    eng.drain()
    eng.tensor_copy(w["reach"][:, :], w["run8"][:, 7:8])
    eng.scalar_tensor_tensor(w["hit8"][:, :], w["run8"][:, :], w["theta"][:, :], w["top8"][:, :],
                             ALU.is_ge, ALU.mult)
    eng.drain()
    eng.tensor_reduce(w["cut"][:, :], w["hit8"][:, :], AX.X, ALU.max)
    eng.drain()
    eng.tensor_tensor(w["cut"][:, :], w["cut"][:, :], w["top8"][:, 7:8], ALU.max)
    eng.drain()
    eng.scalar_tensor_tensor(w["hit8"][:, :], w["top8"][:, :], w["cut"][:, :], w["top8"][:, :],
                             ALU.is_gt, ALU.mult, accum_out=w["above"][:, :])
    eng.drain()
    eng.tensor_tensor(w["above"][:, :], w["above"][:, :], w["mass_hi"][:, :], ALU.add)


def open_rows(eng, w):
    eng.drain()
    eng.tensor_tensor(w["best"][:, :], w["reach"][:, :], w["mass_cut"][:, :], ALU.max)
    eng.drain()
    eng.tensor_tensor(w["flags"][:, 0:1], w["best"][:, :], w["theta"][:, :], ALU.is_lt)


def mass_from(eng, w, e, t, out):
    eng.scalar_tensor_tensor(w["work"][:, 0:e.shape[1]], e, t, e, ALU.is_ge, ALU.mult, accum_out=out)


def search_round(eng, w, e):
    mass_from(eng, w, e, w["cut"][:, :], w["mass_cut"][:, :])
    open_rows(eng, w)
    eng.drain()
    eng.copy_predicated(w["hi"][:, :], w["flags"][:, 0:1].bitcast(I32), w["cut"][:, :])
    eng.copy_predicated(w["mass_hi"][:, :], w["flags"][:, 0:1].bitcast(I32), w["mass_cut"][:, :])
    for _ in range(3):
        eng.drain()
        eng.tensor_tensor(w["bits"][:, :], w["lo"][:, :].bitcast(I32), w["hi"][:, :].bitcast(I32), ALU.add)
        eng.drain()
        eng.tensor_scalar(w["mid"][:, :].bitcast(I32), w["bits"][:, :], 0.5, None, ALU.mult)
        eng.drain()
        mass_from(eng, w, e, w["mid"][:, :], w["mass_mid"][:, :])
        eng.drain()
        eng.scalar_tensor_tensor(w["up"][:, :], w["mass_mid"][:, :], w["theta"][:, :], w["flags"][:, 0:1],
                                 ALU.is_ge, ALU.mult)
        eng.scalar_tensor_tensor(w["down"][:, :], w["mass_mid"][:, :], w["theta"][:, :], w["flags"][:, 0:1],
                                 ALU.is_lt, ALU.mult)
        eng.drain()
        eng.copy_predicated(w["lo"][:, :], w["up"][:, :].bitcast(I32), w["mid"][:, :])
        eng.copy_predicated(w["hi"][:, :], w["down"][:, :].bitcast(I32), w["mid"][:, :])
        eng.copy_predicated(w["mass_hi"][:, :], w["down"][:, :].bitcast(I32), w["mass_mid"][:, :])
    eng.drain()
    eng.scalar_tensor_tensor(w["work"][:, 0:e.shape[1]], e, w["hi"][:, :], e, ALU.is_lt, ALU.mult)
    eng.drain()
    eng.max(w["top8"][:, :], w["work"][:, 0:e.shape[1]])
    eng.drain()
    crossing(eng, w)
    open_rows(eng, w)


def tie_round(eng, w, src):
    eng.tensor_scalar(w["hit8"][:, :], w["index8"][:, :], w["cut"][:, :], None, ALU.mult)
    eng.drain()
    eng.tensor_scalar(w["hit8"][:, :], w["hit8"][:, :], w["left"][:, :], w["cut"][:, :], ALU.is_lt, ALU.mult)
    eng.drain()
    eng.match_replace(out=w["work"][:, :], in_to_replace=w["hit8"][:, :], in_values=src, imm_value=BIG_E)
    eng.scalar_tensor_tensor(w["left"][:, :], w["cut"][:, :], -8.0, w["left"][:, :], ALU.mult, ALU.add)
    eng.drain()
    eng.tensor_scalar(w["flags"][:, 0:1], w["left"][:, :], 0.0, None, ALU.is_gt)


def top_p_select(eng, w, e_pad, width, valid, total, flag, regs):
    e = e_pad[:, 0:valid]
    eng.tensor_scalar(w["theta"][:, :], total, TOP_P, None, ALU.mult)
    eng.max(w["top8"][:, :], e)
    eng.memset(w["mass_hi"][:, :], 0.0)
    eng.memset(w["mass_cut"][:, :], 0.0)
    eng.memset(w["hi"][:, :], 2.0)
    eng.memset(w["lo"][:, :], 0.9 * (1.0 - TOP_P) / width)
    eng.drain()
    crossing(eng, w)
    open_rows(eng, w)
    any_row_flag(eng, w, flag, regs)
    with eng.Fori(0, HOT_ROUNDS):
        with eng.If(eng.snap(flag) > 0):
            search_round(eng, w, e)
            any_row_flag(eng, w, flag, regs)
    with eng.If(eng.snap(flag) > 0):
        with eng.Fori(0, 2 * P):
            with eng.If(eng.snap(flag) > 0):
                search_round(eng, w, e)
                any_row_flag(eng, w, flag, regs)
    eng.drain()
    eng.tensor_tensor(w["left"][:, :], w["theta"][:, :], w["above"][:, :], ALU.subtract)
    eng.drain()
    tie_round(eng, w, e_pad)
    any_row_flag(eng, w, flag, regs)
    with eng.If(eng.snap(flag) > 0):
        tie_round(eng, w, w["work"][:, :])
        eng.drain()
        tie_round(eng, w, w["work"][:, :])
        any_row_flag(eng, w, flag, regs)
        with eng.If(eng.snap(flag) > 0):
            with eng.Fori(0, width // 8):
                with eng.If(eng.snap(flag) > 0):
                    tie_round(eng, w, w["work"][:, :])
                    any_row_flag(eng, w, flag, regs)
    eng.drain()
    eng.scalar_tensor_tensor(e_pad[:, 0:width], w["work"][:, 0:width], w["cut"][:, :],
                             e_pad[:, 0:width], ALU.is_gt, ALU.mult, accum_out=w["kept"][:, :])
    eng.drain()


def work_buffers(sb, width):
    w = {"work": sb("work", [P, width + 8]), "flags": sb("flags", [P, 32]), "flags_t": sb("flags_t", [P, 32]),
         "flag_int": sb("flag_int", [P, 1], I32), "index8": sb("index8", [P, 8])}
    for n in ("top8", "run8", "hit8", "zero8"):
        w[n] = sb(n, [P, 8])
    for n in ("flag_max", "reach", "cut", "above", "best", "theta", "mass_cut", "mass_hi", "hi", "lo",
              "kept", "bits", "mid", "mass_mid", "up", "down", "left"):
        w[n] = sb(n, [P, 1])
    return w


def layer0(nc, d, dims, H, ident):
    N, NP, T = dims
    PAIRS = T // 2
    CH = 512
    NC = -(-NP // CH)
    DA = d["W2T"].shape[0]
    PROJ = 3 * NC
    STEP_CH = PROJ + T * NC

    def cols(c, end=NP):
        return slice(c * CH, min((c + 1) * CH, end))

    with ExitStack() as ctx:
        sb, ps, sem = scope(nc, ctx)
        qT = sb("qT", [DA, NP])
        kT = sb("kT", [DA, NP])
        XT = sb("XT", [P, NP])
        XR = [sb(f"XR{i}", [P, T, P + 1]) for i in range(3)]
        adj = [sb(f"adj{i}", [P, NP]) for i in range(2)]
        s = [sb(f"s{i}", [P, N]) for i in range(2)]
        e = [sb(f"e{i}", [P, NP + 8]) for i in range(2)]
        wT = [sb(f"wT{i}", [P, CH]) for i in range(2)]
        w = work_buffers(sb, NP)
        h1 = w["work"][0:DA, 0:NP]
        W1T = sb("W1T", [P, DA])
        W2T = sb("W2T", [DA, DA])
        W3T = sb("W3T", [P, DA])
        UT = sb("UT", [P, 2, 2, P])
        qs = [sb(f"qs{i}", [DA, P]) for i in range(2)]
        gate = sb("gate", [P, 1])
        top = [sb(f"top{i}", [P, 8]) for i in range(2)]
        negmax = [sb(f"negmax{i}", [P, 1]) for i in range(2)]
        total = [sb(f"total{i}", [P, 1]) for i in range(2)]
        rawR = [sb(f"rawR{i}", [P, P + 1]) for i in range(2)]
        inv_sum = [sb(f"inv_sum{i}", [P, 1]) for i in range(2)]
        inv_kept = [sb(f"inv_kept{i}", [P, 1]) for i in range(2)]
        rowR = [sb(f"rowR{i}", [P, P]) for i in range(2)]
        rowA = [sb(f"rowA{i}", [P, P]) for i in range(2)]
        xTR = [sb(f"xTR{i}", [P, P]) for i in range(2)]
        xTA = [sb(f"xTA{i}", [P, P]) for i in range(2)]
        zs = [sb(f"zs{i}", [P, P]) for i in range(2)]

        lg = [ps(f"lg{i}", [P, CH]) for i in range(2)]
        tr = [ps(f"tr{i}", [P, CH]) for i in range(2)]
        accR = ps("accR", [P, P + 1])
        accA = ps("accA", [P, P])
        xt = ps("xt", [P, 2, P])
        zp = ps("zp", [P, P])

        loaded = sem("l0_loaded")
        consts = sem("l0_consts")
        adj_loaded = [sem(f"l0_adj_loaded{i}") for i in range(2)]
        adj_free = sem("l0_adj_free")
        qs_ready = sem("l0_qs_ready")
        qs_free = sem("l0_qs_free")
        lg_ready = sem("l0_lg_ready")
        lg_free = sem("l0_lg_free")
        negmax_ready = sem("l0_negmax_ready")
        e_ready = sem("l0_e_ready")
        e_free = sem("l0_e_free")
        w_ready = sem("l0_w_ready")
        tr_ready = sem("l0_tr_ready")
        wT_ready = sem("l0_wT_ready")
        wT_free = sem("l0_wT_free")
        accR_ready = sem("l0_accR_ready")
        rawR_ready = sem("l0_rawR_ready")
        sum_ready = sem("l0_sum_ready")
        inv_ready = sem("l0_inv_ready")
        rowR_ready = sem("l0_rowR_ready")
        xtR_ready = sem("l0_xtR_ready")
        xTR_ready = sem("l0_xTR_ready")
        accA_ready = sem("l0_accA_ready")
        rowA_ready = sem("l0_rowA_ready")
        xtA_ready = sem("l0_xtA_ready")
        xTA_ready = sem("l0_xTA_ready")
        z_ready = sem("l0_z_ready")
        zs_ready = sem("l0_zs_ready")
        added = sem("l0_added")
        N_LOADS = 8

        def seq(step, p, slot):
            return (p + step * PAIRS) * 2 + slot

        def chunk(step, p, slot, c):
            return step * STEP_CH + PROJ + (p * 2 + slot) * NC + c

        with nc.Block() as block:

            @block.sync
            def _(eng):
                eng.dma_start(XR[0][:, :, 0:P], d["x_rows"]).then_inc(loaded, 16)
                eng.dma_start(H[:, :, :], d["x_rows"]).then_inc(loaded, 16)
                eng.dma_start(XT[:, :], d["x_t"]).then_inc(loaded, 16)
                eng.dma_start(W1T[:, :], d["W1T"]).then_inc(loaded, 16)
                eng.dma_start(W2T[:, :], d["W2T"]).then_inc(loaded, 16)
                eng.dma_start(W3T[:, :], d["W3T"]).then_inc(loaded, 16)
                eng.dma_start(UT[:, 0, :, :], d["U1T"]).then_inc(loaded, 16)
                eng.dma_start(UT[:, 1, :, :], d["U2T"]).then_inc(loaded, 16)
                for step in range(2):
                    with eng.Fori(0, PAIRS) as p:
                        for k in range(2):
                            eng.wait_ge(adj_free, seq(step, p, k) + 1)
                            eng.dma_start(adj[k][:, :], d["adjT"][bass.ds((p * 2 + k) * P, P), :]).then_inc(adj_loaded[k], 16)
                eng.wait_ge(added, 2 * T)

            @block.gpsimd
            def _(eng):
                eng.memset(ident[:, :], 0.0)
                for k in range(3):
                    eng.memset(XR[k][:, :, P:P + 1], 1.0)
                eng.drain()
                eng.affine_select(out=ident[:, :], in_=ident[:, :], compare_op=ALU.not_equal, fill=1.0,
                                  base=0, pattern=[[-1, P]], channel_multiplier=1)
                eng.drain()
                eng.sem_inc(consts, 1)
                eng.wait_ge(loaded, 16 * N_LOADS)
                for step in range(2):
                    eng.wait_ge(lg_free, 2 + step * STEP_CH + PROJ)

                    def give_q(p, k):
                        eng.wait_ge(qs_free, seq(step, p, k) + 1)
                        eng.tensor_copy(qs[k][:, :], qT[:, bass.ds((p * 2 + k) * P, P)])
                        eng.drain()
                        eng.sem_inc(qs_ready, 1)

                    def add_self(p, k):
                        src = XR[0] if step == 0 else XR[2]
                        eng.wait_ge(rawR_ready, seq(step, p, k) + 2)
                        eng.tensor_tensor(rawR[k][:, :], rawR[k][:, :], src[:, bass.ds(p * 2 + k, 1), :]
                                          .rearrange("p a n -> p (a n)"), ALU.add)
                        eng.drain()
                        eng.sem_inc(sum_ready, 1)

                    def give_rows(p, k):
                        eng.wait_ge(inv_ready, seq(step, p, k) + 1)
                        eng.tensor_tensor(rowR[k][:, :], rawR[k][:, 0:P], inv_sum[k][:, :].to_broadcast([P, P]),
                                          ALU.mult)
                        eng.drain()
                        eng.sem_inc(rowR_ready, 1)
                        if step == 0:
                            eng.tensor_copy(XR[2][:, bass.ds(p * 2 + k, 1), 0:P], rowR[k][:, :].unsqueeze(1))

                    def give_attended(p, k):
                        i = p * 2 + k
                        if step == 0:
                            eng.wait_ge(xTA_ready, seq(step, p, k) + 1)
                            eng.tensor_copy(XR[1][:, bass.ds(i, 1), 0:P], rowA[k][:, :].unsqueeze(1))
                            eng.tensor_copy(XT[:, bass.ds(i * P, P)], xTA[k][:, :])
                        eng.wait_ge(zs_ready, seq(step, p, k) + 2)
                        eng.tensor_tensor(H[:, bass.ds(i, 1), :], H[:, bass.ds(i, 1), :],
                                          zs[k][:, :].unsqueeze(1), ALU.add)
                        eng.drain()
                        eng.sem_inc(added, 1)

                    def pair(p, last):
                        add_self(p, 0)
                        add_self(p, 1)
                        if not last:
                            give_q(p + 1, 0)
                            give_q(p + 1, 1)
                        give_rows(p, 0)
                        give_rows(p, 1)
                        give_attended(p, 0)
                        give_attended(p, 1)

                    give_q(0, 0)
                    give_q(0, 1)
                    with eng.Fori(0, PAIRS - 1) as p:
                        pair(p, False)
                    pair(PAIRS - 1, True)

            @block.tensor
            def _(eng):
                eng.sem_inc(adj_free, 2)
                eng.sem_inc(qs_free, 2)
                eng.sem_inc(e_free, 2)
                eng.sem_inc(wT_free, 2)
                eng.wait_ge(loaded, 16 * N_LOADS)
                eng.wait_ge(consts, 1)
                for step in range(2):
                    xf = XR[0] if step == 0 else XR[2]
                    xa = XR[0] if step == 0 else XR[1]

                    def project(which, lhsT, rhs, c):
                        n = step * STEP_CH + which * NC + c
                        eng.wait_ge(lg_free, n + 1)
                        eng.matmul(lg[n % 2][0:DA, 0:rhs.shape[1]], lhsT, rhs, start=True, stop=True)\
                           .then_inc(lg_ready, 1)

                    def logits(p, k):
                        eng.wait_ge(qs_ready, seq(step, p, k) + 1)
                        for c in range(NC):
                            n = chunk(step, p, k, c)
                            b = chunk(step, 0, k, c) % 2
                            sl = cols(c, N)
                            eng.wait_ge(lg_free, n + 1)
                            eng.matmul(lg[b][:, 0:sl.stop - sl.start], qs[k][:, :], kT[:, sl],
                                       start=True, stop=True).then_inc(lg_ready, 1)
                        eng.drain()
                        eng.sem_inc(qs_free, 1)

                    def rows(p, k):
                        eng.wait_ge(adj_loaded[k], (p + step * PAIRS + 1) * 16)
                        eng.wait_ge(rawR_ready, seq(step, p, k) + 1)
                        for j in range(T):
                            mm = eng.matmul(accR[:, :], adj[k][:, j * P:(j + 1) * P], xf[:, j, :],
                                            start=(j == 0), stop=(j == T - 1))
                        mm.then_inc(accR_ready, 1)
                        eng.drain()
                        eng.sem_inc(adj_free, 1)

                    def rows_transposed(p, k):
                        eng.wait_ge(rowR_ready, seq(step, p, k) + 1)
                        eng.wait_ge(xTR_ready, seq(step, p, k) + 1)
                        eng.transpose(xt[:, 0, :], rowR[k][:, :], ident[:, :]).then_inc(xtR_ready, 1)

                    def attend(p, k):
                        t = seq(step, p, k)
                        eng.wait_ge(w_ready, t + 1)

                        def turn(c):
                            sl = cols(c)
                            for j in range(sl.start // P, sl.stop // P):
                                o = j * P - sl.start
                                mm = eng.transpose(tr[(k * NC + c) % 2][:, o:o + P],
                                                   e[k][:, j * P:(j + 1) * P], ident[:, :])
                            mm.then_inc(tr_ready, 1)

                        turn(0)
                        for c in range(NC):
                            if c + 1 < NC:
                                turn(c + 1)
                            if c + 2 == NC:
                                eng.drain()
                                eng.sem_inc(e_free, 1)
                            eng.wait_ge(wT_ready, t * NC + c + 1)
                            if c == 0:
                                eng.wait_ge(rowA_ready, t + 1)
                            sl = cols(c)
                            for j in range(sl.start // P, sl.stop // P):
                                o = j * P - sl.start
                                mm = eng.matmul(accA[:, :], wT[(k * NC + c) % 2][:, o:o + P], xa[:, j, 0:P],
                                                start=(j == 0), stop=(j == T - 1))
                            if c == NC - 1:
                                mm.then_inc(accA_ready, 1)
                            eng.drain()
                            eng.sem_inc(wT_free, 1)

                    def update(p, k):
                        t = seq(step, p, k)
                        eng.wait_ge(rowA_ready, t + 2)
                        eng.wait_ge(xTR_ready, seq(step, p, 1) + 2)
                        eng.transpose(xt[:, 1, :], rowA[k][:, :], ident[:, :]).then_inc(xtA_ready, 1)
                        eng.wait_ge(zs_ready, t + 1)
                        eng.matmul(zp[:, :], xTR[k][:, :], UT[:, 0, step, :], start=True, stop=False)
                        eng.wait_ge(xTA_ready, t + 1)
                        eng.matmul(zp[:, :], xTA[k][:, :], UT[:, 1, step, :], start=False, stop=True)\
                           .then_inc(z_ready, 1)

                    def pair(p, last):
                        rows(p, 0)
                        rows(p, 1)
                        if not last:
                            logits(p + 1, 0)
                            logits(p + 1, 1)
                        rows_transposed(p, 0)
                        rows_transposed(p, 1)
                        for k in range(2):
                            attend(p, k)
                            update(p, k)

                    eng.wait_ge(added, step * T)
                    for c in range(NC):
                        project(0, W1T[:, :], XT[:, cols(c)], c)
                    for c in range(NC):
                        eng.wait_ge(lg_free, 2 + step * STEP_CH + c + 1)
                        project(1, W2T[:, :], h1[:, cols(c)], c)
                    for c in range(NC):
                        project(2, W3T[:, :], XT[:, cols(c)], c)
                    eng.wait_ge(lg_free, 2 + step * STEP_CH + PROJ)
                    logits(0, 0)
                    logits(0, 1)
                    with eng.Fori(0, PAIRS - 1) as p:
                        pair(p, False)
                    pair(PAIRS - 1, True)

            @block.scalar
            def _(eng):
                eng.sem_inc(lg_free, 2)
                for copied in (rawR_ready, xTR_ready, zs_ready, rowA_ready):
                    eng.sem_inc(copied, 1)
                for step in range(2):

                    def project(which, dst, c):
                        n = step * STEP_CH + which * NC + c
                        eng.wait_ge(lg_ready, n + 1)
                        sl = cols(c)
                        eng.activation(dst[:, sl], lg[n % 2][0:DA, 0:sl.stop - sl.start], ACT.Copy)\
                           .then_inc(lg_free, 1)

                    def copy_logits(p, k):
                        for c in range(NC):
                            sl = cols(c, N)
                            eng.wait_ge(lg_ready, chunk(step, p, k, c) + 1)
                            eng.activation(s[k][:, sl], lg[chunk(step, 0, k, c) % 2][:, 0:sl.stop - sl.start],
                                           ACT.Copy).then_inc(lg_free, 1)

                    def exps(p, k):
                        t = seq(step, p, k)
                        eng.wait_ge(negmax_ready, t + 1)
                        eng.wait_ge(e_free, t + 1)
                        eng.activation(e[k][:, 0:N], s[k][:, :], ACT.Exp, bias=negmax[k][:, :],
                                       accum_out=total[k][:, :])
                        eng.drain()
                        eng.sem_inc(e_ready, 1)

                    def copy_rows(p, k):
                        t = seq(step, p, k)
                        eng.wait_ge(accR_ready, t + 1)
                        eng.activation(rawR[k][:, :], accR[:, :], ACT.Copy).then_inc(rawR_ready, 1)

                    def copy_rows_transposed(p, k):
                        t = seq(step, p, k)
                        eng.wait_ge(xtR_ready, t + 1)
                        eng.activation(xTR[k][:, :], xt[:, 0, :], ACT.Copy).then_inc(xTR_ready, 1)

                    def copy_attended(p, k):
                        t = seq(step, p, k)
                        for c in range(NC):
                            sl = cols(c)
                            n = t * NC + c
                            eng.wait_ge(tr_ready, n + 1)
                            eng.wait_ge(wT_free, n + 1)
                            eng.activation(wT[(k * NC + c) % 2][:, 0:sl.stop - sl.start],
                                           tr[(k * NC + c) % 2][:, 0:sl.stop - sl.start],
                                           ACT.Copy).then_inc(wT_ready, 1)
                        eng.wait_ge(accA_ready, t + 1)
                        eng.activation(rowA[k][:, :], accA[:, :], ACT.Copy, scale=inv_kept[k][:, :])\
                           .then_inc(rowA_ready, 1)
                        eng.wait_ge(xtA_ready, t + 1)
                        eng.activation(xTA[k][:, :], xt[:, 1, :], ACT.Copy).then_inc(xTA_ready, 1)
                        eng.wait_ge(z_ready, t + 1)
                        eng.activation(zs[k][:, :], zp[:, :], ACT.Copy).then_inc(zs_ready, 1)

                    def pair(p, last):
                        exps(p, 0)
                        exps(p, 1)
                        copy_rows(p, 0)
                        copy_rows(p, 1)
                        if not last:
                            copy_logits(p + 1, 0)
                            copy_logits(p + 1, 1)
                        copy_rows_transposed(p, 0)
                        copy_rows_transposed(p, 1)
                        copy_attended(p, 0)
                        copy_attended(p, 1)

                    for c in range(NC):
                        project(0, h1, c)
                    for c in range(NC):
                        project(1, qT, c)
                    for c in range(NC):
                        project(2, kT, c)
                    copy_logits(0, 0)
                    copy_logits(0, 1)
                    with eng.Fori(0, PAIRS - 1) as p:
                        pair(p, False)
                    pair(PAIRS - 1, True)

            @block.vector
            def _(eng):
                flag = eng.alloc_register("open_flag")
                regs = [eng.alloc_register(f"group_flag{q}") for q in range(4)]
                eng.memset(w["flags"][:, :], 0.0)
                eng.memset(w["zero8"][:, :], 0.0)
                for n in range(8):
                    eng.memset(w["index8"][:, n:n + 1], float(n))
                for k in range(2):
                    eng.memset(e[k][:, N:NP + 8], 0.0)
                eng.drain()
                for step in range(2):
                    with eng.Fori(0, PAIRS) as p:
                        for k in range(2):
                            eng.wait_ge(lg_free, 2 + chunk(step, p, k, NC - 1) + 1)
                            eng.memset(gate[:, :], 0.0)
                            eng.max(top[k][:, :], s[k][:, :])
                            eng.drain()
                            eng.tensor_scalar(negmax[k][:, :], top[k][:, 0:1], -1.0, None, ALU.mult)\
                               .then_inc(negmax_ready, 1)
                        for k in range(2):
                            eng.wait_ge(e_ready, seq(step, p, k) + 1)
                            top_p_select(eng, w, e[k][:, :], NP, N, total[k][:, :], flag, regs)
                            eng.reciprocal(inv_kept[k][:, :], w["kept"][:, :]).then_inc(w_ready, 1)
                            if k == 0:
                                for r in range(2):
                                    eng.wait_ge(sum_ready, seq(step, p, r) + 1)
                                    eng.reciprocal(inv_sum[r][:, :], rawR[r][:, P:P + 1]).then_inc(inv_ready, 1)


def layernorm_rows(eng, x, sq, stat, rstd, std_ready, var_ready, turn, T):
    def spread(v):
        return v[:, :].unsqueeze(2).to_broadcast([P, T, P])

    eng.tensor_reduce(stat[:, :], x[:, :, :], AX.X, ALU.add)
    eng.drain()
    eng.tensor_scalar(stat[:, :], stat[:, :], 1.0 / P, None, ALU.mult)
    eng.drain()
    eng.tensor_tensor(x[:, :, :], x[:, :, :], spread(stat), ALU.subtract)
    eng.drain()
    eng.tensor_tensor(sq[:, :, :], x[:, :, :], x[:, :, :], ALU.mult)
    eng.drain()
    eng.tensor_reduce(stat[:, :], sq[:, :, :], AX.X, ALU.add)
    eng.drain()
    eng.tensor_scalar(stat[:, :], stat[:, :], 1.0 / P, EPS, ALU.mult, ALU.add).then_inc(var_ready, 1)
    eng.wait_ge(std_ready, turn)
    eng.reciprocal(rstd[:, :], stat[:, :])
    eng.drain()
    eng.tensor_tensor(x[:, :, :], x[:, :, :], spread(rstd), ALU.mult)
    eng.drain()


def roots(eng, stat, std_ready, var_ready, turns):
    for n in range(turns):
        eng.wait_ge(var_ready, n + 1)
        eng.activation(stat[:, :], stat[:, :], ACT.Sqrt).then_inc(std_ready, 1)


def normalize(nc, d, dims, H):
    N, NP, T = dims
    with ExitStack() as ctx:
        sb, ps, sem = scope(nc, ctx)
        X = sb("ln_x", [P, T, P])
        sq = sb("ln_sq", [P, T, P])
        g = sb("ln_gain", [P, P])
        b = sb("ln_bias", [P, P])
        stat = sb("ln_stat", [P, T])
        rstd = sb("ln_rstd", [P, T])
        loaded, var_ready, std_ready = sem("ln_loaded"), sem("ln_var_ready"), sem("ln_std_ready")
        with nc.Block() as block:
            @block.sync
            def _(eng):
                eng.dma_start(X[:, :, :], d["x_rows"]).then_inc(loaded, 16)
                eng.dma_start(g[:, :], d["ln_g"].partition_broadcast(P)).then_inc(loaded, 16)
                eng.dma_start(b[:, :], d["ln_b"].partition_broadcast(P)).then_inc(loaded, 16)

            @block.scalar
            def _(eng):
                roots(eng, stat, std_ready, var_ready, 2)

            @block.vector
            def _(eng):
                def over_tiles(v):
                    return v[:, :].unsqueeze(1).to_broadcast([P, T, P])

                layernorm_rows(eng, H, sq, stat, rstd, std_ready, var_ready, 1, T)
                eng.wait_ge(loaded, 48)
                eng.tensor_tensor(H[:, :, :], H[:, :, :], over_tiles(g), ALU.mult)
                eng.drain()
                eng.tensor_tensor(H[:, :, :], H[:, :, :], over_tiles(b), ALU.add)
                eng.drain()
                eng.tensor_tensor(H[:, :, :], H[:, :, :], X[:, :, :], ALU.add)
                eng.drain()
                layernorm_rows(eng, H, sq, stat, rstd, std_ready, var_ready, 2, T)


def graph_sums(nc, d, dims, H, ident, diag, nsT, epm, negs):
    N, NP, T = dims
    HEADS = 3
    PAIRS = T // 2
    with ExitStack() as ctx:
        sb, ps, sem = scope(nc, ctx)
        hT = sb("hT", [P, NP])
        adj = [sb(f"g_adj{i}", [P, NP]) for i in range(2)]
        pos = [sb(f"pos{i}", [P, NP], BF16) for i in range(2)]
        neg = [sb(f"neg{i}", [P, NP], BF16) for i in range(2)]
        dblock = [sb(f"dblock{i}", [P, P]) for i in range(2)]
        dsum = [sb(f"dsum{i}", [P, 1]) for i in range(2)]
        WT = sb("gat_WT_s", [P, HEADS, P])
        av = sb("gat_a_s", [P, HEADS, 2])
        V = sb("V", [P, 3, HEADS])
        Y = sb("Y", [P, T, 3, 9], BF16)
        y0 = sb("y0", [P, T, 9])
        y1 = sb("y1", [P, T, 9])
        ones = sb("ones_bf", [P, 1], BF16)
        raw = sb("raw_e", [P, T, 18])
        esum = sb("esum", [P, T, 6])

        tp = [ps(f"g_tp{i}", [P, 512]) for i in range(2)]
        vp = ps("g_vp", [P, 3, 2])
        yp = ps("g_yp", [P, T, 9])
        sp = ps("g_sp", [P, P])
        ep = ps("g_ep", [P, 3, 6])
        np_ = ps("g_np", [P, 1])

        loaded = sem("g_loaded")
        adj_loaded = [sem(f"g_adj_loaded{i}") for i in range(2)]
        adj_free = sem("g_adj_free")
        mask_free = sem("g_mask_free")
        ones_ready = sem("g_ones_ready")
        hT_turned, hT_ready = sem("g_hT_turned"), sem("g_hT_ready")
        v_summed, v_ready = sem("g_v_summed"), sem("g_v_ready")
        y_summed, y_ready = sem("g_y_summed"), sem("g_y_ready")
        mask_ready = sem("g_mask_ready")
        sums_ready, sums_copied = sem("g_sums_ready"), sem("g_sums_copied")
        NC = -(-T // 4)

        with nc.Block() as block:
            @block.sync
            def _(eng):
                eng.dma_start(WT[:, :, :], d["gat_WT"]).then_inc(loaded, 16)
                eng.dma_start(av[:, :, :], d["gat_a"]).then_inc(loaded, 16)
                with eng.Fori(0, PAIRS) as p:
                    for k in range(2):
                        eng.wait_ge(adj_free, p * 2 + k + 1)
                        eng.dma_start(adj[k][:, :], d["adjT"][bass.ds((p * 2 + k) * P, P), :])\
                           .then_inc(adj_loaded[k], 16)

            @block.tensor
            def _(eng):
                eng.sem_inc(adj_free, 2)
                eng.sem_inc(mask_free, 2)
                for c in range(NC):
                    if c >= 2:
                        eng.wait_ge(hT_ready, c - 1)
                    for j in range(4 * c, min(4 * c + 4, T)):
                        mm = eng.transpose(tp[c % 2][:, (j % 4) * P:(j % 4 + 1) * P], H[:, j, :], ident[:, :])
                    mm.then_inc(hT_turned, 1)
                eng.wait_ge(loaded, 32)
                for h in range(HEADS):
                    mm = eng.matmul(vp[:, h, :], WT[:, h, :], av[:, h, :], start=True, stop=True)
                mm.then_inc(v_summed, 1)
                eng.wait_ge(hT_ready, NC)
                eng.wait_ge(v_ready, 1)
                for j in range(T):
                    mm = eng.matmul(yp[:, j, :], hT[:, j * P:(j + 1) * P], V[:, :, :].rearrange("p a b -> p (a b)"),
                                    start=True, stop=True)
                mm.then_inc(y_summed, 1)
                eng.wait_ge(y_ready, 1)
                eng.wait_ge(ones_ready, 1)

                def tile(p, k):
                    t = p * 2 + k
                    eng.wait_ge(mask_ready, t + 1)
                    eng.wait_ge(sums_copied, t + 1)
                    for j in range(T):
                        eng.matmul(sp[:, :], H[:, j, :], adj[k][:, j * P:(j + 1) * P],
                                   start=(j == 0), stop=(j == T - 1))
                    eng.drain()
                    eng.sem_inc(adj_free, 1)
                    for j in range(T):
                        sl = slice(j * P, (j + 1) * P)
                        eng.matmul(ep[:, :, :], pos[k][:, sl], Y[:, j, :, 0:6], start=(j == 0), stop=False)
                        eng.matmul(ep[:, :, :], neg[k][:, sl], Y[:, j, :, 3:9], start=False, stop=(j == T - 1))
                    for j in range(T):
                        eng.matmul(np_[:, :], neg[k][:, j * P:(j + 1) * P], ones[:, :],
                                   start=(j == 0), stop=(j == T - 1))
                    eng.drain()
                    eng.sem_inc(sums_ready, 1)
                    eng.sem_inc(mask_free, 1)

                with eng.Fori(0, PAIRS) as p:
                    tile(p, 0)
                    tile(p, 1)

            @block.scalar
            def _(eng):
                eng.sem_inc(sums_copied, 1)
                for c in range(NC):
                    n = min(512, NP - c * 512)
                    eng.wait_ge(hT_turned, c + 1)
                    eng.activation(hT[:, c * 512:c * 512 + n], tp[c % 2][:, 0:n], ACT.Copy).then_inc(hT_ready, 1)
                with eng.Fori(0, PAIRS) as p:
                    for k in range(2):
                        t = p * 2 + k
                        eng.wait_ge(sums_ready, t + 1)
                        eng.activation(nsT[:, bass.ds(t * P, P)], sp[:, :], ACT.Copy)
                        eng.activation(raw[:, bass.ds(t, 1), :], ep[:, :, :].rearrange("p a b -> p (a b)")
                                       .unsqueeze(1), ACT.Copy)
                        eng.activation(negs[:, bass.ds(t, 1)], np_[:, :], ACT.Copy)
                        eng.drain()
                        eng.sem_inc(sums_copied, 1)

            @block.vector
            def _(eng):
                eng.memset(ones[:, :], 1.0).then_inc(ones_ready, 1)
                eng.wait_ge(v_summed, 1)
                for part in range(3):
                    mm = eng.tensor_copy(V[:, part, :], vp[:, :, part % 2])
                mm.then_inc(v_ready, 1)
                eng.wait_ge(y_summed, 1)
                eng.tensor_copy(y0[:, :, :], yp[:, :, :])
                eng.drain()
                eng.tensor_copy(Y[:, :, 0, :], y0[:, :, :])
                eng.drain()
                eng.tensor_tensor(y1[:, :, :], y0[:, :, :], Y[:, :, 0, :], ALU.subtract)
                eng.drain()
                eng.tensor_copy(Y[:, :, 1, :], y1[:, :, :])
                eng.drain()
                eng.tensor_tensor(y0[:, :, :], y1[:, :, :], Y[:, :, 1, :], ALU.subtract)
                eng.drain()
                eng.tensor_copy(Y[:, :, 2, :], y0[:, :, :]).then_inc(y_ready, 1)
                with eng.Fori(0, PAIRS) as p:
                    for k in range(2):
                        t = p * 2 + k
                        eng.wait_ge(adj_loaded[k], (p + 1) * 16)
                        block_ = adj[k][:, bass.ds(t * P, P)]
                        eng.tensor_tensor(dblock[k][:, :], block_, ident[:, :], ALU.mult)
                        eng.drain()
                        eng.tensor_tensor(block_, block_, dblock[k][:, :], ALU.subtract)
                        eng.tensor_reduce(dsum[k][:, :], dblock[k][:, :], AX.X, ALU.add)
                        eng.drain()
                        eng.tensor_copy(diag[:, bass.ds(t, 1)], dsum[k][:, :])
                        eng.wait_ge(mask_free, t + 1)
                        eng.tensor_scalar(pos[k][:, :], adj[k][:, :], 0.0, None, ALU.is_gt)
                        eng.tensor_scalar(neg[k][:, :], adj[k][:, :], 0.0, None, ALU.is_lt)
                        eng.drain()
                        eng.sem_inc(mask_ready, 1)
                eng.wait_ge(sums_copied, T + 1)
                eng.tensor_tensor(esum[:, :, :], raw[:, :, 0:6], raw[:, :, 6:12], ALU.add)
                eng.drain()
                eng.tensor_tensor(esum[:, :, :], esum[:, :, :], raw[:, :, 12:18], ALU.add)
                eng.drain()
                eng.scalar_tensor_tensor(epm[:, :, :], esum[:, :, :], 0.2, esum[:, :, :], ALU.mult, ALU.max)


def attention(nc, d, dims, H, ident, epm, negs, gsT):
    N, NP, T = dims
    HEADS = 3
    PAIRS = T // 2
    NC = -(-NP // 512)
    with ExitStack() as ctx:
        sb, ps, sem = scope(nc, ctx)
        EB = sb("EB", [P, 2 * HEADS, NP])
        adj = [sb(f"a_adj{i}", [P, NP]) for i in range(2)]
        off = sb("off", [P, NP])
        alt = sb("alt", [P, NP])
        prob = [sb(f"prob{i}", [P, NP]) for i in range(2)]
        pT = [sb(f"pT{i}", [P, 512]) for i in range(2)]
        W = sb("gat_W_s", [P, HEADS, P])
        dblock = sb("a_dblock", [P, P])
        mx = sb("a_mx", [P, 1])
        gate = sb("a_gate", [P, 1])
        negmax = [sb(f"a_negmax{i}", [P, 1]) for i in range(2)]
        den = [sb(f"a_den{i}", [P, 1]) for i in range(2)]
        inv = [sb(f"a_inv{i}", [P, 1]) for i in range(2)]
        rows = sb("a_rows", [P, P])
        rowsT = sb("a_rowsT", [P, HEADS, P])
        w = {"flags": sb("a_flags", [P, 32]), "flags_t": sb("a_flags_t", [P, 32]),
             "flag_max": sb("a_flag_max", [P, 1]), "flag_int": sb("a_flag_int", [P, 1], I32)}

        tr = [ps(f"a_tr{i}", [P, 512]) for i in range(2)]
        acc = ps("a_acc", [P, P])
        rt = ps("a_rt", [P, P])
        sup = ps("a_sup", [P, P])

        loaded = sem("a_loaded")
        adj_loaded = [sem(f"a_adj_loaded{i}") for i in range(2)]
        adj_free = sem("a_adj_free")
        prob_free = sem("a_prob_free")
        eb_turned, eb_ready = sem("a_eb_turned"), sem("a_eb_ready")
        diag_out = sem("a_diag_out")
        logit_ready = sem("a_logit_ready")
        exp_ready = sem("a_exp_ready")
        inv_ready = sem("a_inv_ready")
        weight_ready = sem("a_weight_ready")
        tr_ready = sem("a_tr_ready")
        pT_ready = sem("a_pT_ready")
        pT_free = sem("a_pT_free")
        acc_ready = sem("a_acc_ready")
        rows_ready = sem("a_rows_ready")
        rt_ready = sem("a_rt_ready")
        rowsT_ready = sem("a_rowsT_ready")
        sup_ready = sem("a_sup_ready")
        sup_copied = sem("a_sup_copied")

        def seq(p, k, h):
            return (p * 2 + k) * HEADS + h

        def slot(k, h):
            return (k * HEADS + h) % 2

        with nc.Block() as block:
            @block.sync
            def _(eng):
                eng.dma_start(W[:, :, :], d["gat_W"]).then_inc(loaded, 16)
                with eng.Fori(0, PAIRS) as p:
                    for k in range(2):
                        eng.wait_ge(adj_free, p * 2 + k + 1)
                        eng.dma_start(adj[k][:, :], d["adj"][bass.ds((p * 2 + k) * P, P), :])\
                           .then_inc(adj_loaded[k], 16)

            @block.tensor
            def _(eng):
                eng.sem_inc(prob_free, 2)
                eng.sem_inc(pT_free, 2)
                eng.sem_inc(sup_ready, 1)
                for g in range(2 * HEADS * NC):
                    h, c = g // NC, g % NC
                    if g >= 2:
                        eng.wait_ge(eb_ready, g - 1)
                    for j in range(4 * c, min(4 * c + 4, T)):
                        mm = eng.transpose(tr[g % 2][:, (j % 4) * P:(j % 4 + 1) * P],
                                           epm[:, j, h:h + 1].to_broadcast([P, P]), ident[:, :])
                    mm.then_inc(eb_turned, 1)
                eng.wait_ge(eb_ready, 2 * HEADS * NC)
                eng.wait_ge(loaded, 16)

                def head(p, k, h):
                    q = seq(p, k, h)
                    b = slot(k, h)
                    eng.wait_ge(weight_ready, q + 1)

                    def turn(c):
                        for j in range(4 * c, min(4 * c + 4, T)):
                            mm = eng.transpose(tr[(b * NC + c) % 2][:, (j % 4) * P:(j % 4 + 1) * P],
                                               prob[b][:, j * P:(j + 1) * P], ident[:, :])
                        mm.then_inc(tr_ready, 1)

                    turn(0)
                    for c in range(NC):
                        if c + 1 < NC:
                            turn(c + 1)
                        if c + 2 == NC:
                            eng.drain()
                            eng.sem_inc(prob_free, 1)
                        eng.wait_ge(pT_ready, q * NC + c + 1)
                        if c == 0:
                            eng.wait_ge(rows_ready, q + 1)
                        for j in range(4 * c, min(4 * c + 4, T)):
                            mm = eng.matmul(acc[:, :], pT[(b * NC + c) % 2][:, (j % 4) * P:(j % 4 + 1) * P],
                                            H[:, j, :], start=(j == 0), stop=(j == T - 1))
                        if c == NC - 1:
                            mm.then_inc(acc_ready, 1)
                        eng.drain()
                        eng.sem_inc(pT_free, 1)
                    eng.wait_ge(rows_ready, q + 2)
                    eng.wait_ge(rowsT_ready, q + 1)
                    eng.transpose(rt[:, :], rows[:, :], ident[:, :]).then_inc(rt_ready, 1)

                with eng.Fori(0, PAIRS) as p:
                    for k in range(2):
                        for h in range(HEADS):
                            head(p, k, h)
                        eng.wait_ge(rowsT_ready, seq(p, k, HEADS - 1) + 2)
                        eng.wait_ge(sup_copied, p * 2 + k + 1)
                        for h in range(HEADS):
                            mm = eng.matmul(sup[:, :], W[:, h, :], rowsT[:, h, :],
                                            start=(h == 0), stop=(h == HEADS - 1))
                        mm.then_inc(sup_ready, 1)

            @block.scalar
            def _(eng):
                for copied in (rows_ready, rowsT_ready, sup_copied):
                    eng.sem_inc(copied, 1)
                for g in range(2 * HEADS * NC):
                    h, c = g // NC, g % NC
                    n = min(512, NP - c * 512)
                    eng.wait_ge(eb_turned, g + 1)
                    eng.activation(EB[:, h, c * 512:c * 512 + n], tr[g % 2][:, 0:n], ACT.Copy)\
                       .then_inc(eb_ready, 1)

                def exp(p, k, h):
                    b = slot(k, h)
                    eng.wait_ge(logit_ready, seq(p, k, h) + 1)
                    eng.activation(prob[b][:, :], prob[b][:, :], ACT.Exp, bias=negmax[b][:, :],
                                   accum_out=den[b][:, :])
                    eng.drain()
                    eng.sem_inc(exp_ready, 1)

                def copies(p, k, h):
                    b = slot(k, h)
                    q = seq(p, k, h)
                    for c in range(NC):
                        n = min(512, NP - c * 512)
                        eng.wait_ge(tr_ready, q * NC + c + 1)
                        eng.wait_ge(pT_free, q * NC + c + 1)
                        eng.activation(pT[(b * NC + c) % 2][:, 0:n], tr[(b * NC + c) % 2][:, 0:n], ACT.Copy)\
                           .then_inc(pT_ready, 1)
                    eng.wait_ge(acc_ready, q + 1)
                    eng.wait_ge(inv_ready, q + 1)
                    eng.activation(rows[:, :], acc[:, :], ACT.Copy, scale=inv[b][:, :]).then_inc(rows_ready, 1)
                    eng.wait_ge(rt_ready, q + 1)
                    if h == 0:
                        eng.wait_ge(sup_ready, p * 2 + k + 1)
                    eng.activation(rowsT[:, h, :], rt[:, :], ACT.Copy).then_inc(rowsT_ready, 1)

                def support(p, k):
                    t = p * 2 + k
                    eng.wait_ge(sup_ready, t + 2)
                    eng.activation(gsT[:, bass.ds(t * P, P)], sup[:, :], ACT.Copy, scale=1.0 / HEADS)
                    eng.drain()
                    eng.sem_inc(sup_copied, 1)

                order = [(k, h) for k in range(2) for h in range(HEADS)]

                def pair(p, last):
                    for n, (k, h) in enumerate(order):
                        if n + 1 < len(order):
                            exp(p, *order[n + 1])
                        elif not last:
                            exp(p + 1, 0, 0)
                        copies(p, k, h)
                        if h == HEADS - 1:
                            support(p, k)

                exp(0, 0, 0)
                with eng.Fori(0, PAIRS - 1) as p:
                    pair(p, False)
                pair(PAIRS - 1, True)

            @block.gpsimd
            def _(eng):
                eng.sem_inc(adj_free, 2)
                with eng.Fori(0, PAIRS) as p:
                    for k in range(2):
                        for h in range(HEADS):
                            b = slot(k, h)
                            eng.wait_ge(exp_ready, seq(p, k, h) + 1)
                            eng.tensor_tensor(prob[b][:, :], prob[b][:, :], adj[k][:, :], ALU.mult)
                            eng.drain()
                            eng.sem_inc(weight_ready, 1)
                        eng.sem_inc(adj_free, 1)

            @block.vector
            def _(eng):
                flag = eng.alloc_register("negative_flag")
                regs = [eng.alloc_register(f"neg_group{q}") for q in range(4)]
                eng.memset(w["flags"][:, :], 0.0)
                eng.drain()
                eng.tensor_reduce(w["flags"][:, 0:1], negs[:, :], AX.X, ALU.max)
                any_row_flag(eng, w, flag, regs)
                eng.wait_ge(eb_ready, 2 * HEADS * NC)
                with eng.Fori(0, PAIRS) as p:
                    for k in range(2):
                        t = p * 2 + k
                        eng.wait_ge(adj_loaded[k], (p + 1) * 16)
                        block_ = adj[k][:, bass.ds(t * P, P)]
                        eng.tensor_tensor(dblock[:, :], block_, ident[:, :], ALU.mult)
                        eng.drain()
                        eng.tensor_tensor(block_, block_, dblock[:, :], ALU.subtract)
                        eng.drain()
                        for h in range(HEADS):
                            q = seq(p, k, h)
                            b = slot(k, h)
                            if h == 0:
                                eng.tensor_scalar(off[:, :], adj[k][:, :], 0.0, NEG, ALU.is_le, ALU.mult)
                                eng.drain()
                            eng.wait_ge(prob_free, q + 1)
                            eng.memset(gate[:, :], 0.0)
                            eng.tensor_tensor_reduce(prob[b][:, :], off[:, :], EB[:, h, :], 1.0, -3.0e38,
                                                     ALU.add, ALU.max, mx[:, :])
                            eng.drain()
                            with eng.If(eng.snap(flag) > 0):
                                eng.tensor_scalar(alt[:, :], adj[k][:, :], 0.0, NEG, ALU.is_ge, ALU.mult)
                                eng.drain()
                                eng.tensor_tensor(alt[:, :], alt[:, :], EB[:, HEADS + h, :], ALU.add)
                                eng.drain()
                                eng.tensor_tensor(prob[b][:, :], prob[b][:, :], alt[:, :], ALU.max)
                                eng.drain()
                                eng.tensor_reduce(mx[:, :], prob[b][:, :], AX.X, ALU.max)
                                eng.drain()
                            eng.tensor_scalar(negmax[b][:, :], mx[:, :], -1.0, None, ALU.mult)\
                               .then_inc(logit_ready, 1)
                            eng.wait_ge(exp_ready, q + 1)
                            eng.reciprocal(inv[b][:, :], den[b][:, :]).then_inc(inv_ready, 1)


def gates_and_output(nc, d, dims, H, ident, diag, nsT, gsT):
    N, NP, T = dims
    PAIRS = T // 2
    with ExitStack() as ctx:
        sb, ps, sem = scope(nc, ctx)
        Wi = [sb(f"Wi{g}", [P, 3 * P]) for g in range(2)]
        Wh = [sb(f"Wh{g}", [P, 3 * P]) for g in range(2)]
        bi = [sb(f"bi{g}", [1, 3 * P]) for g in range(2)]
        bh = [sb(f"bh{g}", [1, 3 * P]) for g in range(2)]
        ones = sb("ones_row", [1, P])
        O = sb("O", [P, T, P])
        sq = sb("o_sq", [P, T, P])
        stat = sb("o_stat", [P, T])
        rstd = sb("o_rstd", [P, T])
        h = [sb(f"h_tile{k}", [P, P]) for k in range(2)]
        sT = [[sb(f"sT{g}{k}", [P, P]) for k in range(2)] for g in range(2)]
        hTt = [sb(f"hT_tile{k}", [P, P]) for k in range(2)]
        rz = [sb(f"rz{g}", [P, 2 * P]) for g in range(2)]
        cand = [sb(f"cand{g}", [P, P]) for g in range(2)]
        nn = [sb(f"nn{g}", [P, P]) for g in range(2)]
        mix = [sb(f"mix{g}", [P, P]) for g in range(2)]
        tp = ps("o_tp", [P, P])
        gp = [ps(f"o_gp{g}", [P, 4 * P]) for g in range(2)]

        loaded, ones_ready = sem("o_loaded"), sem("o_ones_ready")
        tiles_ready, tiles_free = sem("o_tiles_ready"), sem("o_tiles_free")
        tp_ready, hT_ready = sem("o_tp_ready"), sem("o_hT_ready")
        gates_summed, gates_used = sem("o_gates_summed"), sem("o_gates_used")
        rz_ready, cand_ready, nn_ready, mixed = (sem("o_rz_ready"), sem("o_cand_ready"),
                                                 sem("o_nn_ready"), sem("o_mixed"))
        var_ready, std_ready = sem("o_var_ready"), sem("o_std_ready")
        normed, stored = sem("o_normed"), sem("o_stored")

        with nc.Block() as block:
            @block.sync
            def _(eng):
                for g, name in enumerate(("edge", "node")):
                    eng.dma_start(Wi[g][:, :], d[f"{name}_WihT"]).then_inc(loaded, 16)
                    eng.dma_start(Wh[g][:, :], d[f"{name}_WhhT"]).then_inc(loaded, 16)
                    eng.dma_start(bi[g][:, :], d[f"{name}_bih"]).then_inc(loaded, 16)
                    eng.dma_start(bh[g][:, :], d[f"{name}_bhh"]).then_inc(loaded, 16)
                eng.wait_ge(normed, 1)
                whole = N // P
                eng.dma_start(d["out"][0:whole * P, :].rearrange("(t p) d -> p t d", p=P), H[:, 0:whole, :])\
                   .then_inc(stored, 16)
                if N % P:
                    eng.dma_start(d["out"][whole * P:N, :], H[0:N % P, whole, :]).then_inc(stored, 16)
                eng.wait_ge(stored, 32 if N % P else 16)

            @block.gpsimd
            def _(eng):
                eng.sem_inc(tiles_free, 2)
                with eng.Fori(0, PAIRS) as p:
                    for k in range(2):
                        t = p * 2 + k
                        eng.wait_ge(tiles_free, t + 1)
                        eng.tensor_copy(h[k][:, :], H[:, bass.ds(t, 1), :].rearrange("p a b -> p (a b)"))
                        eng.tensor_copy(sT[0][k][:, :], nsT[:, bass.ds(t * P, P)])
                        eng.tensor_copy(sT[1][k][:, :], gsT[:, bass.ds(t * P, P)])
                        eng.drain()
                        eng.sem_inc(tiles_ready, 1)

            @block.tensor
            def _(eng):
                eng.wait_ge(loaded, 16 * 8)
                eng.wait_ge(ones_ready, 1)
                with eng.Fori(0, PAIRS) as p:
                    for k in range(2):
                        t = p * 2 + k
                        eng.wait_ge(tiles_ready, t + 1)
                        eng.transpose(tp[:, :], h[k][:, :], ident[:, :]).then_inc(tp_ready, 1)
                        eng.wait_ge(hT_ready, t + 1)
                        for g in range(2):
                            eng.wait_ge(gates_used, t * 2 + g + 1)
                            rzp, inp, hnp = gp[g][:, 0:2 * P], gp[g][:, 2 * P:3 * P], gp[g][:, 3 * P:4 * P]
                            RZ, NN = slice(0, 2 * P), slice(2 * P, 3 * P)
                            eng.matmul(rzp, sT[g][k][:, :], Wi[g][:, RZ], start=True, stop=False)
                            eng.matmul(rzp, hTt[k][:, :], Wh[g][:, RZ], start=False, stop=False)
                            eng.matmul(rzp, ones[:, :], bi[g][:, RZ], start=False, stop=False)
                            eng.matmul(rzp, ones[:, :], bh[g][:, RZ], start=False, stop=True)
                            eng.matmul(inp, sT[g][k][:, :], Wi[g][:, NN], start=True, stop=False)
                            eng.matmul(inp, ones[:, :], bi[g][:, NN], start=False, stop=True)
                            eng.matmul(hnp, hTt[k][:, :], Wh[g][:, NN], start=True, stop=False)
                            eng.matmul(hnp, ones[:, :], bh[g][:, NN], start=False, stop=True)\
                               .then_inc(gates_summed, 1)

            @block.scalar
            def _(eng):
                with eng.Fori(0, PAIRS) as p:
                    for k in range(2):
                        t = p * 2 + k
                        eng.wait_ge(tp_ready, t + 1)
                        eng.activation(hTt[k][:, :], tp[:, :], ACT.Copy).then_inc(hT_ready, 1)
                        for g in range(2):
                            eng.wait_ge(gates_summed, t * 2 + g + 1)
                            eng.wait_ge(mixed, t + 1)
                            eng.activation(rz[g][:, :], gp[g][:, 0:2 * P], ACT.Sigmoid).then_inc(rz_ready, 1)
                            eng.wait_ge(cand_ready, t * 2 + g + 1)
                            eng.activation(nn[g][:, :], cand[g][:, :], ACT.Tanh).then_inc(nn_ready, 1)
                roots(eng, stat, std_ready, var_ready, 1)

            @block.vector
            def _(eng):
                eng.memset(ones[:, :], 1.0).then_inc(ones_ready, 1)
                eng.sem_inc(gates_used, 1)
                eng.sem_inc(mixed, 1)
                with eng.Fori(0, PAIRS) as p:
                    for k in range(2):
                        t = p * 2 + k
                        for g in range(2):
                            eng.wait_ge(rz_ready, t * 2 + g + 1)
                            eng.tensor_tensor(cand[g][:, :], rz[g][:, 0:P], gp[g][:, 3 * P:4 * P], ALU.mult)
                            eng.drain()
                            eng.tensor_tensor(cand[g][:, :], cand[g][:, :], gp[g][:, 2 * P:3 * P], ALU.add)
                            eng.drain()
                            eng.sem_inc(cand_ready, 1)
                            eng.sem_inc(gates_used, 1)
                        for g in range(2):
                            eng.wait_ge(nn_ready, t * 2 + g + 1)
                            eng.tensor_tensor(mix[g][:, :], h[k][:, :], nn[g][:, :], ALU.subtract)
                            eng.drain()
                            eng.tensor_tensor(mix[g][:, :], mix[g][:, :], rz[g][:, P:2 * P], ALU.mult)
                            eng.drain()
                            eng.tensor_tensor(mix[g][:, :], mix[g][:, :], nn[g][:, :], ALU.add)
                            eng.drain()
                        eng.tensor_tensor(O[:, bass.ds(t, 1), :], mix[0][:, :].unsqueeze(1),
                                          mix[1][:, :].unsqueeze(1), ALU.add)
                        eng.drain()
                        eng.sem_inc(mixed, 1)
                        eng.sem_inc(tiles_free, 1)
                eng.tensor_tensor(O[:, :, :], O[:, :, :], diag[:, :].unsqueeze(2).to_broadcast([P, T, P]), ALU.mult)
                eng.drain()
                eng.tensor_tensor(H[:, :, :], H[:, :, :], O[:, :, :], ALU.add)
                eng.drain()
                layernorm_rows(eng, H, sq, stat, rstd, std_ready, var_ready, 1, T)
                eng.sem_inc(normed, 1)


def program(nc, d, dims):
    N, NP, T = dims
    with ExitStack() as ctx:
        sb, ps, sem = scope(nc, ctx)
        H = sb("H", [P, T, P])
        ident = sb("ident", [P, P])
        layer0(nc, d, dims, H, ident)
        normalize(nc, d, dims, H)
        diag = sb("diag", [P, T])
        nsT = sb("nsT", [P, NP])
        epm = sb("epm", [P, T, 6])
        negs = sb("negs", [P, T])
        graph_sums(nc, d, dims, H, ident, diag, nsT, epm, negs)
        gsT = sb("gsT", [P, NP])
        attention(nc, d, dims, H, ident, epm, negs, gsT)
        gates_and_output(nc, d, dims, H, ident, diag, nsT, gsT)


def kernel(x, adj, L0_gnn_W1, L0_gnn_W2, L0_gnn_W3, L0_gnn_U1, L0_gnn_U2, L0_gnn_ln_g, L0_gnn_ln_b,
           L1_gnn_gat_W, L1_gnn_gat_a, L1_gnn_edge_Wih, L1_gnn_edge_Whh, L1_gnn_edge_bih, L1_gnn_edge_bhh,
           L1_gnn_node_Wih, L1_gnn_node_Whh, L1_gnn_node_bih, L1_gnn_node_bhh):
    import numpy as np
    import concourse.bacc as bacc
    from concourse.bass_utils import run_bass_kernel_spmd

    c = np.ascontiguousarray
    N, D = x.shape
    T = -(-N // P)
    T += T % 2
    NP = T * P
    rows = np.concatenate([x] + [x[-1:]] * (NP - N), axis=0)
    adj_rows = np.zeros((NP, NP), adj.dtype)
    adj_rows[:N, :N] = adj
    arrays = {
        "x_rows": rows,
        "x_t": c(rows.T),
        "adj": adj_rows,
        "adjT": c(adj_rows.reshape(T, P, T, P).transpose(0, 3, 2, 1)).reshape(NP, NP),
        "W1T": c(L0_gnn_W1.T), "W2T": c(L0_gnn_W2.T), "W3T": c(L0_gnn_W3.T),
        "U1T": c(L0_gnn_U1.transpose(2, 0, 1)), "U2T": c(L0_gnn_U2.transpose(2, 0, 1)),
        "ln_g": c(L0_gnn_ln_g), "ln_b": c(L0_gnn_ln_b),
        "gat_W": c(L1_gnn_gat_W.transpose(1, 0, 2)), "gat_WT": c(L1_gnn_gat_W.transpose(2, 0, 1)),
        "gat_a": c(L1_gnn_gat_a.reshape(-1, 2, D).transpose(2, 0, 1)),
        "edge_WihT": c(L1_gnn_edge_Wih.T), "edge_WhhT": c(L1_gnn_edge_Whh.T),
        "edge_bih": L1_gnn_edge_bih.reshape(1, -1), "edge_bhh": L1_gnn_edge_bhh.reshape(1, -1),
        "node_WihT": c(L1_gnn_node_Wih.T), "node_WhhT": c(L1_gnn_node_Whh.T),
        "node_bih": L1_gnn_node_bih.reshape(1, -1), "node_bhh": L1_gnn_node_bhh.reshape(1, -1),
    }
    arrays = {f"in_{name}": c(a) for name, a in arrays.items()}
    nc = bacc.Bacc("TRN2", target_bir_lowering=False, num_devices=1)
    d = {name[3:]: nc.dram_tensor(name, a.shape, F32, kind="ExternalInput").ap() for name, a in arrays.items()}
    d["x_rows"] = d["x_rows"].rearrange("(t p) d -> p t d", p=P)
    d["out"] = nc.dram_tensor("out_rows", (N, D), F32, kind="ExternalOutput").ap()
    program(nc, d, (N, NP, T))
    r = run_bass_kernel_spmd(nc, [arrays], core_ids=[0])
    return r.results[0]["out_rows"]
```

```python
from contextlib import ExitStack

import concourse.bass as bass
from concourse import mybir

F32 = mybir.dt.float32
I32 = mybir.dt.int32
BF16 = mybir.dt.bfloat16
ALU = mybir.AluOpType
ACT = mybir.ActivationFunctionType
AX = mybir.AxisListType

P = 128
NEG = -9.0e15
EPS = 1e-5
TOP_P = 0.9
BIG_E = 4.0
HALVINGS = 10
LOW_BITS = 0x37C00000
FIRST_STEP = 1 << 26
OPEN = 16


def scope(nc, ctx):
    def sb(name, shape, dt=F32):
        return ctx.enter_context(nc.sbuf_tensor(name, shape, dt))

    def ps(name, shape, dt=F32):
        return ctx.enter_context(nc.psum_tensor(name, shape, dt))

    def sem(name):
        return ctx.enter_context(nc.semaphore(name))

    return sb, ps, sem


def any_row_flag(eng, w, flag, regs):
    eng.drain()
    eng.transpose(w["flags_t"][:, :], w["flags"][:, :])
    eng.drain()
    eng.tensor_reduce(w["flag_max"][:, :], w["flags_t"][:, :], AX.X, ALU.max)
    eng.drain()
    eng.tensor_copy(w["flag_int"][:, :], w["flag_max"][:, :])
    eng.drain()
    for q in range(4):
        eng.reg_load(regs[q], w["flag_int"][32 * q:32 * q + 1, 0:1])
    eng.reg_add(flag, regs[0], regs[1])
    eng.reg_add(flag, flag, regs[2])
    eng.reg_add(flag, flag, regs[3])


def segment_tops(eng, src, width, cand, seg):
    for n in range(-(-width // seg)):
        eng.max(cand[:, n, :], src[:, n * seg:min((n + 1) * seg, width)])


def solve(eng, works, n_seg):
    def cand(w):
        return w["cand"][:, 0:n_seg, :].rearrange("p a b -> p (a b)")

    def scratch(w):
        return w["cand_work"][:, 0:n_seg * 8]

    def each(*ops):
        for w in works:
            for op in ops:
                op(w)
        eng.drain()

    each(lambda w: eng.tensor_tensor(w["theta1"][:, :], w["theta"][:, :], w["above0"][:, :], ALU.subtract),
         lambda w: eng.memset(w["mid"][:, :], LOW_BITS + FIRST_STEP),
         lambda w: eng.tensor_reduce(w["tau"][:, :], w["cand"][:, 0:n_seg, 7], AX.X, ALU.max))
    step = FIRST_STEP
    for n in range(HALVINGS):
        each(lambda w: eng.scalar_tensor_tensor(scratch(w), cand(w), w["mid"][:, :].bitcast(F32), cand(w),
                                                ALU.is_ge, ALU.mult, accum_out=w["mass"][:, n:n + 1]))
        each(lambda w: eng.tensor_scalar(w["up"][:, :], w["mass"][:, n:n + 1], w["theta1"][:, :], float(step),
                                         ALU.is_ge, ALU.mult))
        back = -step // 2 if n + 1 < HALVINGS else 0
        each(lambda w: eng.scalar_tensor_tensor(w["mid"][:, :], w["up"][:, :], float(back), w["mid"][:, :],
                                                ALU.add, ALU.add))
        step //= 2
    each(lambda w: eng.scalar_tensor_tensor(w["mass"][:, :], w["mass"][:, :], w["theta1"][:, :], w["mass"][:, :],
                                            ALU.is_lt, ALU.mult),
         lambda w: eng.scalar_tensor_tensor(scratch(w), cand(w), w["mid"][:, :].bitcast(F32), cand(w),
                                            ALU.is_lt, ALU.mult))
    each(lambda w: eng.tensor_reduce(w["mass_hi"][:, :], w["mass"][:, :], AX.X, ALU.max),
         lambda w: eng.max(w["top8"][:, :], scratch(w)))
    each(lambda w: eng.tensor_tensor_scan(w["run8"][:, :], w["top8"][:, :], w["zero8"][:, :],
                                          w["mass_hi"][:, :], ALU.add, ALU.add))
    each(lambda w: eng.scalar_tensor_tensor(w["hit8"][:, :], w["run8"][:, :], w["theta1"][:, :],
                                            w["top8"][:, :], ALU.is_ge, ALU.mult))
    each(lambda w: eng.tensor_reduce(w["value"][:, :], w["hit8"][:, :], AX.X, ALU.max))
    each(lambda w: eng.tensor_tensor(w["value"][:, :], w["value"][:, :], w["top8"][:, 7:8], ALU.max))
    each(lambda w: eng.scalar_tensor_tensor(scratch(w), cand(w), w["value"][:, :], cand(w),
                                            ALU.is_ge, ALU.mult, accum_out=w["best"][:, :]),
         lambda w: eng.tensor_tensor(w["bound"][:, :], w["value"][:, :], w["tau"][:, :], ALU.max))
    each(lambda w: eng.tensor_tensor(w["best"][:, :], w["best"][:, :], w["run8"][:, 7:8], ALU.max),
         lambda w: eng.scalar_tensor_tensor(scratch(w), cand(w), w["bound"][:, :], cand(w),
                                            ALU.is_gt, ALU.mult, accum_out=w["above"][:, :]))
    each(lambda w: eng.tensor_tensor(w["up"][:, :], w["best"][:, :], w["theta1"][:, :], ALU.is_ge),
         lambda w: eng.tensor_tensor(w["above"][:, :], w["above"][:, :], w["above0"][:, :], ALU.add))
    each(lambda w: eng.scalar_tensor_tensor(w["known"][:, :], w["value"][:, :], w["tau"][:, :], w["up"][:, :],
                                            ALU.is_ge, ALU.mult))


def set_flags(eng, works):
    for w in works:
        eng.tensor_tensor(w["left"][:, :], w["theta"][:, :], w["above_cut"][:, :], ALU.subtract)
        eng.tensor_scalar(w["up"][:, :], w["known"][:, :], 0.5, float(OPEN), ALU.is_lt, ALU.mult)
    eng.drain()
    for w in works:
        eng.scalar_tensor_tensor(w["many"][:, :], w["cut"][:, :], 8.0, w["left"][:, :], ALU.mult, ALU.is_lt)
    eng.drain()
    for w in works:
        eng.tensor_tensor(w["flags"][:, 0:1], w["up"][:, :], w["many"][:, :], ALU.add)


def next_round(eng, w, e, n_seg, seg):
    eng.scalar_tensor_tensor(w["work"][:, 0:e.shape[1]], e, w["cut"][:, :], e, ALU.is_lt, ALU.mult,
                             accum_out=w["below"][:, :])
    eng.drain()
    segment_tops(eng, w["work"], e.shape[1], w["cand"], seg)
    eng.tensor_tensor(w["above0"][:, :], w["total"][:, :], w["below"][:, :], ALU.subtract)
    eng.tensor_copy(w["was_known"][:, :], w["known"][:, :])
    eng.drain()
    eng.tensor_tensor(w["stays"][:, :], w["above0"][:, :], w["theta"][:, :], ALU.is_ge)
    eng.drain()
    eng.tensor_tensor(w["stays"][:, :], w["stays"][:, :], w["was_known"][:, :], ALU.max)
    solve(eng, [w], n_seg)
    eng.tensor_scalar(w["moves"][:, :], w["stays"][:, :], 0.5, None, ALU.is_lt)
    eng.tensor_tensor(w["known"][:, :], w["known"][:, :], w["stays"][:, :], ALU.max)
    eng.drain()
    eng.copy_predicated(w["cut"][:, :], w["moves"][:, :].bitcast(I32), w["bound"][:, :])
    eng.copy_predicated(w["above_cut"][:, :], w["moves"][:, :].bitcast(I32), w["above"][:, :])
    eng.drain()
    set_flags(eng, [w])


def tie_round(eng, w, src):
    eng.tensor_scalar(w["hit8"][:, :], w["index8"][:, :], w["cut"][:, :], None, ALU.mult)
    eng.drain()
    eng.tensor_scalar(w["hit8"][:, :], w["hit8"][:, :], w["left"][:, :], w["cut"][:, :], ALU.is_lt, ALU.mult)
    eng.drain()
    eng.match_replace(out=w["work"][:, :], in_to_replace=w["hit8"][:, :], in_values=src, imm_value=BIG_E)
    eng.scalar_tensor_tensor(w["left"][:, :], w["cut"][:, :], -8.0, w["left"][:, :], ALU.mult, ALU.add)
    eng.drain()


def more_ties(eng, w):
    eng.tensor_scalar(w["flags"][:, 0:1], w["left"][:, :], 0.0, None, ALU.is_gt)


def start_search(eng, works):
    for w in works:
        eng.tensor_scalar(w["theta"][:, :], w["total"][:, :], TOP_P, None, ALU.mult)
        eng.memset(w["above0"][:, :], 0.0)
    eng.drain()
    solve(eng, works, works[0]["n_seg"])
    for w in works:
        eng.tensor_copy(w["cut"][:, :], w["bound"][:, :])
        eng.tensor_copy(w["above_cut"][:, :], w["above"][:, :])
    eng.drain()
    set_flags(eng, works)


def while_over(eng, flag, least, times, body):
    side = 1
    while side ** 3 < times:
        side += 1
    with eng.If(eng.snap(flag) > least):
        with eng.Fori(0, side):
            with eng.If(eng.snap(flag) > least):
                with eng.Fori(0, side):
                    with eng.If(eng.snap(flag) > least):
                        with eng.Fori(0, side):
                            with eng.If(eng.snap(flag) > least):
                                body()


def top_p_select(eng, w, e_pad, width, valid, flag, regs):
    e = e_pad[:, 0:width]
    any_row_flag(eng, w, flag, regs)

    def another():
        next_round(eng, w, e, w["n_seg_next"], w["seg_next"])
        any_row_flag(eng, w, flag, regs)

    with eng.If(eng.snap(flag) > OPEN - 1):
        another()
        with eng.If(eng.snap(flag) > OPEN - 1):
            another()
            while_over(eng, flag, OPEN - 1, width // 8, another)
    eng.drain()
    tie_round(eng, w, e_pad)

    def another_eight():
        tie_round(eng, w, w["work"][:, :])
        more_ties(eng, w)
        any_row_flag(eng, w, flag, regs)

    with eng.If(eng.snap(flag) > 0):
        tie_round(eng, w, w["work"][:, :])
        another_eight()
        while_over(eng, flag, 0, width // 8, another_eight)
    eng.scalar_tensor_tensor(e_pad[:, 0:width], w["work"][:, 0:width], w["cut"][:, :],
                             e_pad[:, 0:width], ALU.is_gt, ALU.mult, accum_out=w["kept"][:, :])
    eng.drain()


def work_buffers(sb, width, seg):
    n_seg = width // seg
    shared = {"work": sb("work", [P, width + 8]), "flags_t": sb("flags_t", [P, 32]),
              "flag_max": sb("flag_max", [P, 1]), "flag_int": sb("flag_int", [P, 1], I32),
              "index8": sb("index8", [P, 8]), "zero8": sb("zero8", [P, 8])}
    works = []
    for k in range(2):
        w = dict(shared)
        w["flags"] = sb(f"flags{k}", [P, 32])
        w["cand"] = sb(f"cand{k}", [P, n_seg, 8])
        w["cand_work"] = w["work"][:, k * n_seg * 8:(k + 1) * n_seg * 8]
        w["mass"] = sb(f"mass{k}", [P, HALVINGS])
        w["mid"] = sb(f"mid{k}", [P, 1], I32)
        for n in ("top8", "run8", "hit8"):
            w[n] = sb(f"{n}_{k}", [P, 8])
        for n in ("total", "theta", "theta1", "above0", "above", "above_cut", "bound", "value", "tau", "best",
                  "cut", "up", "many", "known", "was_known", "stays", "moves", "below", "left", "kept",
                  "mass_hi"):
            w[n] = sb(f"{n}_{k}", [P, 1])
        works.append(w)
    return works


def layer0(nc, d, dims, H, ident):
    N, NP, T = dims
    PAIRS = T // 2
    CH = 512
    SEG = (128, 64)
    SEGS = [-(-NP // g) for g in SEG]
    NC = -(-NP // CH)
    DA = d["W2T"].shape[0]
    PROJ = 3 * NC
    STEP_CH = PROJ + T * NC

    def cols(c, end=NP):
        return slice(c * CH, min((c + 1) * CH, end))

    with ExitStack() as ctx:
        sb, ps, sem = scope(nc, ctx)
        qT = sb("qT", [DA, NP])
        kT = sb("kT", [DA, NP])
        XT = sb("XT", [P, NP])
        XR = [sb(f"XR{i}", [P, T, P + 1]) for i in range(3)]
        adj = [sb(f"adj{i}", [P, NP]) for i in range(2)]
        s = [sb(f"s{i}", [P, N]) for i in range(2)]
        e = [sb(f"e{i}", [P, NP + 8]) for i in range(2)]
        wT = [sb(f"wT{i}", [P, CH]) for i in range(2)]
        works = work_buffers(sb, NP, 64)
        for w in works:
            w["seg_next"], w["n_seg_next"] = 64, NP // 64
        h1 = works[0]["work"][0:DA, 0:NP]
        W1T = sb("W1T", [P, DA])
        W2T = sb("W2T", [DA, DA])
        W3T = sb("W3T", [P, DA])
        UT = sb("UT", [P, 2, 2, P])
        qs = [sb(f"qs{i}", [DA, P]) for i in range(2)]
        gate = sb("gate", [P, 1])
        cand_raw = [sb(f"cand_raw{i}", [P, NP // 64, 8]) for i in range(2)]
        rowmax = [sb(f"rowmax{i}", [P, 1]) for i in range(2)]
        negmax = [sb(f"negmax{i}", [P, 1]) for i in range(2)]
        rawR = [sb(f"rawR{i}", [P, P + 1]) for i in range(2)]
        inv_sum = [sb(f"inv_sum{i}", [P, 1]) for i in range(2)]
        inv_kept = [sb(f"inv_kept{i}", [P, 1]) for i in range(2)]
        rowR = [sb(f"rowR{i}", [P, P]) for i in range(2)]
        rowA = [sb(f"rowA{i}", [P, P]) for i in range(2)]
        xTR = [sb(f"xTR{i}", [P, P]) for i in range(2)]
        xTA = [sb(f"xTA{i}", [P, P]) for i in range(2)]
        zs = [sb(f"zs{i}", [P, P]) for i in range(2)]

        lg = [ps(f"lg{i}", [P, CH]) for i in range(2)]
        tr = [ps(f"tr{i}", [P, CH]) for i in range(2)]
        accR = ps("accR", [P, P + 1])
        accA = ps("accA", [P, P])
        xt = ps("xt", [P, 2, P])
        zp = ps("zp", [P, P])

        loaded = sem("l0_loaded")
        consts = sem("l0_consts")
        adj_loaded = [sem(f"l0_adj_loaded{i}") for i in range(2)]
        adj_free = sem("l0_adj_free")
        qs_ready = sem("l0_qs_ready")
        qs_free = sem("l0_qs_free")
        lg_ready = sem("l0_lg_ready")
        lg_free = sem("l0_lg_free")
        negmax_ready = sem("l0_negmax_ready")
        e_ready = sem("l0_e_ready")
        e_free = sem("l0_e_free")
        w_ready = sem("l0_w_ready")
        tr_ready = sem("l0_tr_ready")
        wT_ready = sem("l0_wT_ready")
        wT_free = sem("l0_wT_free")
        accR_ready = sem("l0_accR_ready")
        rawR_ready = sem("l0_rawR_ready")
        sum_ready = sem("l0_sum_ready")
        inv_ready = sem("l0_inv_ready")
        rowR_ready = sem("l0_rowR_ready")
        xtR_ready = sem("l0_xtR_ready")
        xTR_ready = sem("l0_xTR_ready")
        accA_ready = sem("l0_accA_ready")
        rowA_ready = sem("l0_rowA_ready")
        xtA_ready = sem("l0_xtA_ready")
        xTA_ready = sem("l0_xTA_ready")
        z_ready = sem("l0_z_ready")
        zs_ready = sem("l0_zs_ready")
        added = sem("l0_added")
        N_LOADS = 8

        def seq(step, p, slot):
            return (p + step * PAIRS) * 2 + slot

        def chunk(step, p, slot, c):
            return step * STEP_CH + PROJ + (p * 2 + slot) * NC + c

        with nc.Block() as block:

            @block.sync
            def _(eng):
                eng.dma_start(XR[0][:, :, 0:P], d["x_rows"]).then_inc(loaded, 16)
                eng.dma_start(H[:, :, :], d["x_rows"]).then_inc(loaded, 16)
                eng.dma_start(XT[:, :], d["x_t"]).then_inc(loaded, 16)
                eng.dma_start(W1T[:, :], d["W1T"]).then_inc(loaded, 16)
                eng.dma_start(W2T[:, :], d["W2T"]).then_inc(loaded, 16)
                eng.dma_start(W3T[:, :], d["W3T"]).then_inc(loaded, 16)
                eng.dma_start(UT[:, 0, :, :], d["U1T"]).then_inc(loaded, 16)
                eng.dma_start(UT[:, 1, :, :], d["U2T"]).then_inc(loaded, 16)
                for step in range(2):
                    with eng.Fori(0, PAIRS) as p:
                        for k in range(2):
                            eng.wait_ge(adj_free, seq(step, p, k) + 1)
                            eng.dma_start(adj[k][:, :], d["adjT"][bass.ds((p * 2 + k) * P, P), :]).then_inc(adj_loaded[k], 16)
                eng.wait_ge(added, 2 * T)

            @block.gpsimd
            def _(eng):
                eng.memset(ident[:, :], 0.0)
                for k in range(3):
                    eng.memset(XR[k][:, :, P:P + 1], 1.0)
                eng.drain()
                eng.affine_select(out=ident[:, :], in_=ident[:, :], compare_op=ALU.not_equal, fill=1.0,
                                  base=0, pattern=[[-1, P]], channel_multiplier=1)
                eng.drain()
                eng.sem_inc(consts, 1)
                eng.wait_ge(loaded, 16 * N_LOADS)
                for step in range(2):
                    eng.wait_ge(lg_free, 2 + step * STEP_CH + PROJ)

                    def give_q(p, k):
                        eng.wait_ge(qs_free, seq(step, p, k) + 1)
                        eng.tensor_copy(qs[k][:, :], qT[:, bass.ds((p * 2 + k) * P, P)])
                        eng.drain()
                        eng.sem_inc(qs_ready, 1)

                    def add_self(p, k):
                        src = XR[0] if step == 0 else XR[2]
                        eng.wait_ge(rawR_ready, seq(step, p, k) + 2)
                        eng.tensor_tensor(rawR[k][:, :], rawR[k][:, :], src[:, bass.ds(p * 2 + k, 1), :]
                                          .rearrange("p a n -> p (a n)"), ALU.add)
                        eng.drain()
                        eng.sem_inc(sum_ready, 1)

                    def give_rows(p, k):
                        eng.wait_ge(inv_ready, seq(step, p, k) + 1)
                        eng.tensor_tensor(rowR[k][:, :], rawR[k][:, 0:P], inv_sum[k][:, :].to_broadcast([P, P]),
                                          ALU.mult)
                        eng.drain()
                        eng.sem_inc(rowR_ready, 1)
                        if step == 0:
                            eng.tensor_copy(XR[2][:, bass.ds(p * 2 + k, 1), 0:P], rowR[k][:, :].unsqueeze(1))

                    def give_attended(p, k):
                        i = p * 2 + k
                        if step == 0:
                            eng.wait_ge(xTA_ready, seq(step, p, k) + 1)
                            eng.tensor_copy(XR[1][:, bass.ds(i, 1), 0:P], rowA[k][:, :].unsqueeze(1))
                            eng.tensor_copy(XT[:, bass.ds(i * P, P)], xTA[k][:, :])
                        eng.wait_ge(zs_ready, seq(step, p, k) + 2)
                        eng.tensor_tensor(H[:, bass.ds(i, 1), :], H[:, bass.ds(i, 1), :],
                                          zs[k][:, :].unsqueeze(1), ALU.add)
                        eng.drain()
                        eng.sem_inc(added, 1)

                    def pair(p, last):
                        add_self(p, 0)
                        add_self(p, 1)
                        if not last:
                            give_q(p + 1, 0)
                            give_q(p + 1, 1)
                        give_rows(p, 0)
                        give_rows(p, 1)
                        give_attended(p, 0)
                        give_attended(p, 1)

                    give_q(0, 0)
                    give_q(0, 1)
                    with eng.Fori(0, PAIRS - 1) as p:
                        pair(p, False)
                    pair(PAIRS - 1, True)

            @block.tensor
            def _(eng):
                eng.sem_inc(adj_free, 2)
                eng.sem_inc(qs_free, 2)
                eng.sem_inc(e_free, 2)
                eng.sem_inc(wT_free, 2)
                eng.wait_ge(loaded, 16 * N_LOADS)
                eng.wait_ge(consts, 1)
                for step in range(2):
                    xf = XR[0] if step == 0 else XR[2]
                    xa = XR[0] if step == 0 else XR[1]

                    def project(which, lhsT, rhs, c):
                        n = step * STEP_CH + which * NC + c
                        eng.wait_ge(lg_free, n + 1)
                        eng.matmul(lg[n % 2][0:DA, 0:rhs.shape[1]], lhsT, rhs, start=True, stop=True)\
                           .then_inc(lg_ready, 1)

                    def logits(p, k):
                        eng.wait_ge(qs_ready, seq(step, p, k) + 1)
                        for c in range(NC):
                            n = chunk(step, p, k, c)
                            b = chunk(step, 0, k, c) % 2
                            sl = cols(c, N)
                            eng.wait_ge(lg_free, n + 1)
                            eng.matmul(lg[b][:, 0:sl.stop - sl.start], qs[k][:, :], kT[:, sl],
                                       start=True, stop=True).then_inc(lg_ready, 1)
                        eng.drain()
                        eng.sem_inc(qs_free, 1)

                    def rows(p, k):
                        eng.wait_ge(adj_loaded[k], (p + step * PAIRS + 1) * 16)
                        eng.wait_ge(rawR_ready, seq(step, p, k) + 1)
                        for j in range(T):
                            mm = eng.matmul(accR[:, :], adj[k][:, j * P:(j + 1) * P], xf[:, j, :],
                                            start=(j == 0), stop=(j == T - 1))
                        mm.then_inc(accR_ready, 1)
                        eng.drain()
                        eng.sem_inc(adj_free, 1)

                    def rows_transposed(p, k):
                        eng.wait_ge(rowR_ready, seq(step, p, k) + 1)
                        eng.wait_ge(xTR_ready, seq(step, p, k) + 1)
                        eng.transpose(xt[:, 0, :], rowR[k][:, :], ident[:, :]).then_inc(xtR_ready, 1)

                    def attend(p, k):
                        t = seq(step, p, k)
                        eng.wait_ge(w_ready, t + 1)

                        def turn(c):
                            sl = cols(c)
                            for j in range(sl.start // P, sl.stop // P):
                                o = j * P - sl.start
                                mm = eng.transpose(tr[(k * NC + c) % 2][:, o:o + P],
                                                   e[k][:, j * P:(j + 1) * P], ident[:, :])
                            mm.then_inc(tr_ready, 1)

                        turn(0)
                        for c in range(NC):
                            if c + 1 < NC:
                                turn(c + 1)
                            if c + 2 == NC:
                                eng.drain()
                                eng.sem_inc(e_free, 1)
                            eng.wait_ge(wT_ready, t * NC + c + 1)
                            if c == 0:
                                eng.wait_ge(rowA_ready, t + 1)
                            sl = cols(c)
                            for j in range(sl.start // P, sl.stop // P):
                                o = j * P - sl.start
                                mm = eng.matmul(accA[:, :], wT[(k * NC + c) % 2][:, o:o + P], xa[:, j, 0:P],
                                                start=(j == 0), stop=(j == T - 1))
                            if c == NC - 1:
                                mm.then_inc(accA_ready, 1)
                            eng.drain()
                            eng.sem_inc(wT_free, 1)

                    def update(p, k):
                        t = seq(step, p, k)
                        eng.wait_ge(rowA_ready, t + 2)
                        eng.wait_ge(xTR_ready, seq(step, p, 1) + 2)
                        eng.transpose(xt[:, 1, :], rowA[k][:, :], ident[:, :]).then_inc(xtA_ready, 1)
                        eng.wait_ge(zs_ready, t + 1)
                        eng.matmul(zp[:, :], xTR[k][:, :], UT[:, 0, step, :], start=True, stop=False)
                        eng.wait_ge(xTA_ready, t + 1)
                        eng.matmul(zp[:, :], xTA[k][:, :], UT[:, 1, step, :], start=False, stop=True)\
                           .then_inc(z_ready, 1)

                    def pair(p, last):
                        rows(p, 0)
                        rows(p, 1)
                        if not last:
                            logits(p + 1, 0)
                            logits(p + 1, 1)
                        rows_transposed(p, 0)
                        rows_transposed(p, 1)
                        for k in range(2):
                            attend(p, k)
                            update(p, k)

                    eng.wait_ge(added, step * T)
                    for c in range(NC):
                        project(0, W1T[:, :], XT[:, cols(c)], c)
                    for c in range(NC):
                        eng.wait_ge(lg_free, 2 + step * STEP_CH + c + 1)
                        project(1, W2T[:, :], h1[:, cols(c)], c)
                    for c in range(NC):
                        project(2, W3T[:, :], XT[:, cols(c)], c)
                    eng.wait_ge(lg_free, 2 + step * STEP_CH + PROJ)
                    logits(0, 0)
                    logits(0, 1)
                    with eng.Fori(0, PAIRS - 1) as p:
                        pair(p, False)
                    pair(PAIRS - 1, True)

            @block.scalar
            def _(eng):
                eng.sem_inc(lg_free, 2)
                for copied in (rawR_ready, xTR_ready, zs_ready, rowA_ready):
                    eng.sem_inc(copied, 1)
                for step in range(2):

                    def project(which, dst, c):
                        n = step * STEP_CH + which * NC + c
                        eng.wait_ge(lg_ready, n + 1)
                        sl = cols(c)
                        eng.activation(dst[:, sl], lg[n % 2][0:DA, 0:sl.stop - sl.start], ACT.Copy)\
                           .then_inc(lg_free, 1)

                    def copy_logits(p, k):
                        for c in range(NC):
                            sl = cols(c, N)
                            eng.wait_ge(lg_ready, chunk(step, p, k, c) + 1)
                            eng.activation(s[k][:, sl], lg[chunk(step, 0, k, c) % 2][:, 0:sl.stop - sl.start],
                                           ACT.Copy).then_inc(lg_free, 1)

                    def exps(p, k):
                        t = seq(step, p, k)
                        eng.wait_ge(negmax_ready, t + 1)
                        eng.wait_ge(e_free, t + 1)
                        eng.activation(e[k][:, 0:N], s[k][:, :], ACT.Exp, bias=negmax[k][:, :],
                                       accum_out=works[k]["total"][:, :])
                        eng.activation(works[k]["cand"][:, 0:SEGS[step], :].rearrange("p a b -> p (a b)"),
                                       cand_raw[k][:, 0:SEGS[step], :].rearrange("p a b -> p (a b)"),
                                       ACT.Exp, bias=negmax[k][:, :])
                        eng.drain()
                        eng.sem_inc(e_ready, 1)

                    def copy_rows(p, k):
                        t = seq(step, p, k)
                        eng.wait_ge(accR_ready, t + 1)
                        eng.activation(rawR[k][:, :], accR[:, :], ACT.Copy).then_inc(rawR_ready, 1)

                    def copy_rows_transposed(p, k):
                        t = seq(step, p, k)
                        eng.wait_ge(xtR_ready, t + 1)
                        eng.activation(xTR[k][:, :], xt[:, 0, :], ACT.Copy).then_inc(xTR_ready, 1)

                    def copy_attended(p, k):
                        t = seq(step, p, k)
                        for c in range(NC):
                            sl = cols(c)
                            n = t * NC + c
                            eng.wait_ge(tr_ready, n + 1)
                            eng.wait_ge(wT_free, n + 1)
                            eng.activation(wT[(k * NC + c) % 2][:, 0:sl.stop - sl.start],
                                           tr[(k * NC + c) % 2][:, 0:sl.stop - sl.start],
                                           ACT.Copy).then_inc(wT_ready, 1)
                        eng.wait_ge(accA_ready, t + 1)
                        eng.activation(rowA[k][:, :], accA[:, :], ACT.Copy, scale=inv_kept[k][:, :])\
                           .then_inc(rowA_ready, 1)
                        eng.wait_ge(xtA_ready, t + 1)
                        eng.activation(xTA[k][:, :], xt[:, 1, :], ACT.Copy).then_inc(xTA_ready, 1)
                        eng.wait_ge(z_ready, t + 1)
                        eng.activation(zs[k][:, :], zp[:, :], ACT.Copy).then_inc(zs_ready, 1)

                    def pair(p, last):
                        exps(p, 0)
                        exps(p, 1)
                        copy_rows(p, 0)
                        copy_rows(p, 1)
                        if not last:
                            copy_logits(p + 1, 0)
                            copy_logits(p + 1, 1)
                        copy_rows_transposed(p, 0)
                        copy_rows_transposed(p, 1)
                        copy_attended(p, 0)
                        copy_attended(p, 1)

                    for c in range(NC):
                        project(0, h1, c)
                    for c in range(NC):
                        project(1, qT, c)
                    for c in range(NC):
                        project(2, kT, c)
                    copy_logits(0, 0)
                    copy_logits(0, 1)
                    with eng.Fori(0, PAIRS - 1) as p:
                        pair(p, False)
                    pair(PAIRS - 1, True)

            @block.vector
            def _(eng):
                flag = eng.alloc_register("open_flag")
                regs = [eng.alloc_register(f"group_flag{q}") for q in range(4)]
                for w in works:
                    eng.memset(w["flags"][:, :], 0.0)
                eng.memset(works[0]["zero8"][:, :], 0.0)
                for n in range(8):
                    eng.memset(works[0]["index8"][:, n:n + 1], float(n))
                for k in range(2):
                    eng.memset(e[k][:, N:NP + 8], 0.0)
                eng.drain()
                for step in range(2):
                    with eng.Fori(0, PAIRS) as p:
                        for k in range(2):
                            eng.wait_ge(lg_free, 2 + chunk(step, p, k, NC - 1) + 1)
                            eng.memset(gate[:, :], 0.0)
                            segment_tops(eng, s[k], N, cand_raw[k], SEG[step])
                            eng.drain()
                            eng.tensor_reduce(rowmax[k][:, :], cand_raw[k][:, 0:SEGS[step], 0], AX.X, ALU.max)
                            eng.drain()
                            eng.tensor_scalar(negmax[k][:, :], rowmax[k][:, :], -1.0, None, ALU.mult)\
                               .then_inc(negmax_ready, 1)
                        eng.wait_ge(e_ready, seq(step, p, 1) + 1)
                        for w in works:
                            w["n_seg"] = SEGS[step]
                        start_search(eng, works)
                        for k in range(2):
                            top_p_select(eng, works[k], e[k][:, :], NP, N, flag, regs)
                            eng.reciprocal(inv_kept[k][:, :], works[k]["kept"][:, :]).then_inc(w_ready, 1)
                            if k == 0:
                                for r in range(2):
                                    eng.wait_ge(sum_ready, seq(step, p, r) + 1)
                                    eng.reciprocal(inv_sum[r][:, :], rawR[r][:, P:P + 1]).then_inc(inv_ready, 1)


def layernorm_rows(eng, x, sq, stat, rstd, std_ready, var_ready, turn, T):
    def spread(v):
        return v[:, :].unsqueeze(2).to_broadcast([P, T, P])

    eng.tensor_reduce(stat[:, :], x[:, :, :], AX.X, ALU.add)
    eng.drain()
    eng.tensor_scalar(stat[:, :], stat[:, :], 1.0 / P, None, ALU.mult)
    eng.drain()
    eng.tensor_tensor(x[:, :, :], x[:, :, :], spread(stat), ALU.subtract)
    eng.drain()
    eng.tensor_tensor(sq[:, :, :], x[:, :, :], x[:, :, :], ALU.mult)
    eng.drain()
    eng.tensor_reduce(stat[:, :], sq[:, :, :], AX.X, ALU.add)
    eng.drain()
    eng.tensor_scalar(stat[:, :], stat[:, :], 1.0 / P, EPS, ALU.mult, ALU.add).then_inc(var_ready, 1)
    eng.wait_ge(std_ready, turn)
    eng.reciprocal(rstd[:, :], stat[:, :])
    eng.drain()
    eng.tensor_tensor(x[:, :, :], x[:, :, :], spread(rstd), ALU.mult)
    eng.drain()


def roots(eng, stat, std_ready, var_ready, turns):
    for n in range(turns):
        eng.wait_ge(var_ready, n + 1)
        eng.activation(stat[:, :], stat[:, :], ACT.Sqrt).then_inc(std_ready, 1)


def normalize(nc, d, dims, H):
    N, NP, T = dims
    with ExitStack() as ctx:
        sb, ps, sem = scope(nc, ctx)
        X = sb("ln_x", [P, T, P])
        sq = sb("ln_sq", [P, T, P])
        g = sb("ln_gain", [P, P])
        b = sb("ln_bias", [P, P])
        stat = sb("ln_stat", [P, T])
        rstd = sb("ln_rstd", [P, T])
        loaded, var_ready, std_ready = sem("ln_loaded"), sem("ln_var_ready"), sem("ln_std_ready")
        with nc.Block() as block:
            @block.sync
            def _(eng):
                eng.dma_start(X[:, :, :], d["x_rows"]).then_inc(loaded, 16)
                eng.dma_start(g[:, :], d["ln_g"].partition_broadcast(P)).then_inc(loaded, 16)
                eng.dma_start(b[:, :], d["ln_b"].partition_broadcast(P)).then_inc(loaded, 16)

            @block.scalar
            def _(eng):
                roots(eng, stat, std_ready, var_ready, 2)

            @block.vector
            def _(eng):
                def over_tiles(v):
                    return v[:, :].unsqueeze(1).to_broadcast([P, T, P])

                layernorm_rows(eng, H, sq, stat, rstd, std_ready, var_ready, 1, T)
                eng.wait_ge(loaded, 48)
                eng.tensor_tensor(H[:, :, :], H[:, :, :], over_tiles(g), ALU.mult)
                eng.drain()
                eng.tensor_tensor(H[:, :, :], H[:, :, :], over_tiles(b), ALU.add)
                eng.drain()
                eng.tensor_tensor(H[:, :, :], H[:, :, :], X[:, :, :], ALU.add)
                eng.drain()
                layernorm_rows(eng, H, sq, stat, rstd, std_ready, var_ready, 2, T)


def graph_sums(nc, d, dims, H, ident, diag, nsT, epm, negs):
    N, NP, T = dims
    HEADS = 3
    PAIRS = T // 2
    with ExitStack() as ctx:
        sb, ps, sem = scope(nc, ctx)
        hT = sb("hT", [P, NP])
        adj = [sb(f"g_adj{i}", [P, NP]) for i in range(2)]
        pos = [sb(f"pos{i}", [P, NP], BF16) for i in range(2)]
        neg = [sb(f"neg{i}", [P, NP], BF16) for i in range(2)]
        dblock = [sb(f"dblock{i}", [P, P]) for i in range(2)]
        dsum = [sb(f"dsum{i}", [P, 1]) for i in range(2)]
        WT = sb("gat_WT_s", [P, HEADS, P])
        av = sb("gat_a_s", [P, HEADS, 2])
        V = sb("V", [P, 3, HEADS])
        Y = sb("Y", [P, T, 3, 9], BF16)
        y0 = sb("y0", [P, T, 9])
        y1 = sb("y1", [P, T, 9])
        ones = sb("ones_bf", [P, 1], BF16)
        raw = sb("raw_e", [P, T, 18])
        esum = sb("esum", [P, T, 6])

        tp = [ps(f"g_tp{i}", [P, 512]) for i in range(2)]
        vp = ps("g_vp", [P, 3, 2])
        yp = ps("g_yp", [P, T, 9])
        sp = ps("g_sp", [P, P])
        ep = ps("g_ep", [P, 3, 6])
        np_ = ps("g_np", [P, 1])

        loaded = sem("g_loaded")
        adj_loaded = [sem(f"g_adj_loaded{i}") for i in range(2)]
        adj_free = sem("g_adj_free")
        mask_free = sem("g_mask_free")
        ones_ready = sem("g_ones_ready")
        hT_turned, hT_ready = sem("g_hT_turned"), sem("g_hT_ready")
        v_summed, v_ready = sem("g_v_summed"), sem("g_v_ready")
        y_summed, y_ready = sem("g_y_summed"), sem("g_y_ready")
        mask_ready = sem("g_mask_ready")
        sums_ready, sums_copied = sem("g_sums_ready"), sem("g_sums_copied")
        NC = -(-T // 4)

        with nc.Block() as block:
            @block.sync
            def _(eng):
                eng.dma_start(WT[:, :, :], d["gat_WT"]).then_inc(loaded, 16)
                eng.dma_start(av[:, :, :], d["gat_a"]).then_inc(loaded, 16)
                with eng.Fori(0, PAIRS) as p:
                    for k in range(2):
                        eng.wait_ge(adj_free, p * 2 + k + 1)
                        eng.dma_start(adj[k][:, :], d["adjT"][bass.ds((p * 2 + k) * P, P), :])\
                           .then_inc(adj_loaded[k], 16)

            @block.tensor
            def _(eng):
                eng.sem_inc(adj_free, 2)
                eng.sem_inc(mask_free, 2)
                for c in range(NC):
                    if c >= 2:
                        eng.wait_ge(hT_ready, c - 1)
                    for j in range(4 * c, min(4 * c + 4, T)):
                        mm = eng.transpose(tp[c % 2][:, (j % 4) * P:(j % 4 + 1) * P], H[:, j, :], ident[:, :])
                    mm.then_inc(hT_turned, 1)
                eng.wait_ge(loaded, 32)
                for h in range(HEADS):
                    mm = eng.matmul(vp[:, h, :], WT[:, h, :], av[:, h, :], start=True, stop=True)
                mm.then_inc(v_summed, 1)
                eng.wait_ge(hT_ready, NC)
                eng.wait_ge(v_ready, 1)
                for j in range(T):
                    mm = eng.matmul(yp[:, j, :], hT[:, j * P:(j + 1) * P], V[:, :, :].rearrange("p a b -> p (a b)"),
                                    start=True, stop=True)
                mm.then_inc(y_summed, 1)
                eng.wait_ge(y_ready, 1)
                eng.wait_ge(ones_ready, 1)

                def tile(p, k):
                    t = p * 2 + k
                    eng.wait_ge(mask_ready, t + 1)
                    eng.wait_ge(sums_copied, t + 1)
                    for j in range(T):
                        eng.matmul(sp[:, :], H[:, j, :], adj[k][:, j * P:(j + 1) * P],
                                   start=(j == 0), stop=(j == T - 1))
                    eng.drain()
                    eng.sem_inc(adj_free, 1)
                    for j in range(T):
                        sl = slice(j * P, (j + 1) * P)
                        eng.matmul(ep[:, :, :], pos[k][:, sl], Y[:, j, :, 0:6], start=(j == 0), stop=False)
                        eng.matmul(ep[:, :, :], neg[k][:, sl], Y[:, j, :, 3:9], start=False, stop=(j == T - 1))
                    for j in range(T):
                        eng.matmul(np_[:, :], neg[k][:, j * P:(j + 1) * P], ones[:, :],
                                   start=(j == 0), stop=(j == T - 1))
                    eng.drain()
                    eng.sem_inc(sums_ready, 1)
                    eng.sem_inc(mask_free, 1)

                with eng.Fori(0, PAIRS) as p:
                    tile(p, 0)
                    tile(p, 1)

            @block.scalar
            def _(eng):
                eng.sem_inc(sums_copied, 1)
                for c in range(NC):
                    n = min(512, NP - c * 512)
                    eng.wait_ge(hT_turned, c + 1)
                    eng.activation(hT[:, c * 512:c * 512 + n], tp[c % 2][:, 0:n], ACT.Copy).then_inc(hT_ready, 1)
                with eng.Fori(0, PAIRS) as p:
                    for k in range(2):
                        t = p * 2 + k
                        eng.wait_ge(sums_ready, t + 1)
                        eng.activation(nsT[:, bass.ds(t * P, P)], sp[:, :], ACT.Copy)
                        eng.activation(raw[:, bass.ds(t, 1), :], ep[:, :, :].rearrange("p a b -> p (a b)")
                                       .unsqueeze(1), ACT.Copy)
                        eng.activation(negs[:, bass.ds(t, 1)], np_[:, :], ACT.Copy)
                        eng.drain()
                        eng.sem_inc(sums_copied, 1)

            @block.vector
            def _(eng):
                eng.memset(ones[:, :], 1.0).then_inc(ones_ready, 1)
                eng.wait_ge(v_summed, 1)
                for part in range(3):
                    mm = eng.tensor_copy(V[:, part, :], vp[:, :, part % 2])
                mm.then_inc(v_ready, 1)
                eng.wait_ge(y_summed, 1)
                eng.tensor_copy(y0[:, :, :], yp[:, :, :])
                eng.drain()
                eng.tensor_copy(Y[:, :, 0, :], y0[:, :, :])
                eng.drain()
                eng.tensor_tensor(y1[:, :, :], y0[:, :, :], Y[:, :, 0, :], ALU.subtract)
                eng.drain()
                eng.tensor_copy(Y[:, :, 1, :], y1[:, :, :])
                eng.drain()
                eng.tensor_tensor(y0[:, :, :], y1[:, :, :], Y[:, :, 1, :], ALU.subtract)
                eng.drain()
                eng.tensor_copy(Y[:, :, 2, :], y0[:, :, :]).then_inc(y_ready, 1)
                with eng.Fori(0, PAIRS) as p:
                    for k in range(2):
                        t = p * 2 + k
                        eng.wait_ge(adj_loaded[k], (p + 1) * 16)
                        block_ = adj[k][:, bass.ds(t * P, P)]
                        eng.tensor_tensor(dblock[k][:, :], block_, ident[:, :], ALU.mult)
                        eng.drain()
                        eng.tensor_tensor(block_, block_, dblock[k][:, :], ALU.subtract)
                        eng.tensor_reduce(dsum[k][:, :], dblock[k][:, :], AX.X, ALU.add)
                        eng.drain()
                        eng.tensor_copy(diag[:, bass.ds(t, 1)], dsum[k][:, :])
                        eng.wait_ge(mask_free, t + 1)
                        eng.tensor_scalar(pos[k][:, :], adj[k][:, :], 0.0, None, ALU.is_gt)
                        eng.tensor_scalar(neg[k][:, :], adj[k][:, :], 0.0, None, ALU.is_lt)
                        eng.drain()
                        eng.sem_inc(mask_ready, 1)
                eng.wait_ge(sums_copied, T + 1)
                eng.tensor_tensor(esum[:, :, :], raw[:, :, 0:6], raw[:, :, 6:12], ALU.add)
                eng.drain()
                eng.tensor_tensor(esum[:, :, :], esum[:, :, :], raw[:, :, 12:18], ALU.add)
                eng.drain()
                eng.scalar_tensor_tensor(epm[:, :, :], esum[:, :, :], 0.2, esum[:, :, :], ALU.mult, ALU.max)


def attention(nc, d, dims, H, ident, epm, negs, gsT):
    N, NP, T = dims
    HEADS = 3
    PAIRS = T // 2
    NC = -(-NP // 512)
    with ExitStack() as ctx:
        sb, ps, sem = scope(nc, ctx)
        EB = sb("EB", [P, 2 * HEADS, NP])
        adj = [sb(f"a_adj{i}", [P, NP]) for i in range(2)]
        off = sb("off", [P, NP])
        alt = sb("alt", [P, NP])
        prob = [sb(f"prob{i}", [P, NP]) for i in range(2)]
        pT = [sb(f"pT{i}", [P, 512]) for i in range(2)]
        W = sb("gat_W_s", [P, HEADS, P])
        dblock = sb("a_dblock", [P, P])
        mx = sb("a_mx", [P, 1])
        gate = sb("a_gate", [P, 1])
        negmax = [sb(f"a_negmax{i}", [P, 1]) for i in range(2)]
        den = [sb(f"a_den{i}", [P, 1]) for i in range(2)]
        inv = [sb(f"a_inv{i}", [P, 1]) for i in range(2)]
        rows = sb("a_rows", [P, P])
        rowsT = sb("a_rowsT", [P, HEADS, P])
        w = {"flags": sb("a_flags", [P, 32]), "flags_t": sb("a_flags_t", [P, 32]),
             "flag_max": sb("a_flag_max", [P, 1]), "flag_int": sb("a_flag_int", [P, 1], I32)}

        tr = [ps(f"a_tr{i}", [P, 512]) for i in range(2)]
        acc = ps("a_acc", [P, P])
        rt = ps("a_rt", [P, P])
        sup = ps("a_sup", [P, P])

        loaded = sem("a_loaded")
        adj_loaded = [sem(f"a_adj_loaded{i}") for i in range(2)]
        adj_free = sem("a_adj_free")
        prob_free = sem("a_prob_free")
        eb_turned, eb_ready = sem("a_eb_turned"), sem("a_eb_ready")
        diag_out = sem("a_diag_out")
        logit_ready = sem("a_logit_ready")
        exp_ready = sem("a_exp_ready")
        inv_ready = sem("a_inv_ready")
        weight_ready = sem("a_weight_ready")
        tr_ready = sem("a_tr_ready")
        pT_ready = sem("a_pT_ready")
        pT_free = sem("a_pT_free")
        acc_ready = sem("a_acc_ready")
        rows_ready = sem("a_rows_ready")
        rt_ready = sem("a_rt_ready")
        rowsT_ready = sem("a_rowsT_ready")
        sup_ready = sem("a_sup_ready")
        sup_copied = sem("a_sup_copied")

        def seq(p, k, h):
            return (p * 2 + k) * HEADS + h

        def slot(k, h):
            return (k * HEADS + h) % 2

        with nc.Block() as block:
            @block.sync
            def _(eng):
                eng.dma_start(W[:, :, :], d["gat_W"]).then_inc(loaded, 16)
                with eng.Fori(0, PAIRS) as p:
                    for k in range(2):
                        eng.wait_ge(adj_free, p * 2 + k + 1)
                        eng.dma_start(adj[k][:, :], d["adj"][bass.ds((p * 2 + k) * P, P), :])\
                           .then_inc(adj_loaded[k], 16)

            @block.tensor
            def _(eng):
                eng.sem_inc(prob_free, 2)
                eng.sem_inc(pT_free, 2)
                eng.sem_inc(sup_ready, 1)
                for g in range(2 * HEADS * NC):
                    h, c = g // NC, g % NC
                    if g >= 2:
                        eng.wait_ge(eb_ready, g - 1)
                    for j in range(4 * c, min(4 * c + 4, T)):
                        mm = eng.transpose(tr[g % 2][:, (j % 4) * P:(j % 4 + 1) * P],
                                           epm[:, j, h:h + 1].to_broadcast([P, P]), ident[:, :])
                    mm.then_inc(eb_turned, 1)
                eng.wait_ge(eb_ready, 2 * HEADS * NC)
                eng.wait_ge(loaded, 16)

                def head(p, k, h):
                    q = seq(p, k, h)
                    b = slot(k, h)
                    eng.wait_ge(weight_ready, q + 1)

                    def turn(c):
                        for j in range(4 * c, min(4 * c + 4, T)):
                            mm = eng.transpose(tr[(b * NC + c) % 2][:, (j % 4) * P:(j % 4 + 1) * P],
                                               prob[b][:, j * P:(j + 1) * P], ident[:, :])
                        mm.then_inc(tr_ready, 1)

                    turn(0)
                    for c in range(NC):
                        if c + 1 < NC:
                            turn(c + 1)
                        if c + 2 == NC:
                            eng.drain()
                            eng.sem_inc(prob_free, 1)
                        eng.wait_ge(pT_ready, q * NC + c + 1)
                        if c == 0:
                            eng.wait_ge(rows_ready, q + 1)
                        for j in range(4 * c, min(4 * c + 4, T)):
                            mm = eng.matmul(acc[:, :], pT[(b * NC + c) % 2][:, (j % 4) * P:(j % 4 + 1) * P],
                                            H[:, j, :], start=(j == 0), stop=(j == T - 1))
                        if c == NC - 1:
                            mm.then_inc(acc_ready, 1)
                        eng.drain()
                        eng.sem_inc(pT_free, 1)
                    eng.wait_ge(rows_ready, q + 2)
                    eng.wait_ge(rowsT_ready, q + 1)
                    eng.transpose(rt[:, :], rows[:, :], ident[:, :]).then_inc(rt_ready, 1)

                with eng.Fori(0, PAIRS) as p:
                    for k in range(2):
                        for h in range(HEADS):
                            head(p, k, h)
                        eng.wait_ge(rowsT_ready, seq(p, k, HEADS - 1) + 2)
                        eng.wait_ge(sup_copied, p * 2 + k + 1)
                        for h in range(HEADS):
                            mm = eng.matmul(sup[:, :], W[:, h, :], rowsT[:, h, :],
                                            start=(h == 0), stop=(h == HEADS - 1))
                        mm.then_inc(sup_ready, 1)

            @block.scalar
            def _(eng):
                for copied in (rows_ready, rowsT_ready, sup_copied):
                    eng.sem_inc(copied, 1)
                for g in range(2 * HEADS * NC):
                    h, c = g // NC, g % NC
                    n = min(512, NP - c * 512)
                    eng.wait_ge(eb_turned, g + 1)
                    eng.activation(EB[:, h, c * 512:c * 512 + n], tr[g % 2][:, 0:n], ACT.Copy)\
                       .then_inc(eb_ready, 1)

                def exp(p, k, h):
                    b = slot(k, h)
                    eng.wait_ge(logit_ready, seq(p, k, h) + 1)
                    eng.activation(prob[b][:, :], prob[b][:, :], ACT.Exp, bias=negmax[b][:, :],
                                   accum_out=den[b][:, :])
                    eng.drain()
                    eng.sem_inc(exp_ready, 1)

                def copies(p, k, h):
                    b = slot(k, h)
                    q = seq(p, k, h)
                    for c in range(NC):
                        n = min(512, NP - c * 512)
                        eng.wait_ge(tr_ready, q * NC + c + 1)
                        eng.wait_ge(pT_free, q * NC + c + 1)
                        eng.activation(pT[(b * NC + c) % 2][:, 0:n], tr[(b * NC + c) % 2][:, 0:n], ACT.Copy)\
                           .then_inc(pT_ready, 1)
                    eng.wait_ge(acc_ready, q + 1)
                    eng.wait_ge(inv_ready, q + 1)
                    eng.activation(rows[:, :], acc[:, :], ACT.Copy, scale=inv[b][:, :]).then_inc(rows_ready, 1)
                    eng.wait_ge(rt_ready, q + 1)
                    if h == 0:
                        eng.wait_ge(sup_ready, p * 2 + k + 1)
                    eng.activation(rowsT[:, h, :], rt[:, :], ACT.Copy).then_inc(rowsT_ready, 1)

                def support(p, k):
                    t = p * 2 + k
                    eng.wait_ge(sup_ready, t + 2)
                    eng.activation(gsT[:, bass.ds(t * P, P)], sup[:, :], ACT.Copy, scale=1.0 / HEADS)
                    eng.drain()
                    eng.sem_inc(sup_copied, 1)

                order = [(k, h) for k in range(2) for h in range(HEADS)]

                def pair(p, last):
                    for n, (k, h) in enumerate(order):
                        if n + 1 < len(order):
                            exp(p, *order[n + 1])
                        elif not last:
                            exp(p + 1, 0, 0)
                        copies(p, k, h)
                        if h == HEADS - 1:
                            support(p, k)

                exp(0, 0, 0)
                with eng.Fori(0, PAIRS - 1) as p:
                    pair(p, False)
                pair(PAIRS - 1, True)

            @block.gpsimd
            def _(eng):
                eng.sem_inc(adj_free, 2)
                with eng.Fori(0, PAIRS) as p:
                    for k in range(2):
                        for h in range(HEADS):
                            b = slot(k, h)
                            eng.wait_ge(exp_ready, seq(p, k, h) + 1)
                            eng.tensor_tensor(prob[b][:, :], prob[b][:, :], adj[k][:, :], ALU.mult)
                            eng.drain()
                            eng.sem_inc(weight_ready, 1)
                        eng.sem_inc(adj_free, 1)

            @block.vector
            def _(eng):
                flag = eng.alloc_register("negative_flag")
                regs = [eng.alloc_register(f"neg_group{q}") for q in range(4)]
                eng.memset(w["flags"][:, :], 0.0)
                eng.drain()
                eng.tensor_reduce(w["flags"][:, 0:1], negs[:, :], AX.X, ALU.max)
                any_row_flag(eng, w, flag, regs)
                eng.wait_ge(eb_ready, 2 * HEADS * NC)
                with eng.Fori(0, PAIRS) as p:
                    for k in range(2):
                        t = p * 2 + k
                        eng.wait_ge(adj_loaded[k], (p + 1) * 16)
                        block_ = adj[k][:, bass.ds(t * P, P)]
                        eng.tensor_tensor(dblock[:, :], block_, ident[:, :], ALU.mult)
                        eng.drain()
                        eng.tensor_tensor(block_, block_, dblock[:, :], ALU.subtract)
                        eng.drain()
                        for h in range(HEADS):
                            q = seq(p, k, h)
                            b = slot(k, h)
                            if h == 0:
                                eng.tensor_scalar(off[:, :], adj[k][:, :], 0.0, NEG, ALU.is_le, ALU.mult)
                                eng.drain()
                            eng.wait_ge(prob_free, q + 1)
                            eng.memset(gate[:, :], 0.0)
                            eng.tensor_tensor_reduce(prob[b][:, :], off[:, :], EB[:, h, :], 1.0, -3.0e38,
                                                     ALU.add, ALU.max, mx[:, :])
                            eng.drain()
                            with eng.If(eng.snap(flag) > 0):
                                eng.tensor_scalar(alt[:, :], adj[k][:, :], 0.0, NEG, ALU.is_ge, ALU.mult)
                                eng.drain()
                                eng.tensor_tensor(alt[:, :], alt[:, :], EB[:, HEADS + h, :], ALU.add)
                                eng.drain()
                                eng.tensor_tensor(prob[b][:, :], prob[b][:, :], alt[:, :], ALU.max)
                                eng.drain()
                                eng.tensor_reduce(mx[:, :], prob[b][:, :], AX.X, ALU.max)
                                eng.drain()
                            eng.tensor_scalar(negmax[b][:, :], mx[:, :], -1.0, None, ALU.mult)\
                               .then_inc(logit_ready, 1)
                            eng.wait_ge(exp_ready, q + 1)
                            eng.reciprocal(inv[b][:, :], den[b][:, :]).then_inc(inv_ready, 1)


def gates_and_output(nc, d, dims, H, ident, diag, nsT, gsT):
    N, NP, T = dims
    PAIRS = T // 2
    with ExitStack() as ctx:
        sb, ps, sem = scope(nc, ctx)
        Wi = [sb(f"Wi{g}", [P, 3 * P]) for g in range(2)]
        Wh = [sb(f"Wh{g}", [P, 3 * P]) for g in range(2)]
        bi = [sb(f"bi{g}", [1, 3 * P]) for g in range(2)]
        bh = [sb(f"bh{g}", [1, 3 * P]) for g in range(2)]
        ones = sb("ones_row", [1, P])
        O = sb("O", [P, T, P])
        sq = sb("o_sq", [P, T, P])
        stat = sb("o_stat", [P, T])
        rstd = sb("o_rstd", [P, T])
        h = [sb(f"h_tile{k}", [P, P]) for k in range(2)]
        sT = [[sb(f"sT{g}{k}", [P, P]) for k in range(2)] for g in range(2)]
        hTt = [sb(f"hT_tile{k}", [P, P]) for k in range(2)]
        rz = [sb(f"rz{g}", [P, 2 * P]) for g in range(2)]
        cand = [sb(f"new{g}", [P, P]) for g in range(2)]
        nn = [sb(f"nn{g}", [P, P]) for g in range(2)]
        mix = [sb(f"mix{g}", [P, P]) for g in range(2)]
        tp = ps("o_tp", [P, P])
        gp = [ps(f"o_gp{g}", [P, 4 * P]) for g in range(2)]

        loaded, ones_ready = sem("o_loaded"), sem("o_ones_ready")
        tiles_ready, tiles_free = sem("o_tiles_ready"), sem("o_tiles_free")
        tp_ready, hT_ready = sem("o_tp_ready"), sem("o_hT_ready")
        gates_summed, gates_used = sem("o_gates_summed"), sem("o_gates_used")
        rz_ready, cand_ready, nn_ready, mixed = (sem("o_rz_ready"), sem("o_cand_ready"),
                                                 sem("o_nn_ready"), sem("o_mixed"))
        var_ready, std_ready = sem("o_var_ready"), sem("o_std_ready")
        normed, stored = sem("o_normed"), sem("o_stored")

        with nc.Block() as block:
            @block.sync
            def _(eng):
                for g, name in enumerate(("edge", "node")):
                    eng.dma_start(Wi[g][:, :], d[f"{name}_WihT"]).then_inc(loaded, 16)
                    eng.dma_start(Wh[g][:, :], d[f"{name}_WhhT"]).then_inc(loaded, 16)
                    eng.dma_start(bi[g][:, :], d[f"{name}_bih"]).then_inc(loaded, 16)
                    eng.dma_start(bh[g][:, :], d[f"{name}_bhh"]).then_inc(loaded, 16)
                eng.wait_ge(normed, 1)
                whole = N // P
                eng.dma_start(d["out"][0:whole * P, :].rearrange("(t p) d -> p t d", p=P), H[:, 0:whole, :])\
                   .then_inc(stored, 16)
                if N % P:
                    eng.dma_start(d["out"][whole * P:N, :], H[0:N % P, whole, :]).then_inc(stored, 16)
                eng.wait_ge(stored, 32 if N % P else 16)

            @block.gpsimd
            def _(eng):
                eng.sem_inc(tiles_free, 2)
                with eng.Fori(0, PAIRS) as p:
                    for k in range(2):
                        t = p * 2 + k
                        eng.wait_ge(tiles_free, t + 1)
                        eng.tensor_copy(h[k][:, :], H[:, bass.ds(t, 1), :].rearrange("p a b -> p (a b)"))
                        eng.tensor_copy(sT[0][k][:, :], nsT[:, bass.ds(t * P, P)])
                        eng.tensor_copy(sT[1][k][:, :], gsT[:, bass.ds(t * P, P)])
                        eng.drain()
                        eng.sem_inc(tiles_ready, 1)

            @block.tensor
            def _(eng):
                eng.wait_ge(loaded, 16 * 8)
                eng.wait_ge(ones_ready, 1)
                with eng.Fori(0, PAIRS) as p:
                    for k in range(2):
                        t = p * 2 + k
                        eng.wait_ge(tiles_ready, t + 1)
                        eng.transpose(tp[:, :], h[k][:, :], ident[:, :]).then_inc(tp_ready, 1)
                        eng.wait_ge(hT_ready, t + 1)
                        for g in range(2):
                            eng.wait_ge(gates_used, t * 2 + g + 1)
                            rzp, inp, hnp = gp[g][:, 0:2 * P], gp[g][:, 2 * P:3 * P], gp[g][:, 3 * P:4 * P]
                            RZ, NN = slice(0, 2 * P), slice(2 * P, 3 * P)
                            eng.matmul(rzp, sT[g][k][:, :], Wi[g][:, RZ], start=True, stop=False)
                            eng.matmul(rzp, hTt[k][:, :], Wh[g][:, RZ], start=False, stop=False)
                            eng.matmul(rzp, ones[:, :], bi[g][:, RZ], start=False, stop=False)
                            eng.matmul(rzp, ones[:, :], bh[g][:, RZ], start=False, stop=True)
                            eng.matmul(inp, sT[g][k][:, :], Wi[g][:, NN], start=True, stop=False)
                            eng.matmul(inp, ones[:, :], bi[g][:, NN], start=False, stop=True)
                            eng.matmul(hnp, hTt[k][:, :], Wh[g][:, NN], start=True, stop=False)
                            eng.matmul(hnp, ones[:, :], bh[g][:, NN], start=False, stop=True)\
                               .then_inc(gates_summed, 1)

            @block.scalar
            def _(eng):
                with eng.Fori(0, PAIRS) as p:
                    for k in range(2):
                        t = p * 2 + k
                        eng.wait_ge(tp_ready, t + 1)
                        eng.activation(hTt[k][:, :], tp[:, :], ACT.Copy).then_inc(hT_ready, 1)
                        for g in range(2):
                            eng.wait_ge(gates_summed, t * 2 + g + 1)
                            eng.wait_ge(mixed, t + 1)
                            eng.activation(rz[g][:, :], gp[g][:, 0:2 * P], ACT.Sigmoid).then_inc(rz_ready, 1)
                            eng.wait_ge(cand_ready, t * 2 + g + 1)
                            eng.activation(nn[g][:, :], cand[g][:, :], ACT.Tanh).then_inc(nn_ready, 1)
                roots(eng, stat, std_ready, var_ready, 1)

            @block.vector
            def _(eng):
                eng.memset(ones[:, :], 1.0).then_inc(ones_ready, 1)
                eng.sem_inc(gates_used, 1)
                eng.sem_inc(mixed, 1)
                with eng.Fori(0, PAIRS) as p:
                    for k in range(2):
                        t = p * 2 + k
                        for g in range(2):
                            eng.wait_ge(rz_ready, t * 2 + g + 1)
                            eng.tensor_tensor(cand[g][:, :], rz[g][:, 0:P], gp[g][:, 3 * P:4 * P], ALU.mult)
                            eng.drain()
                            eng.tensor_tensor(cand[g][:, :], cand[g][:, :], gp[g][:, 2 * P:3 * P], ALU.add)
                            eng.drain()
                            eng.sem_inc(cand_ready, 1)
                            eng.sem_inc(gates_used, 1)
                        for g in range(2):
                            eng.wait_ge(nn_ready, t * 2 + g + 1)
                            eng.tensor_tensor(mix[g][:, :], h[k][:, :], nn[g][:, :], ALU.subtract)
                            eng.drain()
                            eng.tensor_tensor(mix[g][:, :], mix[g][:, :], rz[g][:, P:2 * P], ALU.mult)
                            eng.drain()
                            eng.tensor_tensor(mix[g][:, :], mix[g][:, :], nn[g][:, :], ALU.add)
                            eng.drain()
                        eng.tensor_tensor(O[:, bass.ds(t, 1), :], mix[0][:, :].unsqueeze(1),
                                          mix[1][:, :].unsqueeze(1), ALU.add)
                        eng.drain()
                        eng.sem_inc(mixed, 1)
                        eng.sem_inc(tiles_free, 1)
                eng.tensor_tensor(O[:, :, :], O[:, :, :], diag[:, :].unsqueeze(2).to_broadcast([P, T, P]), ALU.mult)
                eng.drain()
                eng.tensor_tensor(H[:, :, :], H[:, :, :], O[:, :, :], ALU.add)
                eng.drain()
                layernorm_rows(eng, H, sq, stat, rstd, std_ready, var_ready, 1, T)
                eng.sem_inc(normed, 1)


def program(nc, d, dims):
    N, NP, T = dims
    with ExitStack() as ctx:
        sb, ps, sem = scope(nc, ctx)
        H = sb("H", [P, T, P])
        ident = sb("ident", [P, P])
        layer0(nc, d, dims, H, ident)
        normalize(nc, d, dims, H)
        diag = sb("diag", [P, T])
        nsT = sb("nsT", [P, NP])
        epm = sb("epm", [P, T, 6])
        negs = sb("negs", [P, T])
        graph_sums(nc, d, dims, H, ident, diag, nsT, epm, negs)
        gsT = sb("gsT", [P, NP])
        attention(nc, d, dims, H, ident, epm, negs, gsT)
        gates_and_output(nc, d, dims, H, ident, diag, nsT, gsT)


def kernel(x, adj, L0_gnn_W1, L0_gnn_W2, L0_gnn_W3, L0_gnn_U1, L0_gnn_U2, L0_gnn_ln_g, L0_gnn_ln_b,
           L1_gnn_gat_W, L1_gnn_gat_a, L1_gnn_edge_Wih, L1_gnn_edge_Whh, L1_gnn_edge_bih, L1_gnn_edge_bhh,
           L1_gnn_node_Wih, L1_gnn_node_Whh, L1_gnn_node_bih, L1_gnn_node_bhh):
    import numpy as np
    import concourse.bacc as bacc
    from concourse.bass_utils import run_bass_kernel_spmd

    c = np.ascontiguousarray
    N, D = x.shape
    T = -(-N // P)
    T += T % 2
    NP = T * P
    rows = np.concatenate([x] + [x[-1:]] * (NP - N), axis=0)
    adj_rows = np.zeros((NP, NP), adj.dtype)
    adj_rows[:N, :N] = adj
    arrays = {
        "x_rows": rows,
        "x_t": c(rows.T),
        "adj": adj_rows,
        "adjT": c(adj_rows.reshape(T, P, T, P).transpose(0, 3, 2, 1)).reshape(NP, NP),
        "W1T": c(L0_gnn_W1.T), "W2T": c(L0_gnn_W2.T), "W3T": c(L0_gnn_W3.T),
        "U1T": c(L0_gnn_U1.transpose(2, 0, 1)), "U2T": c(L0_gnn_U2.transpose(2, 0, 1)),
        "ln_g": c(L0_gnn_ln_g), "ln_b": c(L0_gnn_ln_b),
        "gat_W": c(L1_gnn_gat_W.transpose(1, 0, 2)), "gat_WT": c(L1_gnn_gat_W.transpose(2, 0, 1)),
        "gat_a": c(L1_gnn_gat_a.reshape(-1, 2, D).transpose(2, 0, 1)),
        "edge_WihT": c(L1_gnn_edge_Wih.T), "edge_WhhT": c(L1_gnn_edge_Whh.T),
        "edge_bih": L1_gnn_edge_bih.reshape(1, -1), "edge_bhh": L1_gnn_edge_bhh.reshape(1, -1),
        "node_WihT": c(L1_gnn_node_Wih.T), "node_WhhT": c(L1_gnn_node_Whh.T),
        "node_bih": L1_gnn_node_bih.reshape(1, -1), "node_bhh": L1_gnn_node_bhh.reshape(1, -1),
    }
    arrays = {f"in_{name}": c(a) for name, a in arrays.items()}
    nc = bacc.Bacc("TRN2", target_bir_lowering=False, num_devices=1)
    d = {name[3:]: nc.dram_tensor(name, a.shape, F32, kind="ExternalInput").ap() for name, a in arrays.items()}
    d["x_rows"] = d["x_rows"].rearrange("(t p) d -> p t d", p=P)
    d["out"] = nc.dram_tensor("out_rows", (N, D), F32, kind="ExternalOutput").ap()
    program(nc, d, (N, NP, T))
    r = run_bass_kernel_spmd(nc, [arrays], core_ids=[0])
    return r.results[0]["out_rows"]
```

```python
from contextlib import ExitStack

import concourse.bass as bass
from concourse import mybir

F32 = mybir.dt.float32
I32 = mybir.dt.int32
BF16 = mybir.dt.bfloat16
ALU = mybir.AluOpType
ACT = mybir.ActivationFunctionType
AX = mybir.AxisListType

P = 128
NEG = -9.0e15
EPS = 1e-5
TOP_P = 0.9
BIG_E = 4.0
HALVINGS = (6, 10)
LOW_BITS = 0x37C00000
EXTRACTIONS = (1, 1)
FIRST_STEP = 1 << 26
MANY, MORE, OPEN = 1, 16, 256


def scope(nc, ctx):
    def sb(name, shape, dt=F32):
        return ctx.enter_context(nc.sbuf_tensor(name, shape, dt))

    def ps(name, shape, dt=F32):
        return ctx.enter_context(nc.psum_tensor(name, shape, dt))

    def sem(name):
        return ctx.enter_context(nc.semaphore(name))

    return sb, ps, sem


def spread_flags(eng, works):
    eng.drain()
    for w in works:
        eng.transpose(w["flags_t"][:, :], w["flags"][:, :])
    eng.drain()
    for w in works:
        eng.tensor_reduce(w["flag_max"][:, :], w["flags_t"][:, :], AX.X, ALU.max)
    eng.drain()
    for w in works:
        eng.tensor_copy(w["flag_int"][:, :], w["flag_max"][:, :])
    eng.drain()


def load_flag(eng, w, flag, regs):
    for q in range(4):
        eng.reg_load(regs[q], w["flag_int"][32 * q:32 * q + 1, 0:1])
    eng.reg_add(flag, regs[0], regs[1])
    eng.reg_add(flag, flag, regs[2])
    eng.reg_add(flag, flag, regs[3])


def segment_tops(eng, src, width, cand, seg):
    for n in range(-(-width // seg)):
        eng.max(cand[:, n, :], src[:, n * seg:min((n + 1) * seg, width)])


def solve(eng, works, n_seg, halvings, extractions):
    def cand(w):
        return w["cand"][:, 0:n_seg, :].rearrange("p a b -> p (a b)")

    def scratch(w):
        return w["cand_work"][:, 0:n_seg * 8]

    def each(*ops):
        for w in works:
            for op in ops:
                op(w)
        eng.drain()

    each(lambda w: eng.tensor_tensor(w["theta1"][:, :], w["theta"][:, :], w["above0"][:, :], ALU.subtract),
         lambda w: eng.memset(w["mid"][:, :], LOW_BITS + FIRST_STEP),
         lambda w: eng.tensor_reduce(w["tau"][:, :], w["cand"][:, 0:n_seg, 7], AX.X, ALU.max))
    step = FIRST_STEP
    for n in range(halvings):
        each(lambda w: eng.scalar_tensor_tensor(scratch(w), cand(w), w["mid"][:, :].bitcast(F32), cand(w),
                                                ALU.is_ge, ALU.mult, accum_out=w["mass"][:, n:n + 1]))
        each(lambda w: eng.tensor_scalar(w["up"][:, :], w["mass"][:, n:n + 1], w["theta1"][:, :], float(step),
                                         ALU.is_ge, ALU.mult))
        back = -step // 2 if n + 1 < halvings else 0
        each(lambda w: eng.scalar_tensor_tensor(w["mid"][:, :], w["up"][:, :], float(back), w["mid"][:, :],
                                                ALU.add, ALU.add))
        step //= 2
    each(lambda w: eng.scalar_tensor_tensor(w["mass"][:, 0:halvings], w["mass"][:, 0:halvings], w["theta1"][:, :],
                                            w["mass"][:, 0:halvings], ALU.is_lt, ALU.mult))
    each(lambda w: eng.tensor_reduce(w["mass_hi"][:, :], w["mass"][:, 0:halvings], AX.X, ALU.max))
    for again in range(extractions):
        if again:
            each(lambda w: eng.tensor_tensor(w["up"][:, :], w["best"][:, :], w["theta1"][:, :], ALU.is_lt))
            each(lambda w: eng.copy_predicated(w["mid"][:, :], w["up"][:, :].bitcast(I32), w["value"][:, :].bitcast(I32)),
                 lambda w: eng.copy_predicated(w["mass_hi"][:, :], w["up"][:, :].bitcast(I32), w["best"][:, :]))
        each(lambda w: eng.scalar_tensor_tensor(scratch(w), cand(w), w["mid"][:, :].bitcast(F32), cand(w),
                                                ALU.is_lt, ALU.mult))
        each(lambda w: eng.max(w["top8"][:, :], scratch(w)))
        each(lambda w: eng.tensor_tensor_scan(w["run8"][:, :], w["top8"][:, :], w["zero8"][:, :],
                                              w["mass_hi"][:, :], ALU.add, ALU.add))
        each(lambda w: eng.scalar_tensor_tensor(w["hit8"][:, :], w["run8"][:, :], w["theta1"][:, :],
                                                w["top8"][:, :], ALU.is_ge, ALU.mult))
        each(lambda w: eng.tensor_reduce(w["value"][:, :], w["hit8"][:, :], AX.X, ALU.max))
        each(lambda w: eng.tensor_tensor(w["value"][:, :], w["value"][:, :], w["top8"][:, 7:8], ALU.max))
        each(lambda w: eng.scalar_tensor_tensor(scratch(w), cand(w), w["value"][:, :], cand(w),
                                                ALU.is_ge, ALU.mult, accum_out=w["best"][:, :]))
        each(lambda w: eng.tensor_tensor(w["best"][:, :], w["best"][:, :], w["run8"][:, 7:8], ALU.max))
    each(lambda w: eng.tensor_tensor(w["bound"][:, :], w["value"][:, :], w["tau"][:, :], ALU.max))
    each(lambda w: eng.scalar_tensor_tensor(scratch(w), cand(w), w["bound"][:, :], cand(w),
                                            ALU.is_gt, ALU.mult, accum_out=w["above"][:, :]))
    each(lambda w: eng.tensor_tensor(w["up"][:, :], w["best"][:, :], w["theta1"][:, :], ALU.is_ge),
         lambda w: eng.tensor_tensor(w["above"][:, :], w["above"][:, :], w["above0"][:, :], ALU.add))
    each(lambda w: eng.scalar_tensor_tensor(w["known"][:, :], w["value"][:, :], w["tau"][:, :], w["up"][:, :],
                                            ALU.is_ge, ALU.mult))


def set_flags(eng, works):
    for w in works:
        eng.tensor_tensor(w["left"][:, :], w["theta"][:, :], w["above_cut"][:, :], ALU.subtract)
        eng.tensor_scalar(w["up"][:, :], w["known"][:, :], 0.5, float(OPEN), ALU.is_lt, ALU.mult)
    eng.drain()
    for w in works:
        eng.scalar_tensor_tensor(w["many"][:, :], w["cut"][:, :], 8.0, w["left"][:, :], ALU.mult, ALU.is_lt)
        eng.scalar_tensor_tensor(w["more"][:, :], w["cut"][:, :], 24.0, w["left"][:, :], ALU.mult, ALU.is_lt)
    eng.drain()
    for w in works:
        eng.tensor_tensor(w["many"][:, :], w["up"][:, :], w["many"][:, :], ALU.add)
    eng.drain()
    for w in works:
        eng.scalar_tensor_tensor(w["flags"][:, 0:1], w["more"][:, :], float(MORE - MANY), w["many"][:, :],
                                 ALU.mult, ALU.add)


def next_round(eng, w, e, n_seg, seg):
    eng.scalar_tensor_tensor(w["work"][:, 0:e.shape[1]], e, w["cut"][:, :], e, ALU.is_lt, ALU.mult,
                             accum_out=w["below"][:, :])
    eng.drain()
    segment_tops(eng, w["work"], e.shape[1], w["round_cand"], seg)
    eng.tensor_tensor(w["above0"][:, :], w["whole"][:, :], w["below"][:, :], ALU.subtract)
    eng.tensor_copy(w["was_known"][:, :], w["known"][:, :])
    eng.drain()
    eng.tensor_tensor(w["stays"][:, :], w["above0"][:, :], w["theta"][:, :], ALU.is_ge)
    eng.drain()
    eng.tensor_tensor(w["stays"][:, :], w["stays"][:, :], w["was_known"][:, :], ALU.max)
    solve(eng, [dict(w, cand=w["round_cand"])], n_seg, HALVINGS[1], EXTRACTIONS[1])
    eng.tensor_scalar(w["moves"][:, :], w["stays"][:, :], 0.5, None, ALU.is_lt)
    eng.tensor_tensor(w["known"][:, :], w["known"][:, :], w["stays"][:, :], ALU.max)
    eng.drain()
    eng.copy_predicated(w["cut"][:, :], w["moves"][:, :].bitcast(I32), w["bound"][:, :])
    eng.copy_predicated(w["above_cut"][:, :], w["moves"][:, :].bitcast(I32), w["above"][:, :])
    eng.drain()
    set_flags(eng, [w])


def tie_round(eng, w, src):
    eng.tensor_scalar(w["hit8"][:, :], w["index8"][:, :], w["cut"][:, :], None, ALU.mult)
    eng.drain()
    eng.tensor_scalar(w["hit8"][:, :], w["hit8"][:, :], w["left"][:, :], w["cut"][:, :], ALU.is_lt, ALU.mult)
    eng.drain()
    eng.match_replace(out=w["work"][:, :], in_to_replace=w["hit8"][:, :], in_values=src, imm_value=BIG_E)
    eng.scalar_tensor_tensor(w["left"][:, :], w["cut"][:, :], -8.0, w["left"][:, :], ALU.mult, ALU.add)


def more_ties(eng, w):
    eng.tensor_scalar(w["flags"][:, 0:1], w["left"][:, :], 0.0, float(MORE), ALU.is_gt, ALU.mult)


def start_search(eng, works, n_seg, halvings, extractions):
    for w in works:
        eng.tensor_scalar(w["theta"][:, :], w["total"][:, :], TOP_P, None, ALU.mult)
        eng.tensor_copy(w["whole"][:, :], w["total"][:, :])
        eng.memset(w["above0"][:, :], 0.0)
    eng.drain()
    solve(eng, works, n_seg, halvings, extractions)
    for w in works:
        eng.tensor_copy(w["cut"][:, :], w["bound"][:, :])
        eng.tensor_copy(w["above_cut"][:, :], w["above"][:, :])
    eng.drain()
    set_flags(eng, works)


def while_over(eng, flag, least, times, body):
    side = 1
    while side ** 3 < times:
        side += 1
    with eng.If(eng.snap(flag) > least):
        with eng.Fori(0, side):
            with eng.If(eng.snap(flag) > least):
                with eng.Fori(0, side):
                    with eng.If(eng.snap(flag) > least):
                        with eng.Fori(0, side):
                            with eng.If(eng.snap(flag) > least):
                                body()


def top_p_select(eng, w, e_pad, width, flag, regs):
    e = e_pad[:, 0:width]
    tie_round(eng, w, e_pad)
    load_flag(eng, w, flag, regs)
    eng.drain()

    def another():
        next_round(eng, w, e, w["n_seg"], w["seg"])
        spread_flags(eng, [w])
        load_flag(eng, w, flag, regs)

    with eng.If(eng.snap(flag) > OPEN - 1):
        another()
        with eng.If(eng.snap(flag) > OPEN - 1):
            another()
            while_over(eng, flag, OPEN - 1, width // 8, another)
        eng.drain()
        tie_round(eng, w, e_pad)
        eng.drain()

    def another_eight():
        tie_round(eng, w, w["work"][:, :])
        eng.drain()
        more_ties(eng, w)
        spread_flags(eng, [w])
        load_flag(eng, w, flag, regs)

    with eng.If(eng.snap(flag) > 0):
        tie_round(eng, w, w["work"][:, :])
        eng.drain()
        tie_round(eng, w, w["work"][:, :])
        eng.drain()
        while_over(eng, flag, MORE - 1, width // 8, another_eight)
    eng.scalar_tensor_tensor(e_pad[:, 0:width], w["work"][:, 0:width], w["cut"][:, :],
                             e_pad[:, 0:width], ALU.is_gt, ALU.mult, accum_out=w["kept"][:, :])
    eng.drain()


def work_buffers(sb, width, seg):
    n_seg = width // seg
    shared = {"work": sb("work", [P, width + 8]), "index8": sb("index8", [P, 8]),
              "zero8": sb("zero8", [P, 8]),
              "round_cand": sb("round_cand", [P, n_seg, 8])}
    works = []
    for k in range(2):
        w = dict(shared)
        w["seg"], w["n_seg"] = seg, n_seg
        w["flags"], w["flags_t"] = sb(f"flags{k}", [P, 32]), sb(f"flags_t{k}", [P, 32])
        integers = sb(f"integers{k}", [P, 2], I32)
        w["flag_int"], w["mid"] = integers[:, 0:1], integers[:, 1:2]
        w["cand"] = sb(f"cand{k}", [P, n_seg, 8])
        w["cand_work"] = w["work"][:, k * n_seg * 8:(k + 1) * n_seg * 8]
        w["mass"] = sb(f"mass{k}", [P, max(HALVINGS)])
        for n in ("top8", "run8", "hit8"):
            w[n] = sb(f"{n}_{k}", [P, 8])
        names = ("total", "whole", "theta", "theta1", "above0", "above", "above_cut", "bound", "value", "tau", "best",
                 "cut", "up", "many", "more", "known", "was_known", "stays", "moves", "below", "left", "kept",
                 "mass_hi", "flag_max", "rowmax", "negmax", "inv_sum", "inv_kept")
        scalars = sb(f"scalars{k}", [P, len(names)])
        for i, n in enumerate(names):
            w[n] = scalars[:, i:i + 1]
        works.append(w)
    return works


def layer0(nc, d, dims, H, ident):
    N, NP, T = dims
    PAIRS = T // 2
    CH = 512
    SEG = (128, 32)
    SEGS = [-(-NP // g) for g in SEG]
    NC = -(-NP // CH)
    DA = d["W2T"].shape[0]
    PROJ = 3 * NC
    STEP_CH = PROJ + T * NC

    def cols(c, end=NP):
        return slice(c * CH, min((c + 1) * CH, end))

    with ExitStack() as ctx:
        sb, ps, sem = scope(nc, ctx)
        qT = sb("qT", [DA, NP])
        kT = sb("kT", [P, NP])
        XT = sb("XT", [P, NP])
        XR = [sb(f"XR{i}", [P, T, P + 1]) for i in range(3)]
        adj = [sb(f"adj{i}", [P, NP]) for i in range(2)]
        e = [[sb(f"e{b}{k}", [P, NP + 8]) for k in range(2)] for b in range(2)]
        wT = [sb(f"wT{i}", [P, CH]) for i in range(2)]
        works = work_buffers(sb, NP, SEG[1])
        h1 = works[0]["work"][0:DA, 0:NP]
        rowmax, negmax, inv_sum, inv_kept = ([w[n] for w in works] for n in ("rowmax", "negmax", "inv_sum", "inv_kept"))
        W1T = sb("W1T", [P, DA])
        W2T = sb("W2T", [DA, DA])
        W3T = sb("W3T", [P, DA])
        UT = sb("UT", [P, 2, 2, P])
        qs = [sb(f"qs{i}", [P, P]) for i in range(2)]
        gate = sb("gate", [P, 1])
        rawR = [sb(f"rawR{i}", [P, P + 1]) for i in range(2)]
        rowR = [sb(f"rowR{i}", [P, P]) for i in range(2)]
        rowA = [sb(f"rowA{i}", [P, P]) for i in range(2)]
        xTR = [sb(f"xTR{i}", [P, P]) for i in range(2)]
        xTA = [sb(f"xTA{i}", [P, P]) for i in range(2)]
        zs = [sb(f"zs{i}", [P, P]) for i in range(2)]

        lg = [ps(f"lg{i}", [P, CH]) for i in range(2)]
        tr = [ps(f"tr{i}", [P, CH]) for i in range(2)]
        accR = ps("accR", [P, P + 1])
        accA = ps("accA", [P, P])
        xt = ps("xt", [P, 2, P])
        zp = ps("zp", [P, P])

        loaded = sem("l0_loaded")
        consts, zeroed = sem("l0_consts"), sem("l0_zeroed")
        adj_loaded = [sem(f"l0_adj_loaded{i}") for i in range(2)]
        adj_free = sem("l0_adj_free")
        qs_ready = sem("l0_qs_ready")
        qs_free = sem("l0_qs_free")
        lg_ready = sem("l0_lg_ready")
        lg_free = sem("l0_lg_free")
        negmax_ready = sem("l0_negmax_ready")
        e_ready = sem("l0_e_ready")
        w_ready = sem("l0_w_ready")
        tr_ready = sem("l0_tr_ready")
        wT_ready = sem("l0_wT_ready")
        wT_free = sem("l0_wT_free")
        accR_ready = sem("l0_accR_ready")
        rawR_ready = sem("l0_rawR_ready")
        sum_ready = sem("l0_sum_ready")
        inv_ready = sem("l0_inv_ready")
        rowR_ready = sem("l0_rowR_ready")
        xtR_ready = sem("l0_xtR_ready")
        xTR_ready = sem("l0_xTR_ready")
        accA_ready = sem("l0_accA_ready")
        rowA_ready = sem("l0_rowA_ready")
        xtA_ready = sem("l0_xtA_ready")
        xTA_ready = sem("l0_xTA_ready")
        z_ready = sem("l0_z_ready")
        zs_ready = sem("l0_zs_ready")
        added = sem("l0_added")
        N_LOADS = 8

        def seq(step, p, slot):
            return (p + step * PAIRS) * 2 + slot

        def over_pairs(eng, pair):
            with eng.Fori(0, (PAIRS - 1) // 2) as pp:
                pair(pp * 2, 0, False)
                pair(pp * 2 + 1, 1, False)
            for p in range((PAIRS - 1) // 2 * 2, PAIRS):
                pair(p, p % 2, p + 1 == PAIRS)

        def chunk(step, p, slot, c):
            return step * STEP_CH + PROJ + (p * 2 + slot) * NC + c

        with nc.Block() as block:

            @block.sync
            def _(eng):
                eng.dma_start(XR[0][:, :, 0:P], d["x_rows"]).then_inc(loaded, 16)
                eng.dma_start(H[:, :, :], d["x_rows"]).then_inc(loaded, 16)
                eng.dma_start(XT[:, :], d["x_t"]).then_inc(loaded, 16)
                eng.dma_start(W1T[:, :], d["W1T"]).then_inc(loaded, 16)
                eng.dma_start(W2T[:, :], d["W2T"]).then_inc(loaded, 16)
                eng.dma_start(W3T[:, :], d["W3T"]).then_inc(loaded, 16)
                eng.dma_start(UT[:, 0, :, :], d["U1T"]).then_inc(loaded, 16)
                eng.dma_start(UT[:, 1, :, :], d["U2T"]).then_inc(loaded, 16)
                for step in range(2):
                    with eng.Fori(0, PAIRS) as p:
                        for k in range(2):
                            eng.wait_ge(adj_free, seq(step, p, k) + 1)
                            eng.dma_start(adj[k][:, :], d["adjT"][bass.ds((p * 2 + k) * P, P), :]).then_inc(adj_loaded[k], 16)
                eng.wait_ge(added, 2 * T)

            @block.gpsimd
            def _(eng):
                eng.memset(ident[:, :], 0.0)
                for k in range(3):
                    eng.memset(XR[k][:, :, P:P + 1], 1.0)
                eng.drain()
                eng.affine_select(out=ident[:, :], in_=ident[:, :], compare_op=ALU.not_equal, fill=1.0,
                                  base=0, pattern=[[-1, P]], channel_multiplier=1)
                eng.drain()
                eng.sem_inc(consts, 1)
                eng.wait_ge(loaded, 16 * N_LOADS)
                for step in range(2):
                    eng.wait_ge(lg_free, 2 + step * STEP_CH + PROJ)

                    def give_q(p, k):
                        eng.wait_ge(qs_free, seq(step, p, k) + 1)
                        eng.tensor_copy(qs[k][0:DA, :], qT[:, bass.ds((p * 2 + k) * P, P)])
                        eng.drain()
                        eng.sem_inc(qs_ready, 1)

                    def add_self(p, k):
                        src = XR[0] if step == 0 else XR[2]
                        eng.wait_ge(rawR_ready, seq(step, p, k) + 2)
                        eng.tensor_tensor(rawR[k][:, :], rawR[k][:, :], src[:, bass.ds(p * 2 + k, 1), :]
                                          .rearrange("p a n -> p (a n)"), ALU.add)
                        eng.drain()
                        eng.sem_inc(sum_ready, 1)

                    def give_rows(p, k):
                        eng.wait_ge(inv_ready, seq(step, p, k) + 1)
                        eng.tensor_tensor(rowR[k][:, :], rawR[k][:, 0:P], inv_sum[k][:, :].to_broadcast([P, P]),
                                          ALU.mult)
                        eng.drain()
                        eng.sem_inc(rowR_ready, 1)
                        if step == 0:
                            eng.tensor_copy(XR[2][:, bass.ds(p * 2 + k, 1), 0:P], rowR[k][:, :].unsqueeze(1))

                    def give_attended(p, k):
                        i = p * 2 + k
                        if step == 0:
                            eng.wait_ge(xTA_ready, seq(step, p, k) + 1)
                            eng.tensor_copy(XR[1][:, bass.ds(i, 1), 0:P], rowA[k][:, :].unsqueeze(1))
                            eng.tensor_copy(XT[:, bass.ds(i * P, P)], xTA[k][:, :])
                        eng.wait_ge(zs_ready, seq(step, p, k) + 2)
                        eng.tensor_tensor(H[:, bass.ds(i, 1), :], H[:, bass.ds(i, 1), :],
                                          zs[k][:, :].unsqueeze(1), ALU.add)
                        eng.drain()
                        eng.sem_inc(added, 1)

                    def pair(p, b, last):
                        add_self(p, 0)
                        add_self(p, 1)
                        if not last:
                            give_q(p + 1, 0)
                            give_q(p + 1, 1)
                        give_rows(p, 0)
                        give_rows(p, 1)
                        give_attended(p, 0)
                        give_attended(p, 1)

                    give_q(0, 0)
                    give_q(0, 1)
                    over_pairs(eng, pair)

            @block.tensor
            def _(eng):
                eng.sem_inc(adj_free, 2)
                eng.sem_inc(qs_free, 2)
                eng.sem_inc(wT_free, 2)
                eng.wait_ge(loaded, 16 * N_LOADS)
                eng.wait_ge(consts, 1)
                eng.wait_ge(zeroed, 1)
                for step in range(2):
                    xf = XR[0] if step == 0 else XR[2]
                    xa = XR[0] if step == 0 else XR[1]

                    def project(which, lhsT, rhs, c):
                        n = step * STEP_CH + which * NC + c
                        eng.wait_ge(lg_free, n + 1)
                        eng.matmul(lg[n % 2][0:DA, 0:rhs.shape[1]], lhsT, rhs, start=True, stop=True)\
                           .then_inc(lg_ready, 1)

                    def logits(p, k):
                        eng.wait_ge(qs_ready, seq(step, p, k) + 1)
                        for c in range(NC):
                            n = chunk(step, p, k, c)
                            bank = chunk(step, 0, k, c) % 2
                            sl = cols(c, N)
                            eng.wait_ge(lg_free, n + 1)
                            eng.matmul(lg[bank][:, 0:sl.stop - sl.start], qs[k][:, :], kT[:, sl],
                                       start=True, stop=True).then_inc(lg_ready, 1)
                        eng.drain()
                        eng.sem_inc(qs_free, 1)

                    def rows(p, k):
                        eng.wait_ge(adj_loaded[k], (p + step * PAIRS + 1) * 16)
                        eng.wait_ge(rawR_ready, seq(step, p, k) + 1)
                        for j in range(T):
                            mm = eng.matmul(accR[:, :], adj[k][:, j * P:(j + 1) * P], xf[:, j, :],
                                            start=(j == 0), stop=(j == T - 1))
                        mm.then_inc(accR_ready, 1)
                        eng.drain()
                        eng.sem_inc(adj_free, 1)

                    def rows_transposed(p, k):
                        eng.wait_ge(rowR_ready, seq(step, p, k) + 1)
                        eng.wait_ge(xTR_ready, seq(step, p, k) + 1)
                        eng.transpose(xt[:, 0, :], rowR[k][:, :], ident[:, :]).then_inc(xtR_ready, 1)

                    def attend(p, b, k):
                        t = seq(step, p, k)
                        eng.wait_ge(w_ready, t + 1)

                        def turn(c):
                            sl = cols(c)
                            for j in range(sl.start // P, sl.stop // P):
                                o = j * P - sl.start
                                mm = eng.transpose(tr[(k * NC + c) % 2][:, o:o + P],
                                                   e[b][k][:, j * P:(j + 1) * P], ident[:, :])
                            mm.then_inc(tr_ready, 1)

                        turn(0)
                        for c in range(NC):
                            if c + 1 < NC:
                                turn(c + 1)
                            eng.wait_ge(wT_ready, t * NC + c + 1)
                            if c == 0:
                                eng.wait_ge(rowA_ready, t + 1)
                            sl = cols(c)
                            for j in range(sl.start // P, sl.stop // P):
                                o = j * P - sl.start
                                mm = eng.matmul(accA[:, :], wT[(k * NC + c) % 2][:, o:o + P], xa[:, j, 0:P],
                                                start=(j == 0), stop=(j == T - 1))
                            if c == NC - 1:
                                mm.then_inc(accA_ready, 1)
                                eng.drain()
                                eng.sem_inc(wT_free, 1)
                            else:
                                mm.then_inc(wT_free, 1)

                    def update(p, k):
                        t = seq(step, p, k)
                        eng.wait_ge(rowA_ready, t + 2)
                        eng.wait_ge(xTR_ready, seq(step, p, 1) + 2)
                        eng.transpose(xt[:, 1, :], rowA[k][:, :], ident[:, :]).then_inc(xtA_ready, 1)
                        eng.wait_ge(zs_ready, t + 1)
                        eng.matmul(zp[:, :], xTR[k][:, :], UT[:, 0, step, :], start=True, stop=False)
                        eng.wait_ge(xTA_ready, t + 1)
                        eng.matmul(zp[:, :], xTA[k][:, :], UT[:, 1, step, :], start=False, stop=True)\
                           .then_inc(z_ready, 1)

                    def pair(p, b, last):
                        rows(p, 0)
                        rows(p, 1)
                        if not last:
                            logits(p + 1, 0)
                            logits(p + 1, 1)
                        rows_transposed(p, 0)
                        rows_transposed(p, 1)
                        for k in range(2):
                            attend(p, b, k)
                            update(p, k)

                    eng.wait_ge(added, step * T)
                    for c in range(NC):
                        project(0, W1T[:, :], XT[:, cols(c)], c)
                    for c in range(NC):
                        eng.wait_ge(lg_free, 2 + step * STEP_CH + c + 1)
                        project(1, W2T[:, :], h1[:, cols(c)], c)
                    for c in range(NC):
                        project(2, W3T[:, :], XT[:, cols(c)], c)
                    eng.wait_ge(lg_free, 2 + step * STEP_CH + PROJ)
                    logits(0, 0)
                    logits(0, 1)
                    over_pairs(eng, pair)

            @block.scalar
            def _(eng):
                eng.sem_inc(lg_free, 2)
                for copied in (rawR_ready, xTR_ready, zs_ready, rowA_ready):
                    eng.sem_inc(copied, 1)
                for step in range(2):

                    def project(which, dst, c):
                        n = step * STEP_CH + which * NC + c
                        eng.wait_ge(lg_ready, n + 1)
                        sl = cols(c)
                        eng.activation(dst[:, sl], lg[n % 2][0:DA, 0:sl.stop - sl.start], ACT.Copy)\
                           .then_inc(lg_free, 1)

                    def copy_logits(p, b, k):
                        for c in range(NC):
                            sl = cols(c, N)
                            eng.wait_ge(lg_ready, chunk(step, p, k, c) + 1)
                            eng.activation(e[b][k][:, sl], lg[chunk(step, 0, k, c) % 2][:, 0:sl.stop - sl.start],
                                           ACT.Copy).then_inc(lg_free, 1)

                    def exps(p, b, k):
                        eng.wait_ge(negmax_ready, seq(step, p, k) + 1)
                        eng.activation(e[b][k][:, 0:N], e[b][k][:, 0:N], ACT.Exp, bias=negmax[k][:, :],
                                       accum_out=works[k]["total"][:, :])
                        tops = works[k]["cand"][:, 0:SEGS[step], :].rearrange("p a b -> p (a b)")
                        eng.activation(tops, tops, ACT.Exp, bias=negmax[k][:, :])
                        eng.drain()
                        eng.sem_inc(e_ready, 1)

                    def copy_rows(p, k):
                        t = seq(step, p, k)
                        eng.wait_ge(accR_ready, t + 1)
                        eng.activation(rawR[k][:, :], accR[:, :], ACT.Copy).then_inc(rawR_ready, 1)

                    def copy_rows_transposed(p, k):
                        t = seq(step, p, k)
                        eng.wait_ge(xtR_ready, t + 1)
                        eng.activation(xTR[k][:, :], xt[:, 0, :], ACT.Copy).then_inc(xTR_ready, 1)

                    def copy_attended(p, k):
                        t = seq(step, p, k)
                        for c in range(NC):
                            sl = cols(c)
                            n = t * NC + c
                            eng.wait_ge(tr_ready, n + 1)
                            eng.wait_ge(wT_free, n + 1)
                            eng.activation(wT[(k * NC + c) % 2][:, 0:sl.stop - sl.start],
                                           tr[(k * NC + c) % 2][:, 0:sl.stop - sl.start],
                                           ACT.Copy).then_inc(wT_ready, 1)
                        eng.wait_ge(accA_ready, t + 1)
                        eng.activation(rowA[k][:, :], accA[:, :], ACT.Copy, scale=inv_kept[k][:, :])\
                           .then_inc(rowA_ready, 1)
                        eng.wait_ge(xtA_ready, t + 1)
                        eng.activation(xTA[k][:, :], xt[:, 1, :], ACT.Copy).then_inc(xTA_ready, 1)
                        eng.wait_ge(z_ready, t + 1)
                        eng.activation(zs[k][:, :], zp[:, :], ACT.Copy).then_inc(zs_ready, 1)

                    def pair(p, b, last):
                        copy_rows(p, 0)
                        copy_rows(p, 1)
                        if not last:
                            copy_logits(p + 1, 1 - b, 0)
                            copy_logits(p + 1, 1 - b, 1)
                        copy_rows_transposed(p, 0)
                        copy_rows_transposed(p, 1)
                        copy_attended(p, 0)
                        if not last:
                            exps(p + 1, 1 - b, 0)
                            exps(p + 1, 1 - b, 1)
                        copy_attended(p, 1)

                    for which, dst in enumerate((h1, qT, kT[0:DA, :])):
                        for c in range(NC):
                            project(which, dst, c)
                    for k in range(2):
                        copy_logits(0, 0, k)
                    for k in range(2):
                        exps(0, 0, k)
                    over_pairs(eng, pair)

            @block.vector
            def _(eng):
                flag = eng.alloc_register("open_flag")
                regs = [eng.alloc_register(f"group_flag{q}") for q in range(4)]
                eng.memset(kT[DA:P, :], 0.0)
                for k in range(2):
                    eng.memset(qs[k][DA:P, :], 0.0)
                for w in works:
                    eng.memset(w["flags"][:, :], 0.0)
                eng.memset(works[0]["zero8"][:, :], 0.0)
                for n in range(8):
                    eng.memset(works[0]["index8"][:, n:n + 1], float(n))
                for tile in e[0] + e[1]:
                    eng.memset(tile[:, N:NP + 8], 0.0)
                eng.drain()
                eng.sem_inc(zeroed, 1)
                for step in range(2):

                    def tops(p, b, k):
                        eng.wait_ge(lg_free, 2 + chunk(step, p, k, NC - 1) + 1)
                        eng.memset(gate[:, :], 0.0)
                        segment_tops(eng, e[b][k][:, 0:N], N, works[k]["cand"], SEG[step])
                        eng.drain()
                        eng.tensor_reduce(rowmax[k][:, :], works[k]["cand"][:, 0:SEGS[step], 0], AX.X, ALU.max)
                        eng.drain()
                        eng.tensor_scalar(negmax[k][:, :], rowmax[k][:, :], -1.0, None, ALU.mult)\
                           .then_inc(negmax_ready, 1)

                    def select(p, b, k):
                        top_p_select(eng, works[k], e[b][k][:, :], NP, flag, regs)
                        eng.reciprocal(inv_kept[k][:, :], works[k]["kept"][:, :]).then_inc(w_ready, 1)

                    def pair(p, b, last):
                        eng.wait_ge(e_ready, seq(step, p, 1) + 1)
                        start_search(eng, works, SEGS[step], HALVINGS[step], EXTRACTIONS[step])
                        spread_flags(eng, works)
                        select(p, b, 0)
                        for r in range(2):
                            eng.wait_ge(sum_ready, seq(step, p, r) + 1)
                            eng.reciprocal(inv_sum[r][:, :], rawR[r][:, P:P + 1]).then_inc(inv_ready, 1)
                        if not last:
                            tops(p + 1, 1 - b, 0)
                            tops(p + 1, 1 - b, 1)
                        select(p, b, 1)

                    tops(0, 0, 0)
                    tops(0, 0, 1)
                    over_pairs(eng, pair)


def layernorm_rows(eng, x, sq, stat, rstd, std_ready, var_ready, turn, T):
    def spread(v):
        return v[:, :].unsqueeze(2).to_broadcast([P, T, P])

    eng.tensor_reduce(stat[:, :], x[:, :, :], AX.X, ALU.add)
    eng.drain()
    eng.tensor_scalar(stat[:, :], stat[:, :], 1.0 / P, None, ALU.mult)
    eng.drain()
    eng.tensor_tensor(x[:, :, :], x[:, :, :], spread(stat), ALU.subtract)
    eng.drain()
    eng.tensor_tensor(sq[:, :, :], x[:, :, :], x[:, :, :], ALU.mult)
    eng.drain()
    eng.tensor_reduce(stat[:, :], sq[:, :, :], AX.X, ALU.add)
    eng.drain()
    eng.tensor_scalar(stat[:, :], stat[:, :], 1.0 / P, EPS, ALU.mult, ALU.add).then_inc(var_ready, 1)
    eng.wait_ge(std_ready, turn)
    eng.reciprocal(rstd[:, :], stat[:, :])
    eng.drain()
    eng.tensor_tensor(x[:, :, :], x[:, :, :], spread(rstd), ALU.mult)
    eng.drain()


def roots(eng, stat, std_ready, var_ready, turns):
    for n in range(turns):
        eng.wait_ge(var_ready, n + 1)
        eng.activation(stat[:, :], stat[:, :], ACT.Sqrt).then_inc(std_ready, 1)


def normalize(nc, d, dims, H):
    N, NP, T = dims
    with ExitStack() as ctx:
        sb, ps, sem = scope(nc, ctx)
        X = sb("ln_x", [P, T, P])
        sq = sb("ln_sq", [P, T, P])
        g = sb("ln_gain", [P, P])
        b = sb("ln_bias", [P, P])
        stat = sb("ln_stat", [P, T])
        rstd = sb("ln_rstd", [P, T])
        loaded, var_ready, std_ready = sem("ln_loaded"), sem("ln_var_ready"), sem("ln_std_ready")
        with nc.Block() as block:
            @block.sync
            def _(eng):
                eng.dma_start(X[:, :, :], d["x_rows"]).then_inc(loaded, 16)
                eng.dma_start(g[:, :], d["ln_g"].partition_broadcast(P)).then_inc(loaded, 16)
                eng.dma_start(b[:, :], d["ln_b"].partition_broadcast(P)).then_inc(loaded, 16)

            @block.scalar
            def _(eng):
                roots(eng, stat, std_ready, var_ready, 2)

            @block.vector
            def _(eng):
                def over_tiles(v):
                    return v[:, :].unsqueeze(1).to_broadcast([P, T, P])

                layernorm_rows(eng, H, sq, stat, rstd, std_ready, var_ready, 1, T)
                eng.wait_ge(loaded, 48)
                eng.tensor_tensor(H[:, :, :], H[:, :, :], over_tiles(g), ALU.mult)
                eng.drain()
                eng.tensor_tensor(H[:, :, :], H[:, :, :], over_tiles(b), ALU.add)
                eng.drain()
                eng.tensor_tensor(H[:, :, :], H[:, :, :], X[:, :, :], ALU.add)
                eng.drain()
                layernorm_rows(eng, H, sq, stat, rstd, std_ready, var_ready, 2, T)


def graph_sums(nc, d, dims, H, ident, diag, epm, negs):
    N, NP, T = dims
    HEADS = 3
    BUFS = 4
    with ExitStack() as ctx:
        sb, ps, sem = scope(nc, ctx)
        hT = sb("hT", [P, NP])
        nsT = sb("nsT", [P, NP])
        stored = sem("g_stored")
        adj = [sb(f"g_adj{i}", [P, NP]) for i in range(BUFS)]
        pos = [sb(f"pos{i}", [P, NP], BF16) for i in range(2)]
        neg = [sb(f"neg{i}", [P, NP], BF16) for i in range(2)]
        dblock = [sb(f"dblock{i}", [P, P]) for i in range(2)]
        dsum = [sb(f"dsum{i}", [P, 1]) for i in range(2)]
        WT = sb("gat_WT_s", [P, HEADS, P])
        av = sb("gat_a_s", [P, HEADS, 2])
        V = sb("V", [P, 3, HEADS])
        Y = sb("Y", [P, T, 3, 9], BF16)
        y0 = sb("y0", [P, T, 9])
        y1 = sb("y1", [P, T, 9])
        ones = sb("ones_bf", [P, 1], BF16)
        raw = sb("raw_e", [P, T, 18])
        esum = sb("esum", [P, T, 6])

        tp = [ps(f"g_tp{i}", [P, 512]) for i in range(2)]
        vp = ps("g_vp", [P, 3, 2])
        yp = ps("g_yp", [P, T, 9])
        sp = [tp[k][:, 0:P] for k in range(2)]
        ep = [tp[k][:, P:P + 18] for k in range(2)]
        np_ = [tp[k][:, P + 18:P + 19] for k in range(2)]

        loaded = sem("g_loaded")
        adj_loaded = [sem(f"g_adj_loaded{i}") for i in range(BUFS)]
        adj_free = sem("g_adj_free")
        mask_free = sem("g_mask_free")
        ones_ready = sem("g_ones_ready")
        hT_turned, hT_ready = sem("g_hT_turned"), sem("g_hT_ready")
        v_summed, v_ready = sem("g_v_summed"), sem("g_v_ready")
        y_summed, y_ready = sem("g_y_summed"), sem("g_y_ready")
        mask_ready = sem("g_mask_ready")
        sums_ready = sem("g_sums_ready")
        sums_copied = sem("g_sums_copied")
        NC = -(-T // 4)

        def over_tiles(eng, tile):
            with eng.Fori(0, T // BUFS) as r:
                for q in range(BUFS):
                    tile(r, q)
            for q in range(T % BUFS):
                tile(T // BUFS, q)

        with nc.Block() as block:
            @block.sync
            def _(eng):
                eng.dma_start(WT[:, :, :], d["gat_WT"]).then_inc(loaded, 16)
                eng.dma_start(av[:, :, :], d["gat_a"]).then_inc(loaded, 16)

                def load(r, q):
                    t = r * BUFS + q
                    eng.wait_ge(adj_free, t + 1)
                    eng.dma_start(adj[q][:, :], d["adjT"][bass.ds(t * P, P), :]).then_inc(adj_loaded[q], 16)

                over_tiles(eng, load)
                eng.wait_ge(sums_copied, T + 2)
                eng.dma_start(d["nsT"], nsT[:, :]).then_inc(stored, 16)
                eng.wait_ge(stored, 16)

            @block.tensor
            def _(eng):
                eng.sem_inc(adj_free, BUFS)
                eng.sem_inc(mask_free, 2)
                for c in range(NC):
                    if c >= 2:
                        eng.wait_ge(hT_ready, c - 1)
                    for j in range(4 * c, min(4 * c + 4, T)):
                        mm = eng.transpose(tp[c % 2][:, (j % 4) * P:(j % 4 + 1) * P], H[:, j, :], ident[:, :])
                    mm.then_inc(hT_turned, 1)
                eng.wait_ge(loaded, 32)
                for h in range(HEADS):
                    mm = eng.matmul(vp[:, h, :], WT[:, h, :], av[:, h, :], start=True, stop=True)
                mm.then_inc(v_summed, 1)
                eng.wait_ge(hT_ready, NC)
                eng.wait_ge(v_ready, 1)
                for j in range(T):
                    mm = eng.matmul(yp[:, j, :], hT[:, j * P:(j + 1) * P], V[:, :, :].rearrange("p a b -> p (a b)"),
                                    start=True, stop=True)
                mm.then_inc(y_summed, 1)
                eng.wait_ge(y_ready, 1)
                eng.wait_ge(ones_ready, 1)

                def tile(r, q):
                    t, k = r * BUFS + q, q % 2
                    eng.wait_ge(mask_ready, t + 1)
                    eng.wait_ge(sums_copied, t + 1)
                    for j in range(T):
                        mm = eng.matmul(sp[k], H[:, j, :], adj[q][:, j * P:(j + 1) * P],
                                        start=(j == 0), stop=(j == T - 1))
                    mm.then_inc(adj_free, 1)
                    for j in range(T):
                        sl = slice(j * P, (j + 1) * P)
                        eng.matmul(ep[k], pos[k][:, sl], Y[:, j, :, 0:6], start=(j == 0), stop=False)
                        eng.matmul(ep[k], neg[k][:, sl], Y[:, j, :, 3:9], start=False, stop=(j == T - 1))
                    for j in range(T):
                        eng.matmul(np_[k], neg[k][:, j * P:(j + 1) * P], ones[:, :],
                                   start=(j == 0), stop=(j == T - 1))
                    eng.drain()
                    eng.sem_inc(sums_ready, 1)
                    eng.sem_inc(mask_free, 1)

                over_tiles(eng, tile)

            @block.scalar
            def _(eng):
                eng.sem_inc(sums_copied, 2)
                for c in range(NC):
                    n = min(512, NP - c * 512)
                    eng.wait_ge(hT_turned, c + 1)
                    eng.activation(hT[:, c * 512:c * 512 + n], tp[c % 2][:, 0:n], ACT.Copy).then_inc(hT_ready, 1)

                def copy_sums(r, q):
                    t, k = r * BUFS + q, q % 2
                    eng.wait_ge(sums_ready, t + 1)
                    eng.activation(nsT[:, bass.ds(t * P, P)], sp[k], ACT.Copy)
                    eng.activation(raw[:, bass.ds(t, 1), :], ep[k].unsqueeze(1), ACT.Copy)
                    eng.activation(negs[:, bass.ds(t, 1)], np_[k], ACT.Copy)
                    eng.drain()
                    eng.sem_inc(sums_copied, 1)

                over_tiles(eng, copy_sums)

            @block.vector
            def _(eng):
                eng.memset(ones[:, :], 1.0).then_inc(ones_ready, 1)
                eng.wait_ge(v_summed, 1)
                for part in range(3):
                    mm = eng.tensor_copy(V[:, part, :], vp[:, :, part % 2])
                mm.then_inc(v_ready, 1)
                eng.wait_ge(y_summed, 1)
                eng.tensor_copy(y0[:, :, :], yp[:, :, :])
                eng.drain()
                eng.tensor_copy(Y[:, :, 0, :], y0[:, :, :])
                eng.drain()
                eng.tensor_tensor(y1[:, :, :], y0[:, :, :], Y[:, :, 0, :], ALU.subtract)
                eng.drain()
                eng.tensor_copy(Y[:, :, 1, :], y1[:, :, :])
                eng.drain()
                eng.tensor_tensor(y0[:, :, :], y1[:, :, :], Y[:, :, 1, :], ALU.subtract)
                eng.drain()
                eng.tensor_copy(Y[:, :, 2, :], y0[:, :, :]).then_inc(y_ready, 1)

                def masks(r, q):
                    t, k = r * BUFS + q, q % 2
                    eng.wait_ge(adj_loaded[q], (r + 1) * 16)
                    block_ = adj[q][:, bass.ds(t * P, P)]
                    eng.tensor_tensor(dblock[k][:, :], block_, ident[:, :], ALU.mult)
                    eng.drain()
                    eng.tensor_tensor(block_, block_, dblock[k][:, :], ALU.subtract)
                    eng.tensor_reduce(dsum[k][:, :], dblock[k][:, :], AX.X, ALU.add)
                    eng.drain()
                    eng.tensor_copy(diag[:, bass.ds(t, 1)], dsum[k][:, :])
                    eng.wait_ge(mask_free, t + 1)
                    eng.tensor_scalar(pos[k][:, :], adj[q][:, :], 0.0, None, ALU.is_gt)
                    eng.tensor_scalar(neg[k][:, :], adj[q][:, :], 0.0, None, ALU.is_lt)
                    eng.drain()
                    eng.sem_inc(mask_ready, 1)

                over_tiles(eng, masks)
                eng.wait_ge(sums_copied, T + 2)
                eng.tensor_tensor(esum[:, :, :], raw[:, :, 0:6], raw[:, :, 6:12], ALU.add)
                eng.drain()
                eng.tensor_tensor(esum[:, :, :], esum[:, :, :], raw[:, :, 12:18], ALU.add)
                eng.drain()
                eng.scalar_tensor_tensor(epm[:, :, :], esum[:, :, :], 0.2, esum[:, :, :], ALU.mult, ALU.max)


def attention(nc, d, dims, H, ident, epm, negs, gsT):
    N, NP, T = dims
    HEADS = 3
    PAIRS = T // 2
    NC = -(-NP // 512)
    HALF = NP // 2
    RING = 3
    with ExitStack() as ctx:
        sb, ps, sem = scope(nc, ctx)
        EB = sb("EB", [P, 2 * HEADS, NP])
        adj = [sb(f"a_adj{i}", [P, NP]) for i in range(2)]
        off = sb("off", [P, NP])
        negmask = sb("negmask", [P, NP], mybir.dt.uint8)
        prob = [sb(f"prob{i}", [P, NP]) for i in range(HEADS)]
        pT = [sb(f"pT{i}", [P, 512]) for i in range(RING)]
        W = sb("gat_W_s", [P, HEADS, P])
        dblock = sb("a_dblock", [P, P])
        mx = [sb(f"a_mx{i}", [P, 1]) for i in range(HEADS)]
        gate = sb("a_gate", [P, 1])
        negmax = [sb(f"a_negmax{i}", [P, 1]) for i in range(HEADS)]
        den = [sb(f"a_den{i}", [P, 2]) for i in range(HEADS)]
        inv = [sb(f"a_inv{i}", [P, 1]) for i in range(HEADS)]
        rows = sb("a_rows", [P, P])
        rowsT = sb("a_rowsT", [P, HEADS, P])
        w = {"flags": sb("a_flags", [P, 32]), "flags_t": sb("a_flags_t", [P, 32]),
             "flag_max": sb("a_flag_max", [P, 1]), "flag_int": sb("a_flag_int", [P, 1], I32)}

        tr = [ps(f"a_tr{i}", [P, 512]) for i in range(RING)]
        acc = ps("a_acc", [P, P])
        rt = ps("a_rt", [P, P])
        sup = ps("a_sup", [P, P])

        loaded = sem("a_loaded")
        adj_loaded = [sem(f"a_adj_loaded{i}") for i in range(2)]
        adj_free = sem("a_adj_free")
        prob_free = sem("a_prob_free")
        eb_turned, eb_ready = sem("a_eb_turned"), sem("a_eb_ready")
        diag_out = sem("a_diag_out")
        logit_ready = sem("a_logit_ready")
        exp_ready = sem("a_exp_ready")
        inv_ready = sem("a_inv_ready")
        weight_ready = sem("a_weight_ready")
        tr_ready = sem("a_tr_ready")
        pT_ready = sem("a_pT_ready")
        pT_free = sem("a_pT_free")
        acc_ready = sem("a_acc_ready")
        rows_ready = sem("a_rows_ready")
        rt_ready = sem("a_rt_ready")
        rowsT_ready = sem("a_rowsT_ready")
        sup_ready = sem("a_sup_ready")
        sup_copied = sem("a_sup_copied")

        def seq(p, k, h):
            return (p * 2 + k) * HEADS + h

        def ring(k, h, c):
            return ((k * HEADS + h) * NC + c) % RING

        with nc.Block() as block:
            @block.sync
            def _(eng):
                eng.dma_start(W[:, :, :], d["gat_W"]).then_inc(loaded, 16)
                with eng.Fori(0, PAIRS) as p:
                    for k in range(2):
                        eng.wait_ge(adj_free, p * 2 + k + 1)
                        eng.dma_start(adj[k][:, :], d["adj"][bass.ds((p * 2 + k) * P, P), :])\
                           .then_inc(adj_loaded[k], 16)

            @block.tensor
            def _(eng):
                eng.sem_inc(prob_free, 3)
                eng.sem_inc(pT_free, RING)
                eng.sem_inc(sup_ready, 1)
                for g in range(2 * HEADS * NC):
                    h, c = g // NC, g % NC
                    if g >= 2:
                        eng.wait_ge(eb_ready, g - 1)
                    for j in range(4 * c, min(4 * c + 4, T)):
                        mm = eng.transpose(tr[g % 2][:, (j % 4) * P:(j % 4 + 1) * P],
                                           epm[:, j, h:h + 1].to_broadcast([P, P]), ident[:, :])
                    mm.then_inc(eb_turned, 1)
                eng.wait_ge(eb_ready, 2 * HEADS * NC)
                eng.wait_ge(loaded, 16)

                def finish(p, k, h):
                    q = seq(p, k, h)
                    eng.wait_ge(rows_ready, q + 2)
                    eng.wait_ge(rowsT_ready, q + 1)
                    eng.transpose(rt[:, :], rows[:, :], ident[:, :]).then_inc(rt_ready, 1)
                    if h == HEADS - 1:
                        eng.wait_ge(rowsT_ready, q + 2)
                        eng.wait_ge(sup_copied, p * 2 + k + 1)
                        for g in range(HEADS):
                            mm = eng.matmul(sup[:, :], W[:, g, :], rowsT[:, g, :],
                                            start=(g == 0), stop=(g == HEADS - 1))
                        mm.then_inc(sup_ready, 1)

                def head(p, k, h, before):
                    q = seq(p, k, h)
                    eng.wait_ge(weight_ready, q + 1)

                    def turn(c):
                        for j in range(4 * c, min(4 * c + 4, T)):
                            mm = eng.transpose(tr[ring(k, h, c)][:, (j % 4) * P:(j % 4 + 1) * P],
                                               prob[h][:, j * P:(j + 1) * P], ident[:, :])
                        mm.then_inc(tr_ready, 1)

                    for c in range(RING - 1):
                        turn(c)
                    for c in range(NC):
                        if c + RING - 1 < NC:
                            turn(c + RING - 1)
                        if c == 3 and before is not None:
                            finish(*before)
                        eng.wait_ge(pT_ready, q * NC + c + 1)
                        if c == 0:
                            eng.wait_ge(rows_ready, q + 1)
                        for j in range(4 * c, min(4 * c + 4, T)):
                            mm = eng.matmul(acc[:, :], pT[ring(k, h, c)][:, (j % 4) * P:(j % 4 + 1) * P],
                                            H[:, j, :], start=(j == 0), stop=(j == T - 1))
                            if c + RING == NC and j == 4 * c:
                                mm.then_inc(prob_free, 1)
                        if c == NC - 1:
                            mm.then_inc(acc_ready, 1)
                            eng.drain()
                            eng.sem_inc(pT_free, 1)
                        else:
                            mm.then_inc(pT_free, 1)

                def pair(p, before):
                    for k in range(2):
                        for h in range(HEADS):
                            head(p, k, h, before)
                            before = (p, k, h)

                pair(0, None)
                with eng.Fori(1, PAIRS) as p:
                    pair(p, (p - 1, 1, HEADS - 1))
                finish(PAIRS - 1, 1, HEADS - 1)

            @block.scalar
            def _(eng):
                for copied in (rows_ready, rowsT_ready, sup_copied):
                    eng.sem_inc(copied, 1)
                for g in range(2 * HEADS * NC):
                    h, c = g // NC, g % NC
                    n = min(512, NP - c * 512)
                    eng.wait_ge(eb_turned, g + 1)
                    eng.activation(EB[:, h, c * 512:c * 512 + n], tr[g % 2][:, 0:n], ACT.Copy)\
                       .then_inc(eb_ready, 1)

                def exp(p, k, h, part):
                    sl = slice(0, HALF) if part == 0 else slice(HALF, NP)
                    if part == 0:
                        eng.wait_ge(logit_ready, seq(p, k, h) + 1)
                    eng.activation(prob[h][:, sl], prob[h][:, sl], ACT.Exp, bias=negmax[h][:, :],
                                   accum_out=den[h][:, part:part + 1])
                    if part == 1:
                        eng.drain()
                        eng.sem_inc(exp_ready, 1)

                def finish(p, k, h):
                    q = seq(p, k, h)
                    t = p * 2 + k
                    eng.wait_ge(rt_ready, q + 1)
                    if h == 0:
                        eng.wait_ge(sup_ready, t + 1)
                    eng.activation(rowsT[:, h, :], rt[:, :], ACT.Copy).then_inc(rowsT_ready, 1)
                    if h == HEADS - 1:
                        eng.wait_ge(sup_ready, t + 2)
                        eng.activation(gsT[:, bass.ds(t * P, P)], sup[:, :], ACT.Copy, scale=1.0 / HEADS)
                        eng.drain()
                        eng.sem_inc(sup_copied, 1)

                def copies(p, k, h, before, ahead):
                    q = seq(p, k, h)
                    for c in range(NC):
                        n = min(512, NP - c * 512)
                        eng.wait_ge(tr_ready, q * NC + c + 1)
                        eng.wait_ge(pT_free, q * NC + c + 1)
                        eng.activation(pT[ring(k, h, c)][:, 0:n], tr[ring(k, h, c)][:, 0:n], ACT.Copy)\
                           .then_inc(pT_ready, 1)
                        if c == 4 and before is not None:
                            finish(*before)
                        if c in (1, 3) and ahead is not None:
                            exp(*ahead, c // 2)
                    eng.wait_ge(acc_ready, q + 1)
                    eng.wait_ge(inv_ready, q + 1)
                    eng.activation(rows[:, :], acc[:, :], ACT.Copy, scale=inv[h][:, :]).then_inc(rows_ready, 1)

                order = [(k, h) for k in range(2) for h in range(HEADS)]
                AHEAD = 2

                def pair(p, before, last):
                    for n, (k, h) in enumerate(order):
                        if n + AHEAD < len(order):
                            ahead = (p, *order[n + AHEAD])
                        else:
                            ahead = None if last else (p + 1, *order[n + AHEAD - len(order)])
                        copies(p, k, h, before, ahead)
                        before = (p, k, h)

                for n in range(AHEAD):
                    exp(0, *order[n], 0)
                    exp(0, *order[n], 1)
                pair(0, None, False)
                with eng.Fori(1, PAIRS - 1) as p:
                    pair(p, (p - 1, 1, HEADS - 1), False)
                pair(PAIRS - 1, (PAIRS - 2, 1, HEADS - 1), True)
                finish(PAIRS - 1, 1, HEADS - 1)

            @block.gpsimd
            def _(eng):
                eng.sem_inc(adj_free, 2)
                with eng.Fori(0, PAIRS) as p:
                    for k in range(2):
                        for h in range(HEADS):
                            eng.wait_ge(exp_ready, seq(p, k, h) + 1)
                            eng.tensor_tensor(prob[h][:, :], prob[h][:, :], adj[k][:, :], ALU.mult)
                            eng.drain()
                            eng.sem_inc(weight_ready, 1)
                        eng.sem_inc(adj_free, 1)

            @block.vector
            def _(eng):
                flag = eng.alloc_register("negative_flag")
                regs = [eng.alloc_register(f"neg_group{q}") for q in range(4)]
                eng.memset(w["flags"][:, :], 0.0)
                eng.drain()
                eng.tensor_reduce(w["flags"][:, 0:1], negs[:, :], AX.X, ALU.max)
                spread_flags(eng, [w])
                load_flag(eng, w, flag, regs)
                eng.wait_ge(eb_ready, 2 * HEADS * NC)

                def without_diagonal(p, k):
                    eng.wait_ge(adj_loaded[k], (p + 1) * 16)
                    block_ = adj[k][:, bass.ds((p * 2 + k) * P, P)]
                    eng.tensor_tensor(dblock[:, :], block_, ident[:, :], ALU.mult)
                    eng.drain()
                    eng.tensor_tensor(block_, block_, dblock[:, :], ALU.subtract)
                    eng.drain()
                    eng.tensor_scalar(off[:, :], adj[k][:, :], 0.0, NEG, ALU.is_le, ALU.mult)
                    eng.drain()

                def logits(p, k, h):
                    eng.wait_ge(prob_free, seq(p, k, h) + 1)
                    eng.memset(gate[:, :], 0.0)
                    eng.tensor_tensor_reduce(prob[h][:, :], off[:, :], EB[:, h, :], 1.0, -3.0e38,
                                             ALU.add, ALU.max, mx[h][:, :])
                    eng.drain()
                    with eng.If(eng.snap(flag) > 0):
                        eng.tensor_scalar(negmask[:, :], adj[k][:, :], 0.0, None, ALU.is_lt)
                        eng.drain()
                        eng.copy_predicated(prob[h][:, :], negmask[:, :], EB[:, HEADS + h, :])
                        eng.drain()
                        eng.tensor_reduce(mx[h][:, :], prob[h][:, :], AX.X, ALU.max)
                        eng.drain()
                    eng.tensor_scalar(negmax[h][:, :], mx[h][:, :], -1.0, None, ALU.mult)\
                       .then_inc(logit_ready, 1)

                def inverse(p, k, h):
                    eng.wait_ge(exp_ready, seq(p, k, h) + 1)
                    eng.tensor_reduce(inv[h][:, :], den[h][:, :], AX.X, ALU.add)
                    eng.drain()
                    eng.reciprocal(inv[h][:, :], inv[h][:, :]).then_inc(inv_ready, 1)

                def pair(p, before):
                    for k in range(2):
                        for h in range(HEADS):
                            if h == 0:
                                without_diagonal(p, k)
                            logits(p, k, h)
                            if before is not None:
                                inverse(*before)
                            before = (p, k, h)

                pair(0, None)
                with eng.Fori(1, PAIRS) as p:
                    pair(p, (p - 1, 1, HEADS - 1))
                inverse(PAIRS - 1, 1, HEADS - 1)


def gates_and_output(nc, d, dims, H, ident, diag, gsT):
    N, NP, T = dims
    PAIRS = T // 2
    G = 4
    with ExitStack() as ctx:
        sb, ps, sem = scope(nc, ctx)
        nsT = sb("o_nsT", [P, NP])
        Wi = [sb(f"Wi{g}", [P, 3 * P]) for g in range(2)]
        Wh = [sb(f"Wh{g}", [P, 3 * P]) for g in range(2)]
        bias = [sb(f"bias{g}", [P, 4 * P]) for g in range(2)]
        ones = sb("ones_all", [P, P])
        O = sb("O", [P, T, P])
        sq = sb("o_sq", [P, T, P])
        stat = sb("o_stat", [P, T])
        rstd = sb("o_rstd", [P, T])
        h = [sb(f"h_pair{b}", [P, 2, P]) for b in range(2)]
        sT = [[sb(f"sT{g}{b}", [P, 2, P]) for b in range(2)] for g in range(2)]
        hTt = sb("hT_pair", [P, 2, P])
        rz = sb("rz", [P, G, 2 * P])
        arg = sb("new_arg", [P, G, P])
        new = sb("new_gate", [P, G, P])
        mix = sb("mix", [P, G, P])
        tp = ps("o_tp", [P, 2, P])
        gp = ps("o_gp", [P, G, 4 * P])

        loaded, ones_ready = sem("o_loaded"), sem("o_ones_ready")
        tiles_ready = sem("o_tiles_ready")
        tiles_free = sem("o_tiles_free")
        tp_ready, hT_ready = sem("o_tp_ready"), sem("o_hT_ready")
        gates_summed = sem("o_gates_summed")
        gates_used = sem("o_gates_used")
        rz_ready, arg_ready, new_ready = sem("o_rz_ready"), sem("o_arg_ready"), sem("o_new_ready")
        mixed = sem("o_mixed")
        var_ready, std_ready = sem("o_var_ready"), sem("o_std_ready")
        normed, stored = sem("o_normed"), sem("o_stored")

        def in_pairs(make, eng):
            with eng.Fori(0, PAIRS // 2) as pp:
                make(pp * 2, 0)
                make(pp * 2 + 1, 1)
            if PAIRS % 2:
                make(PAIRS - 1, (PAIRS - 1) % 2)

        with nc.Block() as block:
            @block.sync
            def _(eng):
                for g, name in enumerate(("edge", "node")):
                    eng.dma_start(Wi[g][:, :], d[f"{name}_WihT"]).then_inc(loaded, 16)
                    eng.dma_start(Wh[g][:, :], d[f"{name}_WhhT"]).then_inc(loaded, 16)
                eng.wait_ge(ones_ready, 1)
                for g, name in enumerate(("edge", "node")):
                    eng.dma_start(bias[g][0:1, 0:3 * P], d[f"{name}_bih"]).then_inc(loaded, 16)
                    eng.dma_start(bias[g][1:2, 0:2 * P], d[f"{name}_bhh"][:, 0:2 * P]).then_inc(loaded, 16)
                    eng.dma_start(bias[g][1:2, 3 * P:4 * P], d[f"{name}_bhh"][:, 2 * P:3 * P]).then_inc(loaded, 16)
                eng.dma_start(nsT[:, :], d["nsT"]).then_inc(loaded, 16)
                eng.wait_ge(normed, 1)
                whole = N // P
                eng.dma_start(d["out"][0:whole * P, :].rearrange("(t p) d -> p t d", p=P), H[:, 0:whole, :])\
                   .then_inc(stored, 16)
                if N % P:
                    eng.dma_start(d["out"][whole * P:N, :], H[0:N % P, whole, :]).then_inc(stored, 16)
                eng.wait_ge(stored, 32 if N % P else 16)

            @block.gpsimd
            def _(eng):
                eng.sem_inc(tiles_free, 2)
                eng.wait_ge(loaded, 16 * 11)

                def give(p, b):
                    eng.wait_ge(tiles_free, p + 1)
                    eng.tensor_copy(h[b][:, :, :], H[:, bass.ds(p * 2, 2), :])
                    eng.tensor_copy(sT[0][b][:, :, :].rearrange("p a b -> p (a b)"), nsT[:, bass.ds(p * 2 * P, 2 * P)])
                    eng.tensor_copy(sT[1][b][:, :, :].rearrange("p a b -> p (a b)"), gsT[:, bass.ds(p * 2 * P, 2 * P)])
                    eng.drain()
                    eng.sem_inc(tiles_ready, 1)

                in_pairs(give, eng)

            @block.tensor
            def _(eng):
                eng.wait_ge(loaded, 16 * 11)
                eng.wait_ge(ones_ready, 1)

                def sums(p, b):
                    eng.wait_ge(tiles_ready, p + 1)
                    for k in range(2):
                        mm = eng.transpose(tp[:, k, :], h[b][:, k, :], ident[:, :])
                    mm.then_inc(tp_ready, 1)
                    RZ, NN = slice(0, 2 * P), slice(2 * P, 3 * P)
                    eng.wait_ge(hT_ready, p + 1)
                    for k in range(2):
                        eng.wait_ge(gates_used, p * 2 + k + 1)
                        for g in range(2):
                            out = gp[:, k * 2 + g, :]
                            rzp, inp, hnp = out[:, 0:2 * P], out[:, 2 * P:3 * P], out[:, 3 * P:4 * P]
                            eng.matmul(rzp, ones[:, :], bias[g][:, 0:2 * P], start=True, stop=False)
                            eng.matmul(rzp, sT[g][b][:, k, :], Wi[g][:, RZ], start=False, stop=False)
                            eng.matmul(rzp, hTt[:, k, :], Wh[g][:, RZ], start=False, stop=True)
                            eng.matmul(inp, ones[:, :], bias[g][:, 2 * P:3 * P], start=True, stop=False)
                            eng.matmul(inp, sT[g][b][:, k, :], Wi[g][:, NN], start=False, stop=True)
                            eng.matmul(hnp, ones[:, :], bias[g][:, 3 * P:4 * P], start=True, stop=False)
                            mm = eng.matmul(hnp, hTt[:, k, :], Wh[g][:, NN], start=False, stop=True)
                        mm.then_inc(gates_summed, 1)

                in_pairs(sums, eng)

            @block.scalar
            def _(eng):
                def gates(p, b):
                    eng.wait_ge(tp_ready, p + 1)
                    eng.activation(hTt[:, :, :], tp[:, :, :], ACT.Copy).then_inc(hT_ready, 1)
                    eng.wait_ge(mixed, p + 1)
                    for k in range(2):
                        G2 = slice(k * 2, k * 2 + 2)
                        eng.wait_ge(gates_summed, p * 2 + k + 1)
                        eng.activation(rz[:, G2, :], gp[:, G2, 0:2 * P], ACT.Sigmoid).then_inc(rz_ready, 1)
                        eng.wait_ge(arg_ready, p * 2 + k + 1)
                        eng.activation(new[:, G2, :], arg[:, G2, :], ACT.Sigmoid, scale=2.0).then_inc(new_ready, 1)

                in_pairs(gates, eng)
                roots(eng, stat, std_ready, var_ready, 1)

            @block.vector
            def _(eng):
                eng.memset(ones[:, :], 1.0)
                for g in range(2):
                    eng.memset(bias[g][:, :], 0.0)
                eng.drain()
                eng.sem_inc(ones_ready, 1)
                eng.sem_inc(gates_used, 2)
                eng.sem_inc(mixed, 1)

                def states(p, b):
                    for k in range(2):
                        G2 = slice(k * 2, k * 2 + 2)
                        eng.wait_ge(rz_ready, p * 2 + k + 1)
                        eng.tensor_tensor(arg[:, G2, :], rz[:, G2, 0:P], gp[:, G2, 3 * P:4 * P], ALU.mult)
                        eng.drain()
                        eng.tensor_tensor(arg[:, G2, :], arg[:, G2, :], gp[:, G2, 2 * P:3 * P], ALU.add)
                        eng.drain()
                        eng.sem_inc(arg_ready, 1)
                        eng.sem_inc(gates_used, 1)
                    eng.wait_ge(new_ready, p * 2 + 2)
                    eng.tensor_scalar(new[:, :, :], new[:, :, :], 2.0, -1.0, ALU.mult, ALU.add)
                    eng.drain()
                    for g in range(2):
                        eng.tensor_tensor(mix[:, g:G:2, :], h[b][:, :, :], new[:, g:G:2, :], ALU.subtract)
                    eng.drain()
                    eng.tensor_tensor(mix[:, :, :], mix[:, :, :], rz[:, :, P:2 * P], ALU.mult)
                    eng.drain()
                    eng.tensor_tensor(mix[:, :, :], mix[:, :, :], new[:, :, :], ALU.add)
                    eng.drain()
                    eng.tensor_tensor(O[:, bass.ds(p * 2, 2), :], mix[:, 0:G:2, :], mix[:, 1:G:2, :], ALU.add)
                    eng.drain()
                    eng.sem_inc(mixed, 1)
                    eng.sem_inc(tiles_free, 1)

                in_pairs(states, eng)
                eng.tensor_tensor(O[:, :, :], O[:, :, :], diag[:, :].unsqueeze(2).to_broadcast([P, T, P]), ALU.mult)
                eng.drain()
                eng.tensor_tensor(H[:, :, :], H[:, :, :], O[:, :, :], ALU.add)
                eng.drain()
                layernorm_rows(eng, H, sq, stat, rstd, std_ready, var_ready, 1, T)
                eng.sem_inc(normed, 1)


def program(nc, d, dims):
    N, NP, T = dims
    with ExitStack() as ctx:
        sb, ps, sem = scope(nc, ctx)
        H = sb("H", [P, T, P])
        ident = sb("ident", [P, P])
        layer0(nc, d, dims, H, ident)
        normalize(nc, d, dims, H)
        diag = sb("diag", [P, T])
        epm = sb("epm", [P, T, 6])
        negs = sb("negs", [P, T])
        graph_sums(nc, d, dims, H, ident, diag, epm, negs)
        gsT = sb("gsT", [P, NP])
        attention(nc, d, dims, H, ident, epm, negs, gsT)
        gates_and_output(nc, d, dims, H, ident, diag, gsT)


def kernel(x, adj, L0_gnn_W1, L0_gnn_W2, L0_gnn_W3, L0_gnn_U1, L0_gnn_U2, L0_gnn_ln_g, L0_gnn_ln_b,
           L1_gnn_gat_W, L1_gnn_gat_a, L1_gnn_edge_Wih, L1_gnn_edge_Whh, L1_gnn_edge_bih, L1_gnn_edge_bhh,
           L1_gnn_node_Wih, L1_gnn_node_Whh, L1_gnn_node_bih, L1_gnn_node_bhh):
    import numpy as np
    import concourse.bacc as bacc
    from concourse.bass_utils import run_bass_kernel_spmd

    c = np.ascontiguousarray
    N, D = x.shape
    T = -(-N // P)
    T += T % 2
    NP = T * P
    rows = np.concatenate([x] + [x[-1:]] * (NP - N), axis=0)
    adj_rows = np.zeros((NP, NP), adj.dtype)
    adj_rows[:N, :N] = adj
    arrays = {
        "x_rows": rows,
        "x_t": c(rows.T),
        "adj": adj_rows,
        "adjT": c(adj_rows.reshape(T, P, T, P).transpose(0, 3, 2, 1)).reshape(NP, NP),
        "W1T": c(L0_gnn_W1.T), "W2T": c(L0_gnn_W2.T), "W3T": c(L0_gnn_W3.T),
        "U1T": c(L0_gnn_U1.transpose(2, 0, 1)), "U2T": c(L0_gnn_U2.transpose(2, 0, 1)),
        "ln_g": c(L0_gnn_ln_g), "ln_b": c(L0_gnn_ln_b),
        "gat_W": c(L1_gnn_gat_W.transpose(1, 0, 2)), "gat_WT": c(L1_gnn_gat_W.transpose(2, 0, 1)),
        "gat_a": c(L1_gnn_gat_a.reshape(-1, 2, D).transpose(2, 0, 1)),
        "edge_WihT": c(L1_gnn_edge_Wih.T), "edge_WhhT": c(L1_gnn_edge_Whh.T),
        "edge_bih": L1_gnn_edge_bih.reshape(1, -1), "edge_bhh": L1_gnn_edge_bhh.reshape(1, -1),
        "node_WihT": c(L1_gnn_node_Wih.T), "node_WhhT": c(L1_gnn_node_Whh.T),
        "node_bih": L1_gnn_node_bih.reshape(1, -1), "node_bhh": L1_gnn_node_bhh.reshape(1, -1),
    }
    arrays = {f"in_{name}": c(a) for name, a in arrays.items()}
    nc = bacc.Bacc("TRN2", target_bir_lowering=False, num_devices=1)
    d = {name[3:]: nc.dram_tensor(name, a.shape, F32, kind="ExternalInput").ap() for name, a in arrays.items()}
    d["x_rows"] = d["x_rows"].rearrange("(t p) d -> p t d", p=P)
    d["nsT"] = nc.dram_tensor("nsT_scratch", (P, NP), F32, kind="Internal").ap()
    d["out"] = nc.dram_tensor("out_rows", (N, D), F32, kind="ExternalOutput").ap()
    program(nc, d, (N, NP, T))
    r = run_bass_kernel_spmd(nc, [arrays], core_ids=[0])
    return r.results[0]["out_rows"]
```
